# Optimizing a Trainium2 kernel written in Bass

```python
import numpy as np
import jax
import jax.numpy as jnp

def _softmax(x, axis=-1):
    return jax.nn.softmax(x, axis=axis)

def _gelu(x):
    return jax.nn.gelu(x, approximate=True)

def _silu(x):
    return jax.nn.silu(x)

def _sigmoid(x):
    return jax.nn.sigmoid(x)

def _layernorm(x, axis=-1, eps=1e-05):
    m = jnp.mean(x, axis=axis, keepdims=True)
    v = jnp.var(x, axis=axis, keepdims=True)
    return (x - m) / jnp.sqrt(v + eps)

def _scatter_add(tgt, idx, src, axis=0):
    return tgt.at[idx].add(src)

def _segment_sum(src, seg, n):
    return jax.ops.segment_sum(src, seg, n)
kernel_name = 'mk_adj_resnorm_d4_adj_r2_64a9f6'

def setup_inputs(seed: int=0):
    np.random.seed(seed)
    _w = jnp.asarray

    def _rec_inputs():
        import jax
        import jax.numpy as jnp
        _gk = jax.random.key(seed)
        x = -0.001547 + 1.001 * jax.random.normal(jax.random.fold_in(_gk, 1), (64, 128, 128), jnp.float32)
        _w = (1.0 + jnp.arange(128, dtype=jnp.float32)) ** (-0.5)
        _w = _w / _w.mean()
        _pij = jnp.clip(0.125 * _w[:, None] * _w[None, :], 0.0, 1.0)
        _a = jax.random.uniform(jax.random.fold_in(_gk, 2), (64, 128, 128)) < _pij
        _a = jnp.logical_or(_a, jnp.eye(128, dtype=bool))
        adj = _a.astype(jnp.int32)
        _nm = jnp.ones((64, 128), dtype=bool)
        nodemask = jnp.where(_nm, 1.0, 0.0).astype(jnp.float32)
        return (x, adj, nodemask)
    x, adj, nodemask = _rec_inputs()

    def _L0_gnn_setup():
        import jax, jax.numpy as jnp
        import numpy as np
        D_MODEL = 128
        NUM_REL = 40

        def _direction(x, W, Wg, b, bg, adj, rel_ids):
            h = x @ W.T
            g = h @ Wg.T
            vals = (h[:, :, None, :] + b) * jax.nn.sigmoid(g[:, :, None, :] + bg)
            onehot = (adj[..., None] == rel_ids).astype(h.dtype)
            return jnp.einsum('bnmr,bmrd->bnd', onehot, vals)
        key = jax.random.key(seed)
        ks = jax.random.split(key, 16)
        B, N, d = (2, 256, D_MODEL)
        s = 0.02
        inp = {'node': jax.random.normal(ks[0], (B, N, d), dtype=jnp.float32), 'node_mask': jnp.ones((B, N), dtype=jnp.float32), 'adj_mat': jax.random.randint(ks[1], (B, N, N), 0, 41, dtype=jnp.int32), 'W_fwd': jax.random.normal(ks[2], (d, d), dtype=jnp.float32) * s, 'W_bwd': jax.random.normal(ks[3], (d, d), dtype=jnp.float32) * s, 'W_loop': jax.random.normal(ks[4], (d, d), dtype=jnp.float32) * s, 'Wg_fwd': jax.random.normal(ks[5], (d, d), dtype=jnp.float32) * s, 'Wg_bwd': jax.random.normal(ks[6], (d, d), dtype=jnp.float32) * s, 'Wg_loop': jax.random.normal(ks[7], (d, d), dtype=jnp.float32) * s, 'b_fwd': jax.random.normal(ks[8], (NUM_REL - 1, d), dtype=jnp.float32) * s, 'b_bwd': jax.random.normal(ks[9], (NUM_REL - 1, d), dtype=jnp.float32) * s, 'b_loop': jax.random.normal(ks[10], (1, d), dtype=jnp.float32) * s, 'bg_fwd': jax.random.normal(ks[11], (NUM_REL - 1, d), dtype=jnp.float32) * s, 'bg_bwd': jax.random.normal(ks[12], (NUM_REL - 1, d), dtype=jnp.float32) * s, 'bg_loop': jax.random.normal(ks[13], (1, d), dtype=jnp.float32) * s}
        return inp
    _L0_gnn_all = _L0_gnn_setup()
    _L0_gnn_in = {k: v for k, v in _L0_gnn_all.items() if k in ('W_fwd', 'W_bwd', 'W_loop', 'Wg_fwd', 'Wg_bwd', 'Wg_loop', 'b_fwd', 'b_bwd', 'b_loop', 'bg_fwd', 'bg_bwd', 'bg_loop')}
    del _L0_gnn_all

    def _L1_gnn_setup():
        import jax, jax.numpy as jnp
        import numpy as np
        B, N, F_IN, F_OUT = (1, 4096, 128, 128)
        ALPHA = 0.2
        NEG_INF = -9000000000000000.0
        key = jax.random.key(seed)
        ks = jax.random.split(key, 8)
        feat = jax.random.normal(ks[0], (B, N, F_IN), dtype=jnp.float32)
        adj = jax.random.randint(ks[1], (B, N, N), 0, 2, dtype=jnp.int32)
        s = 1.414 * (6.0 / (F_IN + F_OUT)) ** 0.5
        W = jax.random.uniform(ks[2], (F_IN, F_OUT), minval=-s, maxval=s, dtype=jnp.float32)
        a_1 = jax.random.normal(ks[3], (F_OUT, 1), dtype=jnp.float32) * 0.1
        a_2 = jax.random.normal(ks[4], (F_OUT, 1), dtype=jnp.float32) * 0.1
        a_12 = jax.random.normal(ks[5], (F_OUT, F_OUT), dtype=jnp.float32) * (1.0 / F_OUT ** 0.5)
        W_1 = jax.random.uniform(ks[6], (F_IN, F_OUT), minval=-s, maxval=s, dtype=jnp.float32)
        W_2 = jax.random.uniform(ks[7], (F_IN, F_OUT), minval=-s, maxval=s, dtype=jnp.float32)
        return {'feat': feat, 'adj': adj, 'W': W, 'a_1': a_1, 'a_2': a_2, 'a_12': a_12, 'W_1': W_1, 'W_2': W_2}
    _L1_gnn_all = _L1_gnn_setup()
    _L1_gnn_in = {k: v for k, v in _L1_gnn_all.items() if k in ('W', 'a_1', 'a_2', 'a_12', 'W_1', 'W_2')}
    del _L1_gnn_all

    def _L2_gnn_setup():
        import math
        import jax, jax.numpy as jnp
        import numpy as np
        B, N, E, H = (1, 2048, 128, 8)
        D = E // H
        key = jax.random.key(seed)
        ks = jax.random.split(key, 10)
        s = 1.0 / math.sqrt(E)
        return {'x': jax.random.normal(ks[0], (B, N, E), dtype=jnp.float32), 'adjacency': jax.random.randint(ks[1], (B, N, N), 0, 2, dtype=jnp.int32), 'Wq': jax.random.normal(ks[2], (E, E), dtype=jnp.float32) * s, 'bq': jnp.zeros((E,), dtype=jnp.float32), 'Wk': jax.random.normal(ks[3], (E, E), dtype=jnp.float32) * s, 'bk': jnp.zeros((E,), dtype=jnp.float32), 'Wv': jax.random.normal(ks[4], (E, E), dtype=jnp.float32) * s, 'bv': jnp.zeros((E,), dtype=jnp.float32), 'Wo': jax.random.normal(ks[5], (E, E), dtype=jnp.float32) * s, 'bo': jnp.zeros((E,), dtype=jnp.float32)}
    _L2_gnn_all = _L2_gnn_setup()
    _L2_gnn_in = {k: v for k, v in _L2_gnn_all.items() if k in ('Wq', 'bq', 'Wk', 'bk', 'Wv', 'bv', 'Wo', 'bo')}
    del _L2_gnn_all

    def _L3_gnn_setup():
        import jax, jax.numpy as jnp
        import numpy as np
        B, N, D_IN, D_OUT, H = (8, 512, 128, 128, 8)
        HD = D_OUT // H
        ALPHA = 0.2
        key = jax.random.key(seed)
        k1, k2, k3, k4 = jax.random.split(key, 4)
        h = jax.random.normal(k1, (B, N, D_IN), dtype=jnp.float32)
        adj_mask = jax.random.randint(k2, (B, N, N), 0, 2, dtype=jnp.int64)
        idx = jnp.arange(N)
        adj_mask = adj_mask.at[:, idx, idx].set(1)
        lim_W = float(np.sqrt(6.0 / (D_IN + D_OUT)))
        W = jax.random.uniform(k3, (D_IN, D_OUT), minval=-lim_W, maxval=lim_W, dtype=jnp.float32)
        lim_a = float(np.sqrt(6.0 / (2 * HD + 1)))
        a = jax.random.uniform(k4, (2 * HD,), minval=-lim_a, maxval=lim_a, dtype=jnp.float32)
        return {'h': h, 'adj_mask': adj_mask, 'W': W, 'a': a}
    _L3_gnn_all = _L3_gnn_setup()
    _L3_gnn_in = {k: v for k, v in _L3_gnn_all.items() if k in ('W', 'a')}
    del _L3_gnn_all
    return {'x': x, 'adj': adj, 'nodemask': nodemask, 'L0_gnn_W_fwd': _L0_gnn_in['W_fwd'], 'L0_gnn_W_bwd': _L0_gnn_in['W_bwd'], 'L0_gnn_W_loop': _L0_gnn_in['W_loop'], 'L0_gnn_Wg_fwd': _L0_gnn_in['Wg_fwd'], 'L0_gnn_Wg_bwd': _L0_gnn_in['Wg_bwd'], 'L0_gnn_Wg_loop': _L0_gnn_in['Wg_loop'], 'L0_gnn_b_fwd': _L0_gnn_in['b_fwd'], 'L0_gnn_b_bwd': _L0_gnn_in['b_bwd'], 'L0_gnn_b_loop': _L0_gnn_in['b_loop'], 'L0_gnn_bg_fwd': _L0_gnn_in['bg_fwd'], 'L0_gnn_bg_bwd': _L0_gnn_in['bg_bwd'], 'L0_gnn_bg_loop': _L0_gnn_in['bg_loop'], 'L1_gnn_W': _L1_gnn_in['W'], 'L1_gnn_a_1': _L1_gnn_in['a_1'], 'L1_gnn_a_2': _L1_gnn_in['a_2'], 'L1_gnn_a_12': _L1_gnn_in['a_12'], 'L1_gnn_W_1': _L1_gnn_in['W_1'], 'L1_gnn_W_2': _L1_gnn_in['W_2'], 'L2_gnn_Wq': _L2_gnn_in['Wq'], 'L2_gnn_bq': _L2_gnn_in['bq'], 'L2_gnn_Wk': _L2_gnn_in['Wk'], 'L2_gnn_bk': _L2_gnn_in['bk'], 'L2_gnn_Wv': _L2_gnn_in['Wv'], 'L2_gnn_bv': _L2_gnn_in['bv'], 'L2_gnn_Wo': _L2_gnn_in['Wo'], 'L2_gnn_bo': _L2_gnn_in['bo'], 'L3_gnn_W': _L3_gnn_in['W'], 'L3_gnn_a': _L3_gnn_in['a']}

def reference(x, adj, nodemask, L0_gnn_W_fwd, L0_gnn_W_bwd, L0_gnn_W_loop, L0_gnn_Wg_fwd, L0_gnn_Wg_bwd, L0_gnn_Wg_loop, L0_gnn_b_fwd, L0_gnn_b_bwd, L0_gnn_b_loop, L0_gnn_bg_fwd, L0_gnn_bg_bwd, L0_gnn_bg_loop, L1_gnn_W, L1_gnn_a_1, L1_gnn_a_2, L1_gnn_a_12, L1_gnn_W_1, L1_gnn_W_2, L2_gnn_Wq, L2_gnn_bq, L2_gnn_Wk, L2_gnn_bk, L2_gnn_Wv, L2_gnn_bv, L2_gnn_Wo, L2_gnn_bo, L3_gnn_W, L3_gnn_a):
    import jax
    import jax.numpy as jnp

    def _L0_gnn_ref(node, node_mask, adj_mat, W_fwd, W_bwd, W_loop, Wg_fwd, Wg_bwd, Wg_loop, b_fwd, b_bwd, b_loop, bg_fwd, bg_bwd, bg_loop):
        import jax, jax.numpy as jnp
        import numpy as np
        D_MODEL = 128
        NUM_REL = 40

        def _direction(x, W, Wg, b, bg, adj, rel_ids):
            h = x @ W.T
            g = h @ Wg.T
            vals = (h[:, :, None, :] + b) * jax.nn.sigmoid(g[:, :, None, :] + bg)
            onehot = (adj[..., None] == rel_ids).astype(h.dtype)
            return jnp.einsum('bnmr,bmrd->bnd', onehot, vals)
        rels = jnp.arange(2, NUM_REL + 1, dtype=adj_mat.dtype)
        rel1 = jnp.array([1], dtype=adj_mat.dtype)
        adj_t = jnp.swapaxes(adj_mat, -1, -2)
        out = _direction(node, W_fwd, Wg_fwd, b_fwd, bg_fwd, adj_mat, rels)
        out = out + _direction(node, W_bwd, Wg_bwd, b_bwd, bg_bwd, adj_t, rels)
        out = out + _direction(node, W_loop, Wg_loop, b_loop, bg_loop, adj_t, rel1)
        return jax.nn.relu(out)

    def _L1_gnn_ref(feat, adj, W, a_1, a_2, a_12, W_1, W_2):
        import jax, jax.numpy as jnp
        import numpy as np
        B, N, F_IN, F_OUT = (1, 4096, 128, 128)
        ALPHA = 0.2
        NEG_INF = -9000000000000000.0
        h = jnp.matmul(feat, W)
        Ax = jnp.matmul(h, a_1)
        Ay = jnp.matmul(h, a_2)
        A_xy = jnp.matmul(jnp.matmul(h, a_12), jnp.swapaxes(h, 1, 2))
        logits = jnp.swapaxes(Ax, 1, 2) + Ay + A_xy
        e = jax.nn.leaky_relu(logits, negative_slope=ALPHA)
        e = jnp.where(adj > 0, e, NEG_INF)
        attention = jax.nn.softmax(e, axis=-1)
        h_prime = jnp.matmul(attention, feat)
        h_out = jnp.matmul(feat, W_1) + jnp.matmul(h_prime, W_2)
        return jax.nn.elu(h_out)

    def _L2_gnn_ref(x, adjacency, Wq, bq, Wk, bk, Wv, bv, Wo, bo):
        import math
        import jax, jax.numpy as jnp
        import numpy as np
        B, N, E, H = (1, 2048, 128, 8)
        D = E // H
        b, n, e = x.shape

        def heads(y):
            return y.reshape(b, n, H, D).transpose(0, 2, 1, 3)
        q = heads(x @ Wq.T + bq)
        k = heads(x @ Wk.T + bk)
        v = heads(x @ Wv.T + bv)
        scores = jnp.einsum('bhnd,bhmd->bhnm', q, k) / math.sqrt(D)
        mask = adjacency[:, None, :, :] == 0
        scores = jnp.where(mask, -jnp.inf, scores)
        w = jax.nn.softmax(scores, axis=-1)
        out = jnp.einsum('bhnm,bhmd->bhnd', w, v)
        out = out.transpose(0, 2, 1, 3).reshape(b, n, e)
        return out @ Wo.T + bo

    def _L3_gnn_ref(h, adj_mask, W, a):
        import jax, jax.numpy as jnp
        import numpy as np
        B, N, D_IN, D_OUT, H = (8, 512, 128, 128, 8)
        HD = D_OUT // H
        ALPHA = 0.2
        b, n, _ = h.shape
        Wh = (h @ W).reshape(b, n, H, HD).transpose(0, 2, 1, 3)
        a1, a2 = (a[:HD], a[HD:])
        e1 = jnp.einsum('bhnd,d->bhn', Wh, a1)
        e2 = jnp.einsum('bhnd,d->bhn', Wh, a2)
        e = e1[:, :, :, None] + e2[:, :, None, :]
        mask = adj_mask[:, None, :, :] == 0
        e = jnp.where(mask, -jnp.inf, e)
        e = jnp.where(e >= 0, e, ALPHA * e)
        attn = jax.nn.softmax(e, axis=-1)
        h_prime = jnp.einsum('bhij,bhjd->bhid', attn, Wh)
        return h_prime.transpose(0, 2, 1, 3).reshape(b, n, D_OUT)
    x = _layernorm(x + _L0_gnn_ref(x, nodemask, adj, L0_gnn_W_fwd, L0_gnn_W_bwd, L0_gnn_W_loop, L0_gnn_Wg_fwd, L0_gnn_Wg_bwd, L0_gnn_Wg_loop, L0_gnn_b_fwd, L0_gnn_b_bwd, L0_gnn_b_loop, L0_gnn_bg_fwd, L0_gnn_bg_bwd, L0_gnn_bg_loop), axis=-1)
    x = _layernorm(x + _L1_gnn_ref(x, adj, L1_gnn_W, L1_gnn_a_1, L1_gnn_a_2, L1_gnn_a_12, L1_gnn_W_1, L1_gnn_W_2), axis=-1)
    x = _layernorm(x + _L2_gnn_ref(x, adj, L2_gnn_Wq, L2_gnn_bq, L2_gnn_Wk, L2_gnn_bk, L2_gnn_Wv, L2_gnn_bv, L2_gnn_Wo, L2_gnn_bo), axis=-1)
    x = _layernorm(x + _L3_gnn_ref(x, adj, L3_gnn_W, L3_gnn_a), axis=-1)
    return x

_drawn_inputs = setup_inputs


def setup_inputs(seed=0):
    import zlib

    import numpy as np

    out = dict(_drawn_inputs(seed))
    spreads = {'L2_gnn_bq': (0.0, 0.272),
     'L2_gnn_bk': (0.0, 0.8),
     'L2_gnn_bv': (0.0, 0.1),
     'L2_gnn_bo': (0.0, 0.1)}
    factors = {'L0_gnn_bg_loop': 4.587, 'L1_gnn_a_2': 8.0}
    for name, (base, spread) in spreads.items():
        noise = np.random.default_rng([zlib.crc32(name.encode()), seed]).standard_normal(out[name].shape)
        drawn = base * np.exp(spread * noise) if base else spread * noise
        out[name] = jnp.asarray(drawn.astype(out[name].dtype))
    for name, factor in factors.items():
        out[name] = (out[name] * factor).astype(out[name].dtype)
    return out
```

```python
from contextlib import ExitStack

import concourse.bass as bass
from concourse import mybir

F32 = mybir.dt.float32
BF16 = mybir.dt.bfloat16
I32 = mybir.dt.int32
ALU = mybir.AluOpType
ACT = mybir.ActivationFunctionType
AX = mybir.AxisListType

GRAPHS, N, D = 64, 128, 128
G = 4
BATCHES = GRAPHS // G
W = G * D
HEADS = 8
HD = D // HEADS
HP = 32
HQ = 4
UNITS = G * HEADS // HQ
ALPHA = 0.2
EPS = 1e-5
MASKED = -1e30
REL_LAST = 40
RELS = REL_LAST - 1


def need(eng, sem, value):
    if not isinstance(value, int) or value > 0:
        eng.wait_ge(sem, value)


def need_or(eng, sem, value, before, count):
    if isinstance(value, int) and value <= 0:
        eng.wait_ge(before, count)
    else:
        eng.wait_ge(sem, value)


def real(b):
    return not isinstance(b, int) or 0 <= b < BATCHES


def every_batch(eng, body, before=False, after=False):
    if before:
        body(-1, 1, -1)
    for b in range(4):
        body(b, b % 2, b // 2)
    with eng.Fori(2, BATCHES // 2 - 1) as turn:
        body(2 * turn, 0, turn)
        body(2 * turn + 1, 1, turn)
    last = BATCHES // 2 - 1
    body(2 * last, 0, last)
    body(2 * last + 1, 1, last)
    if after:
        body(BATCHES, 0, last + 1)


def build(nc, t, out, layers=4):
    ctx = ExitStack()
    with ctx:
        def sb(name, shape, dt=F32):
            return ctx.enter_context(nc.sbuf_tensor(name, shape, dt))

        sems = {}

        def sem(name):
            if name not in sems:
                sems[name] = ctx.enter_context(nc.semaphore(name))
            return sems[name]

        bank = [ctx.enter_context(nc.psum_tensor(f"bank{i}", [128, 512], F32)) for i in range(8)]

        def cols(i, n=D):
            return slice(i * n, i * n + n)

        identf = sb("identf", [128, 128])
        identb = sb("identb", [128, 128], BF16)
        headmask = sb("headmask", [128, HEADS])
        sel1 = sb("sel1", [128, HEADS * 128], BF16)
        sel2 = sb("sel2", [128, HEADS * 128], BF16)
        neghalf = sb("neghalf", [128, G])
        NAT = ["L0_gnn_W_loop", "L0_gnn_Wg_loop", "L1_gnn_W", "L1_gnn_a_12", "L2_gnn_Wq", "L2_gnn_Wk",
               "L2_gnn_Wv", "L2_gnn_Wo", "L3_gnn_W", "L0_gnn_W_fwd", "L0_gnn_Wg_fwd", "L0_gnn_W_bwd",
               "L0_gnn_Wg_bwd"]
        nat_all = sb("nat_all", [128, len(NAT) * 128])
        nat = {n: nat_all[:, cols(i)] for i, n in enumerate(NAT)}
        hg_w = {k: sb(f"hg_w_{k}", [128, 2 * D]) for k in ("loop", "fwd", "bwd")}
        hg_bias = sb("hg_bias", [128, 2 * D])
        a_cols = sb("a_cols", [128, 2])
        qk_bias = sb("qk_bias", [128, 3])
        bv_row = sb("bv_row", [128, D])
        bo_row = sb("bo_row", [128, D])
        a3_row = sb("a3_row", [128, 2 * HD])
        w12 = sb("w12", [128, 2 * D])
        w1T = sb("w1T", [128, 128])
        a12T = sb("a12T", [128, 128])
        a12w = sb("a12w", [128, 128])
        bil = sb("bil", [128, 128])
        wa1 = sb("wa1", [128, 128])
        wa2 = sb("wa2", [128, 128])
        gT = {k: sb(f"gT_{k}", [128, 128]) for k in ("loop", "fwd", "bwd")}
        qT_w = sb("qT_w", [128, 128])
        kT_w = sb("kT_w", [128, 128])
        vT_w = sb("vT_w", [128, 128])
        wo_pad = sb("wo_pad", [128, HEADS * HP])
        woT_pad = sb("woT_pad", [128, 2 * D])
        a3_prod = sb("a3_prod", [128, 2 * D])
        a3_sum = sb("a3_sum", [128, 2 * HEADS])
        a3_w = sb("a3_w", [128, 128])

        X = sb("X", [128, GRAPHS * D])
        mask1 = sb("mask1", [128, GRAPHS * N], BF16)
        mask2 = sb("mask2", [128, GRAPHS * N], BF16)
        top = sb("top", [128, BATCHES])
        topmost = sb("topmost", [128, 1])
        toprow = sb("toprow", [1, 1])
        flag = sb("flag", [1, 1], I32)

        xs = [sb(f"xs{s}", [128, W]) for s in range(2)]
        adj = [sb(f"adj{s}", [128, W], I32) for s in range(2)]
        xT = [sb(f"xT{s}", [128, W]) for s in range(2)]
        xn = [sb(f"xn{s}", [128, W]) for s in range(2)]
        yb = [sb(f"yb{s}", [128, W]) for s in range(2)]
        bn = [sb(f"bn{s}", [128, G * 6]) for s in range(2)]
        mv = [sb(f"mv{s}", [128, G * 2]) for s in range(2)]
        ln = [sb(f"ln{s}", [128, 3 * G]) for s in range(2)]
        loopm = [sb(f"loopm{s}", [128, W]) for s in range(2)]
        hg = [sb(f"hg{s}", [128, 2 * W]) for s in range(2)]
        vals = [sb(f"vals{s}", [128, W]) for s in range(2)]
        uT = [hg[s][:, 0:W] for s in range(2)]
        y2 = [hg[s][:, W:2 * W] for s in range(2)]
        lk = [sb(f"lk{s}", [128, W]) for s in range(2)]
        e1 = [loopm[s] for s in range(2)]
        small_t = [vals[s] for s in range(2)]
        pT1 = [sb(f"pT1{s}", [128, W]) for s in range(2)]
        elu = [sb(f"elu{s}", [128, W]) for s in range(2)]
        nm1 = [sb(f"nm1{s}", [128, G]) for s in range(2)]
        den1 = [sb(f"den1{s}", [128, G]) for s in range(2)]
        rd1 = [sb(f"rd1{s}", [128, G]) for s in range(2)]
        qT = [uT[s] for s in range(2)]
        kT = sb("kT", [128, W])
        kexp = sb("kexp", [128, 2 * HEADS * W])
        vx = [sb(f"vx{s}", [128, G * HEADS * HP]) for s in range(2)]
        P = [sb(f"P{i}", [128, HQ * N]) for i in range(4)]
        pT = [sb(f"pT{i}", [128, HQ * N]) for i in range(2)]
        t3 = [sb(f"t3{i}", [128, HQ * N]) for i in range(2)]
        nmx = [sb(f"nmx{i}", [128, HQ]) for i in range(4)]
        den = [sb(f"den{i}", [128, HQ]) for i in range(4)]
        rd = [sb(f"rd{i}", [128, HQ]) for i in range(4)]
        rd3 = [sb(f"rd3{i}", [128, HEADS]) for i in range(2)]
        oT = [sb(f"oT{i}", [128, 2 * N]) for i in range(2)]
        eT = [sb(f"eT{s}", [128, W], BF16) for s in range(2)]
        er = sb("er", [128, W])

        block = ctx.enter_context(nc.Block())

        def v3(ap, a):
            return ap.rearrange("p (a c) -> p a c", a=a)

        def over(ap, shape):
            return ap.broadcast_to(shape)

        def x_of(b):
            return X[:, bass.ts(b, W)]

        def heads_of(mask, b, g):
            return mask[:, bass.ts(G * b + g, N)].unsqueeze(1).broadcast_to([128, HQ, N])

        prep = []

        def add(dst, lhsT, rhs=None, after=-1):
            prep.append((dst, lhsT, rhs, after))
            return len(prep) - 1

        for k in ("loop", "fwd", "bwd"):
            add(hg_w[k][:, 0:D], nat[f"L0_gnn_W_{k}"])
            p = add(gT[k][:], nat[f"L0_gnn_Wg_{k}"])
            add(hg_w[k][:, D:2 * D], nat[f"L0_gnn_W_{k}"], gT[k][:], p)
        p = add(w1T[:], nat["L1_gnn_W"])
        add(wa1[:], w1T[:], a_cols[:, 0:1].broadcast_to([128, 128]), p)
        add(wa2[:], w1T[:], a_cols[:, 1:2].broadcast_to([128, 128]), p)
        p = add(a12T[:], nat["L1_gnn_a_12"])
        p = add(a12w[:], a12T[:], w1T[:], p)
        add(bil[:], w1T[:], a12w[:], p)
        add(qT_w[:], nat["L2_gnn_Wq"])
        add(kT_w[:], nat["L2_gnn_Wk"])
        add(vT_w[:], nat["L2_gnn_Wv"])
        add(woT_pad[:, 0:D], wo_pad[:, 0:D])
        add(woT_pad[:, D:2 * D], wo_pad[:, D:2 * D])

        gx, ga = xs[0][:, 0:D], adj[0][:, 0:N]
        gaf, gxT = yb[0][:, 0:N], xT[0][:, 0:D]
        onehot = pT1[0][:, 0:2 * N]
        ghg, gvals = hg[0][:, 0:4 * D], vals[0][:, 0:2 * D]
        gbias = lk[0][:, 0:4 * D]
        gsum = kexp[:, 0:GRAPHS * D]
        rel = sb("rel", [128, 1])
        gmv, gbn, gln = mv[0][:, 0:2], bn[0][:, 0:6], ln[0][:, 0:3]
        STEPS = GRAPHS * (RELS + 1)

        def if_general(eng, body):
            eng.wait_ge(sem("flag_set"), 1)
            value = eng.value_load(flag[0:1, 0:1], min_val=0, max_val=1)
            with eng.If(value > 0):
                eng.wait_ge(sem("L0_norm_done"), BATCHES)
                body(eng)
                eng.wait_ge(sem("G_kept"), 16 * GRAPHS)

        def general_steps(eng, step, bias=None):
            step(0, 0, True, 0)
            with eng.Fori(1, GRAPHS) as g:
                step(g, g, True, 0)
            with eng.Fori(0, RELS) as r:
                if bias:
                    bias(r)
                with eng.Fori(0, GRAPHS) as g:
                    step(GRAPHS * (r + 1) + g, g, False, r)

        def general_sync(sp):
            def body(sp):
                def bias(r):
                    sp.wait_ge(sem("G_hg"), GRAPHS * (r + 1))
                    for i, n in enumerate(("b_fwd", "bg_fwd", "b_bwd", "bg_bwd")):
                        src = t[f"L0_gnn_{n}"][bass.ds(r, 1), :].rearrange("a d -> (a d)").partition_broadcast(128)
                        sp.dma_start(gbias[:, cols(i)], src).then_inc(sem("G_bias"), 16)

                def load(i, g, loop, r):
                    need(sp, sem("G_sum"), i)
                    sp.dma_start(gx, t["x"][bass.ds(g, 1)].rearrange("g n d -> (g n) d")).then_inc(sem("G_x"), 16)
                    sp.dma_start(ga, t["adj"][bass.ds(g, 1)].rearrange("g n d -> (g n) d")).then_inc(sem("G_adj"), 16)
                general_steps(sp, load, bias)

                def again(g):
                    sp.wait_ge(sem("G_sum"), STEPS)
                    need(sp, sem("G_y"), g)
                    sp.dma_start(gx, t["x"][bass.ds(g, 1)].rearrange("g n d -> (g n) d")).then_inc(sem("G_x"), 16)
                    sp.wait_ge(sem("G_norm"), g + 1)
                    sp.dma_start(X[:, bass.ts(g, D)], xn[0][:, 0:D]).then_inc(sem("G_kept"), 16)
                for s in range(2):
                    sp.wait_ge(sem(f"L0_kept{s}"), 16 * BATCHES // 2)
                again(0)
                with sp.Fori(1, GRAPHS) as g:
                    again(g)
            if_general(sp, body)

        def general_dve(dve):
            dve.wait_ge(sem("L0_masks_done"), BATCHES)
            nc.vector.tensor_reduce(topmost[:], top[:], AX.X, ALU.max).then_inc(sem("top_set"), 1)
            dve.wait_ge(sem("top_mm"), 1)
            nc.vector.tensor_reduce(toprow[:], bank[7][0:1, 0:128], AX.X, ALU.max).then_inc(sem("top_set"), 1)
            dve.wait_ge(sem("top_set"), 2)
            nc.vector.tensor_scalar(flag[:], toprow[:], 2.0, None, ALU.is_ge).then_inc(sem("flag_set"), 1)

            def body(dve):
                nc.vector.memset(rel[:], 1.0).then_inc(sem("G_rel"), 1)
                nc.vector.memset(gvals, 0.0).then_inc(sem("G_rel"), 1)
                dve.wait_ge(sem("G_rel"), 2)

                def bias(r):
                    dve.wait_ge(sem("G_onehot"), GRAPHS * (r + 1))
                    dve.wait_ge(sem("G_bias"), 64 * (r + 1))
                    nc.vector.tensor_scalar(rel[:], rel[:], 1.0, None, ALU.add).then_inc(sem("G_rel"), 1)

                def step(i, g, loop, r):
                    dve.wait_ge(sem("G_adj"), 16 * (i + 1))
                    nc.vector.tensor_copy(gaf, ga).then_inc(sem("G_adjf"), 1)
                    dve.wait_ge(sem("G_T_mm"), i + 1)
                    nc.vector.tensor_copy(gxT, bank[0][:, 0:128]).then_inc(sem("G_xT"), 1)
                    if not loop:
                        dve.wait_ge(sem("G_rel"), r + 3)
                        nc.vector.tensor_scalar(onehot[:, 0:N], bank[1][:, 0:N], rel[:], None, ALU.is_equal)
                    nc.vector.tensor_scalar(onehot[:, N:2 * N], gaf, rel[:], None, ALU.is_equal).then_inc(sem("G_onehot"), 1)
                    dve.wait_ge(sem("G_hg_mm"), i + 1)
                    if loop:
                        nc.vector.tensor_tensor(ghg[:, 0:2 * D], bank[2][:, 0:2 * D], hg_bias[:], ALU.add).then_inc(sem("G_hg"), 1)
                    else:
                        nc.vector.tensor_tensor(ghg, bank[2][:], gbias, ALU.add).then_inc(sem("G_hg"), 1)
                    dve.wait_ge(sem("G_gate"), i + 1)
                    n = 1 if loop else 2
                    h = v3(ghg, 4)
                    nc.vector.tensor_tensor(v3(gvals, 2)[:, 0:n, :], h[:, 0:2 * n:2, :], h[:, 1:2 * n:2, :], ALU.mult)\
                      .then_inc(sem("G_vals"), 1)
                    dve.wait_ge(sem("G_z_mm"), i + 1)
                    total = gsum[:, bass.ts(g, D)]
                    if loop:
                        nc.vector.tensor_copy(total, bank[3][:, 0:D]).then_inc(sem("G_sum"), 1)
                    else:
                        nc.vector.tensor_tensor(total, bank[3][:, 0:D], total, ALU.add).then_inc(sem("G_sum"), 1)
                general_steps(dve, step, bias)

                def norm(g):
                    dve.wait_ge(sem("G_sum"), STEPS)
                    dve.wait_ge(sem("G_x"), 16 * (STEPS + g + 1))
                    need(dve, sem("G_norm"), g)
                    nc.vector.scalar_tensor_tensor(yb[0][:, 0:D], gsum[:, bass.ts(g, D)], 0.0, gx, ALU.max, ALU.add)\
                      .then_inc(sem("G_y"), 1)
                    dve.wait_ge(sem("G_y"), g + 1)
                    nc.vector.bn_stats(gbn, yb[0][:, 0:D])
                    dve.drain()
                    nc.vector.bn_aggr(gmv, gbn)
                    dve.drain()
                    nc.vector.tensor_scalar(gln[:, 0:1], gmv[:, 0:1], -1.0, None, ALU.mult)
                    nc.vector.tensor_scalar(gln[:, 1:2], gmv[:, 1:2], EPS, None, ALU.add).then_inc(sem("G_stats"), 1)
                norm(0)
                with dve.Fori(1, GRAPHS) as g:
                    norm(g)
            if_general(dve, body)

        def general_act(act):
            def body(act):
                def step(i, g, loop, r):
                    act.wait_ge(sem("G_hg"), i + 1)
                    gate = v3(ghg, 4)[:, 1:(2 if loop else 4):2, :]
                    nc.scalar.activation(gate, gate, ACT.Sigmoid).then_inc(sem("G_gate"), 1)
                general_steps(act, step)
            if_general(act, body)

        def general_pe(pe):
            pe.wait_ge(sem("top_set"), 1)
            nc.tensor.transpose(bank[7][0:1, 0:128], topmost[:], identf[:]).then_inc(sem("top_mm"), 1)

            def body(pe):
                def step(i, g, loop, r):
                    mm = nc.tensor.matmul
                    pe.wait_ge(sem("G_x"), 16 * (i + 1))
                    pe.wait_ge(sem("G_adjf"), i + 1)
                    nc.tensor.transpose(bank[0][:, 0:128], gx, identf[:])
                    nc.tensor.transpose(bank[1][:, 0:128], gaf, identf[:]).then_inc(sem("G_T_mm"), 1)
                    pe.wait_ge(sem("G_onehot"), i + 1)
                    if loop:
                        mm(bank[2][:, 0:2 * D], gxT, hg_w["loop"][:], start=True, stop=True).then_inc(sem("G_hg_mm"), 1)
                    else:
                        mm(bank[2][:, 0:2 * D], gxT, hg_w["fwd"][:], start=True, stop=True)
                        mm(bank[2][:, 2 * D:4 * D], gxT, hg_w["bwd"][:], start=True, stop=True).then_inc(sem("G_hg_mm"), 1)
                    pe.wait_ge(sem("G_vals"), i + 1)
                    if loop:
                        mm(bank[3][:, 0:D], onehot[:, N:2 * N], gvals[:, 0:D], start=True, stop=True).then_inc(sem("G_z_mm"), 1)
                    else:
                        mm(bank[3][:, 0:D], onehot[:, 0:N], gvals[:, 0:D], start=True, stop=False)
                        mm(bank[3][:, 0:D], onehot[:, N:2 * N], gvals[:, D:2 * D], start=False, stop=True).then_inc(sem("G_z_mm"), 1)
                general_steps(pe, step)
            if_general(pe, body)

        def general_pool(pool):
            def body(pool):
                def norm(g):
                    need(pool, sem("G_kept"), 16 * g)
                    pool.wait_ge(sem("G_stats"), g + 1)
                    nc.gpsimd.tensor_tensor(gln[:, 2:3], gln[:, 1:2], neghalf[:, 0:1], ALU.pow)
                    pool.drain()
                    nc.gpsimd.tensor_scalar(xn[0][:, 0:D], yb[0][:, 0:D], gln[:, 0:1], gln[:, 2:3], ALU.add, ALU.mult)\
                      .then_inc(sem("G_norm"), 1)
                norm(0)
                with pool.Fori(1, GRAPHS) as g:
                    norm(g)
            if_general(pool, body)

        @block.sync
        def _(sp):
            def load(b, s, turn):
                need(sp, sem("L0_y_done"), b - 1)
                need(sp, sem("L0_masks_done"), b - 1)
                sp.dma_start(v3(xs[s][:], G), t["x"][bass.ts(b, G)].rearrange("g n d -> n g d"))\
                  .then_inc(sem(f"x_loaded{s}"), 16)
                sp.dma_start(v3(adj[s][:], G), t["adj"][bass.ts(b, G)].rearrange("g n m -> n g m"))\
                  .then_inc(sem(f"adj_loaded{s}"), 16)

            def keep(L, b, s, turn):
                sp.wait_ge(sem(f"L{L}_norm_done"), b + 1)
                if L < layers - 1:
                    sp.dma_start(x_of(b), xn[s][:]).then_inc(sem(f"L{L}_kept{s}"), 16)
                else:
                    sp.dma_start(out[bass.ts(b, G)].rearrange("g n d -> n g d"), v3(xn[s][:], G))\
                      .then_inc(sem(f"L{L}_kept{s}"), 16)

            def layer(L, load, lag):
                def both(b, s, turn):
                    if real(b):
                        load(b, s, turn)
                    if real(b - lag):
                        keep(L, b - lag, (s + lag) % 2, turn)
                every_batch(sp, both)
                for b in range(BATCHES, BATCHES + lag):
                    both(b, b % 2, b // 2)

            def stage(L):
                def load(b, s, turn):
                    if isinstance(b, int) and b < 2:
                        sp.wait_ge(sem("L0_y_done" if L == 1 else f"L{L - 1}_xT_mm"), BATCHES - 1 + b)
                        free = None
                    else:
                        free = sp.snap(b - 1)
                        sp.wait_ge(sem(f"L{L}_xT_mm"), free)
                    sp.wait_ge(sem(f"L{L - 1}_kept{s}"), 16 * (turn + 1))
                    sp.dma_start(xs[s][:], x_of(b)).then_inc(sem(f"L{L}_staged{s}"), 16)
                return load

            layer(0, load, 2)
            general_sync(sp)
            for L, lag in ((1, 3), (2, 4), (3, 4)):
                if L < layers:
                    layer(L, stage(L), lag)
            for s in range(2):
                sp.wait_ge(sem(f"L{layers - 1}_kept{s}"), 16 * BATCHES // 2)

        def norm_pool(pool, L, b, s, turn):
            if isinstance(b, int) and b < 2:
                if L > 0:
                    pool.wait_ge(sem(f"L{L - 1}_kept{s}"), 16 * BATCHES // 2)
            else:
                pool.wait_ge(sem(f"L{L}_kept{s}"), 16 * turn)
            pool.wait_ge(sem(f"L{L}_stats_done"), b + 1)
            nc.gpsimd.tensor_tensor(ln[s][:, 2 * G:3 * G], ln[s][:, G:2 * G], neghalf[:], ALU.pow)
            pool.drain()
            for g in range(G):
                last = nc.gpsimd.tensor_scalar(xn[s][:, cols(g)], yb[s][:, cols(g)], ln[s][:, g:g + 1],
                                               ln[s][:, 2 * G + g:2 * G + g + 1], ALU.add, ALU.mult)
            last.then_inc(sem(f"L{L}_norm_done"), 1)

        def y_slot_free(dve, L, b):
            if isinstance(b, int) and b < 2:
                if L > 0:
                    dve.wait_ge(sem(f"L{L - 1}_norm_done"), BATCHES - 1 + b)
            else:
                dve.wait_ge(sem(f"L{L}_norm_done"), b - 1)

        def stats_dve(dve, L, b, s):
            dve.wait_ge(sem(f"L{L}_y_done"), b + 1)
            for g in range(G):
                nc.vector.bn_stats(bn[s][:, cols(g, 6)], yb[s][:, cols(g)])
            dve.drain()
            for g in range(G):
                nc.vector.bn_aggr(mv[s][:, cols(g, 2)], bn[s][:, cols(g, 6)])
            dve.drain()
            m = v3(mv[s][:], G)
            nc.vector.tensor_scalar(ln[s][:, 0:G], m[:, :, 0], -1.0, None, ALU.mult)
            nc.vector.tensor_scalar(ln[s][:, G:2 * G], m[:, :, 1], EPS, None, ALU.add)\
              .then_inc(sem(f"L{L}_stats_done"), 1)

        @block.gpsimd
        def _(pool):
            nc.gpsimd.memset(identf[:], 0.0)
            nc.gpsimd.memset(sel1[:], 0.0)
            nc.gpsimd.memset(sel2[:], 0.0)
            nc.gpsimd.memset(headmask[:], 1.0)
            nc.gpsimd.memset(neghalf[:], -0.5).then_inc(sem("pool_set"), 1)
            steps = 1
            pool.wait_ge(sem("pool_set"), steps)

            def select(out_, pattern, base, op=ALU.not_equal, fill=1.0, step=1):
                nonlocal steps
                nc.gpsimd.affine_select(out=out_, in_=out_, compare_op=op, fill=fill, base=base,
                                        pattern=pattern, channel_multiplier=step).then_inc(sem("pool_set"), 1)
                steps += 1
                pool.wait_ge(sem("pool_set"), steps)

            select(identf[:], [[-1, 128]], 0)
            nc.gpsimd.tensor_copy(identb[:], identf[:]).then_inc(sem("ident"), 1)
            select(headmask[:], [[-HD, HEADS]], 0, ALU.is_ge, 0.0)
            select(headmask[:], [[HD, HEADS]], HD - 1, ALU.is_ge, 0.0, -1)
            for part in range(3):
                select(sel2[:].rearrange("p (h c) -> p h c", h=HEADS), [[-1, HEADS], [0, 128]], -32 * part)
                select(sel1[:].rearrange("p (h c) -> p h c", h=HEADS), [[-1, HEADS], [0, 128]], -32 * part - HEADS)
            nc.gpsimd.memset(er[:, 0:1], 0.0).then_inc(sem("pool_ready"), 1)

            def layer0(b, s, turn):
                pool.wait_ge(sem("L0_gate"), b + 1)
                need(pool, sem("L0_z_mm"), b - 1)
                hgv = v3(hg[s][:], 2 * G)
                nc.gpsimd.tensor_tensor(v3(vals[s][:], G), hgv[:, 0:2 * G:2, :], hgv[:, 1:2 * G:2, :], ALU.mult)\
                  .then_inc(sem("L0_vals"), 1)
                if real(b - 1):
                    norm_pool(pool, 0, b - 1, 1 - s, turn - 1 + s)
            every_batch(pool, layer0)
            norm_pool(pool, 0, BATCHES - 1, 1, BATCHES // 2 - 1)
            general_pool(pool)
            if layers > 1:
                every_batch(pool, lambda b, s, turn: norm_pool(pool, 1, b, s, turn))
            if layers > 2:
                def layer2(b, s, turn):
                    if real(b + 1):
                        pool.wait_ge(sem("L2_k"), b + 2)
                        need(pool, sem("L2_s_mm"), UNITS * b)
                        nc.gpsimd.tensor_tensor(kexp[:, cols((1 - s) * HEADS, W)], kT[:],
                                                headmask[:, 0:1].broadcast_to([128, W]), ALU.mult)
                        for h in range(1, HEADS):
                            last = nc.gpsimd.tensor_scalar(kexp[:, cols((1 - s) * HEADS + h, W)], kT[:],
                                                           headmask[:, h:h + 1], 1.0, ALU.mult, ALU.mult)
                        last.then_inc(sem("L2_kexp"), 1)
                    if real(b - 1):
                        norm_pool(pool, 2, b - 1, 1 - s, turn - 1 + s)
                every_batch(pool, layer2, before=True, after=True)
            if layers > 3:
                def layer3(b, s, turn):
                    for u in range(UNITS):
                        if real(b):
                            pool.wait_ge(sem("L3_max"), UNITS * b + u + 1)
                            nc.gpsimd.tensor_tensor(v3(P[u % 4][:], HQ), v3(P[u % 4][:], HQ),
                                                    nmx[u % 4][:].unsqueeze(2).broadcast_to([128, HQ, N]), ALU.add)\
                              .then_inc(sem("L3_less_max"), 1)
                        if u == 1 and real(b - 2):
                            norm_pool(pool, 3, b - 2, s, turn - 1)
                    if isinstance(b, int) and b == BATCHES:
                        norm_pool(pool, 3, b - 1, 1 - s, turn - 1 + s)
                every_batch(pool, layer3, after=True)


        @block.scalar
        def _(act):
            def row(ap, n):
                return ap.rearrange("a n -> (a n)").partition_broadcast(128) if len(ap.shape) == 2 else ap.partition_broadcast(128)

            def col(ap):
                return ap.rearrange("n a -> n a") if len(ap.shape) == 2 else ap.unsqueeze(1)
            loads = [(nat[n], t[n][:, :]) for n in NAT]
            loads += [(hg_bias[:, 0:D], row(t["L0_gnn_b_loop"], D)), (hg_bias[:, D:2 * D], row(t["L0_gnn_bg_loop"], D)),
                      (a_cols[:, 0:1], col(t["L1_gnn_a_1"])), (a_cols[:, 1:2], col(t["L1_gnn_a_2"])),
                      (w12[:, 0:D], t["L1_gnn_W_1"][:, :]), (w12[:, D:2 * D], t["L1_gnn_W_2"][:, :]),
                      (qk_bias[:, 0:1], col(t["L2_gnn_bq"])), (qk_bias[:, 1:2], col(t["L2_gnn_bk"])),
                      (bv_row[:], row(t["L2_gnn_bv"], D)), (bo_row[:], row(t["L2_gnn_bo"], D)),
                      (a3_row[:], row(t["L3_gnn_a"], 2 * HD))]
            for dst, src in loads:
                act.dma_start(dst, src).then_inc(sem("params"), 16)
            sems["n_params"] = 16 * len(loads)
            act.wait_ge(sem("params"), 16 * len(loads))
            nc.scalar.mul(qk_bias[:, 2:3], qk_bias[:, 0:1], HD ** -0.5).then_inc(sem("bq_scaled"), 1)

            def layer0(b, s, turn):
                act.wait_ge(sem("L0_xT_mm"), b + 1)
                need(act, sem("L0_hg_mm"), b - 1)
                nc.scalar.copy(xT[s][:], bank[0][:]).then_inc(sem("L0_xT"), 1)
                act.wait_ge(sem("L0_hg"), b + 1)
                g = v3(hg[s][:], 2 * G)[:, 1:2 * G:2, :]
                nc.scalar.activation(g, g, ACT.Sigmoid).then_inc(sem("L0_gate"), 1)
            every_batch(act, layer0)
            general_act(act)

            def l1_front(b, s):
                act.wait_ge(sem("L1_xT_mm"), b + 1)
                need(act, sem("L1_z_mm"), b - 1)
                nc.scalar.copy(xT[s][:], bank[0][:]).then_inc(sem("L1_xT"), 1)
                act.wait_ge(sem("L1_u_mm"), b + 1)
                nc.scalar.activation(uT[s], bank[1][:], ACT.Identity, bias=wa1[:, 0:1]).then_inc(sem("L1_uT"), 1)
                act.wait_ge(sem("L1_y2_mm"), b + 1)
                nc.scalar.copy(y2[s], bank[3][:]).then_inc(sem("L1_y2"), 1)
                act.wait_ge(sem("L1_logits_mm"), b + 1)
                need(act, sem("L1_leaky"), b - 1)
                nc.scalar.mul(small_t[s][:], bank[2][:], ALPHA).then_inc(sem("L1_scaled"), 1)
                act.wait_ge(sem("L1_max"), b + 1)
                need(act, sem("L1_pT_mm"), b - 1)
                for g in range(G):
                    last = nc.scalar.activation(e1[s][:, cols(g)], lk[s][:, cols(g)], ACT.Exp,
                                                bias=nm1[s][:, g:g + 1], accum_out=den1[s][:, g:g + 1])
                last.then_inc(sem("L1_exp"), 1)

            def l1_back(b, s):
                act.wait_ge(sem("L1_pT_mm"), b + 1)
                need(act, sem("L1_z_mm"), b - 1)
                nc.scalar.copy(pT1[s][:], bank[4][:]).then_inc(sem("L1_pT"), 1)
                act.wait_ge(sem("L1_neg"), b + 1)
                nc.scalar.activation(elu[s][:], elu[s][:], ACT.Exp).then_inc(sem("L1_elu_exp"), 1)

            def layer1(b, s, turn):
                l1_front(b, s)
                if real(b - 1):
                    l1_back(b - 1, 1 - s)
            if layers > 1:
                every_batch(act, layer1)
                l1_back(BATCHES - 1, 1)

            def copy_pT(L, b, u, lag):
                bb, uu = b + (u - lag) // UNITS, (u - lag) % UNITS
                if real(bb):
                    act.wait_ge(sem(f"L{L}_pT_mm"), UNITS * bb + uu + 1)
                    need(act, sem(f"L{L}_pv_mm"), UNITS * bb + uu - 1)
                    nc.scalar.copy(pT[uu % 2][:], bank[2 + uu % 2][:]).then_inc(sem(f"L{L}_pT"), 1)

            def copy_oT(L, b, u, lag):
                if (u - lag) % 2 == 0:
                    bb, g = b + (u - lag) // UNITS, (u - lag) % UNITS // 2
                    if real(bb):
                        act.wait_ge(sem(f"L{L}_pv_mm"), UNITS * bb + 2 * g + 2)
                        need(act, sem(f"L{L}_out_mm"), G * bb + g - 1)
                        nc.scalar.copy(oT[g % 2][:], bank[6][:, cols(g % 2, 2 * N)]).then_inc(sem(f"L{L}_oT"), 1)

            def layer2(b, s, turn):
                for u in range(UNITS):
                    if u == 6 and real(b + 1):
                        act.wait_ge(sem("L2_q_mm"), b + 2)
                        need(act, sem("L2_s_mm"), UNITS * b)
                        nc.scalar.activation(qT[1 - s], bank[4][:], ACT.Identity, bias=qk_bias[:, 2:3],
                                             scale=HD ** -0.5).then_inc(sem("L2_q"), 1)
                    copy_oT(2, b, u, 5)
                    if real(b):
                        U = UNITS * b + u
                        act.wait_ge(sem("L2_max"), U + 1)
                        need(act, sem("L2_pT_mm"), U - 3)
                        for j in range(HQ):
                            last = nc.scalar.activation(P[u % 4][:, cols(j)], bank[u % 2][:, cols(j)], ACT.Exp,
                                                        bias=nmx[u % 4][:, j:j + 1], accum_out=den[u % 4][:, j:j + 1])
                        last.then_inc(sem("L2_exp"), 1)
                    copy_pT(2, b, u, 2)
            if layers > 2:
                every_batch(act, layer2, before=True, after=True)

            def layer3(b, s, turn):
                for u in range(UNITS):
                    if u == 2 and real(b + 1):
                        act.wait_ge(sem("L3_xT_mm"), b + 2)
                        need(act, sem("L3_wh_mm"), b)
                        nc.scalar.copy(xT[1 - s][:], bank[4][:]).then_inc(sem("L3_xT"), 1)
                    if u == 7 and real(b + 1):
                        act.wait_ge(sem("L3_wh_mm"), b + 2)
                        need(act, sem("L3_pv_mm"), UNITS * b)
                        nc.scalar.copy(vx[1 - s][:].rearrange("p (g h c) -> p g h c", g=G, h=HEADS)[:, :, :, 0:HD],
                                       bank[4][:].rearrange("p (g h c) -> p g h c", g=G, h=HEADS)).then_inc(sem("L3_wh"), 1)
                    if real(b):
                        U = UNITS * b + u
                        act.wait_ge(sem("L3_s_mm"), U + 1)
                        need(act, sem("L3_leaky"), U - 1)
                        nc.scalar.mul(t3[u % 2][:], bank[u % 2][:], ALPHA).then_inc(sem("L3_scaled"), 1)
                    copy_oT(3, b, u, 6)
                    bb, uu = b + (u - 1) // UNITS, (u - 1) % UNITS
                    if real(bb):
                        act.wait_ge(sem("L3_less_max"), UNITS * bb + uu + 1)
                        nc.scalar.activation(P[uu % 4][:], P[uu % 4][:], ACT.Exp).then_inc(sem("L3_exp"), 1)
                    copy_pT(3, b, u, 3)
            if layers > 3:
                every_batch(act, layer3, before=True, after=True)


        @block.vector
        def _(dve):
            for s in range(2):
                nc.vector.memset(vx[s][:], 0.0)
            nc.vector.memset(wo_pad[:], 0.0)
            nc.vector.memset(a3_w[:], 0.0).then_inc(sem("dve_set"), 1)
            dve.wait_ge(sem("dve_set"), 1)
            for s in range(2):
                nc.vector.memset(vx[s][:].rearrange("p (a c) -> p a c", c=HP)[:, :, HD:HD + 1], 1.0)
            dve.wait_ge(sem("params"), sems["n_params"])
            nc.vector.tensor_copy(v3(wo_pad[:], HEADS)[:, :, 0:HD], v3(nat["L2_gnn_Wo"], HEADS))\
              .then_inc(sem("wo_padded"), 1)
            for half in range(2):
                nc.vector.tensor_tensor(v3(a3_prod[:, cols(half)], HEADS), v3(nat["L3_gnn_W"], HEADS),
                                        a3_row[:, cols(half, HD)].unsqueeze(1).broadcast_to([128, HEADS, HD]), ALU.mult)\
                  .then_inc(sem("dve_set"), 1)
            dve.wait_ge(sem("dve_set"), 3)
            nc.vector.tensor_reduce(a3_sum[:], v3(a3_prod[:], 2 * HEADS), AX.X, ALU.add).then_inc(sem("dve_set"), 1)
            dve.wait_ge(sem("dve_set"), 4)
            for part in range(3):
                nc.vector.tensor_copy(a3_w[:, 32 * part:32 * part + HEADS], a3_sum[:, HEADS:2 * HEADS])
                nc.vector.tensor_copy(a3_w[:, 32 * part + HEADS:32 * part + 2 * HEADS], a3_sum[:, 0:HEADS])\
                  .then_inc(sem("dve_set"), 1)
            for i, (dst, *_) in enumerate(prep):
                dve.wait_ge(sem("prep_mm"), i + 1)
                nc.vector.tensor_copy(dst, bank[i % 4][:, 0:dst.shape[-1]]).then_inc(sem("prep"), 1)

            def l0_front(b, s, turn):
                dve.wait_ge(sem(f"adj_loaded{s}"), 16 * (turn + 1))
                need(dve, sem("L0_z_mm"), b - 1)
                nc.vector.tensor_scalar(loopm[s][:], adj[s][:], 1.0, None, ALU.is_equal).then_inc(sem("L0_loopm"), 1)
                nc.vector.tensor_scalar(mask1[:, bass.ts(b, W)], adj[s][:], 0.0, MASKED, ALU.is_le, ALU.mult)
                nc.vector.tensor_scalar(mask2[:, bass.ts(b, W)], adj[s][:], 0.0, MASKED, ALU.is_equal, ALU.mult)
                nc.vector.tensor_reduce(top[:, bass.ds(b, 1)], adj[s][:], AX.X, ALU.max).then_inc(sem("L0_masks_done"), 1)
                dve.wait_ge(sem("L0_hg_mm"), b + 1)
                need(dve, sem("L0_vals"), b - 1)
                for i in range(2):
                    last = nc.vector.tensor_tensor(
                        v3(hg[s][:, cols(i, W)], 2), v3(bank[1 + i][:], 2),
                        hg_bias[:].unsqueeze(1).broadcast_to([128, 2, 2 * D]), ALU.add)
                last.then_inc(sem("L0_hg"), 1)

            def l0_back(b, s):
                dve.wait_ge(sem("L0_z_mm"), b + 1)
                y_slot_free(dve, 0, b)
                nc.vector.scalar_tensor_tensor(yb[s][:], bank[3][:], 0.0, xs[s][:], ALU.max, ALU.add)\
                  .then_inc(sem("L0_y_done"), 1)
                stats_dve(dve, 0, b, s)

            def layer0(b, s, turn):
                l0_front(b, s, turn)
                if real(b - 1):
                    l0_back(b - 1, 1 - s)
            every_batch(dve, layer0)
            l0_back(BATCHES - 1, 1)
            general_dve(dve)

            def l1_back(b, s):
                dve.wait_ge(sem("L1_z_mm"), b + 1)
                nc.vector.tensor_scalar(elu[s][:], bank[5][:], 0.0, None, ALU.min).then_inc(sem("L1_neg"), 1)
                dve.wait_ge(sem("L1_elu_exp"), b + 1)
                nc.vector.scalar_tensor_tensor(elu[s][:], bank[5][:], 0.0, elu[s][:], ALU.max, ALU.add)\
                  .then_inc(sem("L1_elu"), 1)
                dve.wait_ge(sem("L1_elu"), b + 1)
                y_slot_free(dve, 1, b)
                nc.vector.scalar_tensor_tensor(yb[s][:], elu[s][:], -1.0, x_of(b), ALU.add, ALU.add)\
                  .then_inc(sem("L1_y_done"), 1)
                stats_dve(dve, 1, b, s)

            def layer1(b, s, turn):
                dve.wait_ge(sem("L1_scaled"), b + 1)
                need(dve, sem("L1_exp"), b - 1)
                nc.vector.tensor_tensor(lk[s][:], bank[2][:], small_t[s][:], ALU.max).then_inc(sem("L1_leaky"), 1)
                dve.wait_ge(sem("L1_leaky"), b + 1)
                nc.vector.tensor_reduce(nm1[s][:], v3(lk[s][:], G), AX.X, ALU.max, negate=True).then_inc(sem("L1_max"), 1)
                if real(b - 1):
                    l1_back(b - 1, 1 - s)
                dve.wait_ge(sem("L1_exp"), b + 1)
                nc.vector.reciprocal(rd1[s][:], den1[s][:]).then_inc(sem("L1_rden"), 1)
                dve.wait_ge(sem("L1_rden"), b + 1)
                nc.vector.tensor_tensor(v3(e1[s][:], G), v3(e1[s][:], G), rd1[s][:].unsqueeze(2).broadcast_to([128, G, N]),
                                        ALU.mult).then_inc(sem("L1_p"), 1)
            if layers > 1:
                every_batch(dve, layer1)
                l1_back(BATCHES - 1, 1)

            def layer2(b, s, turn):
                for u in range(UNITS):
                    if real(b):
                        U = UNITS * b + u
                        dve.wait_ge(sem("L2_s_mm"), U + 1)
                        need(dve, sem("L2_exp"), U - 3)
                        nc.vector.tensor_reduce(nmx[u % 4][:], v3(bank[u % 2][:], HQ), AX.X, ALU.max, negate=True)\
                          .then_inc(sem("L2_max"), 1)
                    if u == 2 and real(b + 1):
                        dve.wait_ge(sem("L2_xT_mm"), b + 2)
                        need(dve, sem("L2_v_mm"), b)
                        nc.vector.tensor_copy(xT[1 - s][:], bank[4][:]).then_inc(sem("L2_xT"), 1)
                    if u == 4 and real(b + 1):
                        dve.wait_ge(sem("L2_k_mm"), b + 2)
                        need(dve, sem("L2_kexp"), b + 1)
                        nc.vector.tensor_scalar(kT[:], bank[5][:], qk_bias[:, 1:2], None, ALU.add).then_inc(sem("L2_k"), 1)
                    if u == 0 and real(b):
                        dve.wait_ge(sem("L2_v_mm"), b + 1)
                        need(dve, sem("L2_pv_mm"), UNITS * (b - 1))
                        nc.vector.tensor_tensor(
                            vx[s][:].rearrange("p (g h c) -> p g h c", g=G, h=HEADS)[:, :, :, 0:HD],
                            bank[5][:].rearrange("p (g h c) -> p g h c", g=G, h=HEADS),
                            bv_row[:].rearrange("p (h c) -> p h c", h=HEADS).unsqueeze(1).broadcast_to([128, G, HEADS, HD]),
                            ALU.add).then_inc(sem("L2_v"), 1)
                    bb, uu = b + (u - 1) // UNITS, (u - 1) % UNITS
                    if real(bb):
                        U = UNITS * bb + uu
                        dve.wait_ge(sem("L2_exp"), U + 1)
                        nc.vector.reciprocal(rd[uu % 4][:], den[uu % 4][:]).then_inc(sem("L2_rden"), 1)
                        dve.wait_ge(sem("L2_rden"), U + 1)
                        nc.vector.tensor_tensor(v3(P[uu % 4][:], HQ), v3(P[uu % 4][:], HQ),
                                                rd[uu % 4][:].unsqueeze(2).broadcast_to([128, HQ, N]), ALU.mult)\
                          .then_inc(sem("L2_p"), 1)
                    if u == 5 and real(b - 1):
                        dve.wait_ge(sem("L2_out_mm"), G * b)
                        y_slot_free(dve, 2, b - 1)
                        nc.vector.tensor_tensor(v3(yb[1 - s][:], G), v3(bank[7][:], G),
                                                bo_row[:].unsqueeze(1).broadcast_to([128, G, D]), ALU.add)\
                          .then_inc(sem("L2_out"), 1)
                        dve.wait_ge(sem("L2_out"), b)
                        nc.vector.tensor_tensor(yb[1 - s][:], yb[1 - s][:], x_of(b - 1), ALU.add)\
                          .then_inc(sem("L2_y_done"), 1)
                    if u == 6 and real(b - 1):
                        stats_dve(dve, 2, b - 1, 1 - s)
            if layers > 2:
                every_batch(dve, layer2, before=True, after=True)

            def layer3(b, s, turn):
                for u in range(UNITS):
                    if real(b):
                        U = UNITS * b + u
                        dve.wait_ge(sem("L3_scaled"), U + 1)
                        need(dve, sem("L3_pT_mm"), U - 3)
                        nc.vector.tensor_tensor(P[u % 4][:], bank[u % 2][:], t3[u % 2][:], ALU.max)\
                          .then_inc(sem("L3_leaky"), 1)
                        dve.wait_ge(sem("L3_leaky"), U + 1)
                        need(dve, sem("L3_less_max"), U - 3)
                        nc.vector.tensor_reduce(nmx[u % 4][:], v3(P[u % 4][:], HQ), AX.X, ALU.max, negate=True)\
                          .then_inc(sem("L3_max"), 1)
                    if u == 4 and real(b + 1):
                        dve.wait_ge(sem("L3_e_mm"), b + 2)
                        need(dve, sem("L3_s_mm"), UNITS * b)
                        dst = eT[1 - s]
                        nc.vector.tensor_copy(dst[:], bank[5][:]).then_inc(sem("L3_part"), 1)
                        dve.wait_ge(sem("L3_part"), 4 * (b + 1) + 1)
                        nc.vector.tensor_tensor(er[:], bank[5][:], dst[:], ALU.subtract).then_inc(sem("L3_part"), 1)
                        dve.wait_ge(sem("L3_part"), 4 * (b + 1) + 2)
                        nc.vector.tensor_copy(dst[32:64, :], er[32:64, :])
                        nc.vector.tensor_copy(dst[64:96, :], er[64:96, :]).then_inc(sem("L3_part"), 1)
                        dve.wait_ge(sem("L3_part"), 4 * (b + 1) + 3)
                        nc.vector.tensor_tensor(er[64:96, :], er[64:96, :], dst[64:96, :], ALU.subtract)\
                          .then_inc(sem("L3_part"), 1)
                        dve.wait_ge(sem("L3_part"), 4 * (b + 1) + 4)
                        nc.vector.tensor_copy(dst[64:96, :], er[64:96, :]).then_inc(sem("L3_e"), 1)
                    if u % 2 == 0:
                        bb, g = b + (u - 8) // UNITS, u // 2
                        if real(bb):
                            o = bank[7][:, cols(g % 2, 2 * N)].rearrange("p (h c) -> p h c", h=HEADS)
                            dve.wait_ge(sem("L3_out_mm"), G * bb + g + 1)
                            if g == 0:
                                y_slot_free(dve, 3, bb)
                            nc.vector.reciprocal(rd3[g % 2][:], o[:, :, HD]).then_inc(sem("L3_rden"), 1)
                            dve.wait_ge(sem("L3_rden"), G * bb + g + 1)
                            nc.vector.tensor_tensor(v3(yb[1 - s][:, cols(g)], HEADS), o[:, :, 0:HD],
                                                    rd3[g % 2][:].unsqueeze(2).broadcast_to([128, HEADS, HD]), ALU.mult)\
                              .then_inc(sem("L3_out"), 1)
                    if u == 7 and real(b - 1):
                        dve.wait_ge(sem("L3_out"), G * b)
                        nc.vector.tensor_tensor(yb[1 - s][:], yb[1 - s][:], x_of(b - 1), ALU.add)\
                          .then_inc(sem("L3_y_done"), 1)
                        stats_dve(dve, 3, b - 1, 1 - s)
            if layers > 3:
                every_batch(dve, layer3, before=True, after=True)


        @block.tensor
        def _(pe):
            mm = nc.tensor.matmul
            pe.wait_ge(sem("ident"), 1)
            pe.wait_ge(sem("params"), sems["n_params"])
            pe.wait_ge(sem("wo_padded"), 1)
            for i, (dst, lhsT, rhs, after) in enumerate(prep):
                need(pe, sem("prep"), max(after + 1, i - 3))
                o = bank[i % 4][:, 0:128]
                if rhs is None:
                    last = nc.tensor.transpose(o, lhsT, identf[:])
                else:
                    last = mm(o, lhsT, rhs, start=True, stop=True)
                last.then_inc(sem("prep_mm"), 1)
            pe.wait_ge(sem("prep"), len(prep))
            pe.wait_ge(sem("pool_ready"), 1)

            def transposes(dst, src, n):
                for i in range(n):
                    last = nc.tensor.transpose(dst[:, cols(i)], src[:, cols(i)], identf[:])
                return last

            def l0_front(b, s, turn):
                pe.wait_ge(sem(f"x_loaded{s}"), 16 * (turn + 1))
                need(pe, sem("L0_xT"), b)
                transposes(bank[0], xs[s], G).then_inc(sem("L0_xT_mm"), 1)
                pe.wait_ge(sem("L0_xT"), b + 1)
                need(pe, sem("L0_hg"), b)
                for g in range(G):
                    last = mm(bank[1 + g // 2][:, cols(g % 2, 2 * D)], xT[s][:, cols(g)], hg_w["loop"][:], start=True, stop=True)
                last.then_inc(sem("L0_hg_mm"), 1)

            def l0_back(b, s):
                pe.wait_ge(sem("L0_vals"), b + 1)
                pe.wait_ge(sem("L0_loopm"), b + 1)
                need(pe, sem("L0_y_done"), b)
                for g in range(G):
                    last = mm(bank[3][:, cols(g)], loopm[s][:, cols(g)], vals[s][:, cols(g)], start=True, stop=True)
                last.then_inc(sem("L0_z_mm"), 1)

            def layer0(b, s, turn):
                l0_front(b, s, turn)
                if real(b - 1):
                    l0_back(b - 1, 1 - s)
            every_batch(pe, layer0)
            l0_back(BATCHES - 1, 1)
            general_pe(pe)

            def l1_front(b, s, turn):
                pe.wait_ge(sem(f"L1_staged{s}"), 16 * (turn + 1))
                need(pe, sem("L1_xT"), b)
                transposes(bank[0], xs[s], G).then_inc(sem("L1_xT_mm"), 1)
                pe.wait_ge(sem("L1_xT"), b + 1)
                need(pe, sem("L1_uT"), b)
                mm(bank[1][:], bil[:], xT[s][:], start=True, stop=True).then_inc(sem("L1_u_mm"), 1)
                need_or(pe, sem("L1_y2"), b, sem("L0_y_done"), BATCHES)
                for g in range(G):
                    last = mm(bank[3][:, cols(g)], xT[s][:, cols(g)], w12[:, D:2 * D], start=True, stop=True)
                last.then_inc(sem("L1_y2_mm"), 1)
                need(pe, sem("L1_leaky"), b)
                mm(bank[2][:], identb[:], mask1[:, bass.ts(b, W)], start=True, stop=False)
                for g in range(G):
                    mm(bank[2][:, cols(g)], xT[s][:, cols(g)], wa2[:], start=False, stop=False)
                pe.wait_ge(sem("L1_uT"), b + 1)
                for g in range(G):
                    last = mm(bank[2][:, cols(g)], uT[s][:, cols(g)], xT[s][:, cols(g)], start=False, stop=g == G - 1)
                last.then_inc(sem("L1_logits_mm"), 1)

            def l1_back(b, s):
                pe.wait_ge(sem("L1_p"), b + 1)
                need(pe, sem("L1_pT"), b)
                transposes(bank[4], e1[s], G).then_inc(sem("L1_pT_mm"), 1)
                pe.wait_ge(sem("L1_pT"), b + 1)
                need(pe, sem("L1_elu"), b)
                for g in range(G):
                    mm(bank[5][:, cols(g)], xT[s][:, cols(g)], w12[:, 0:D], start=True, stop=False)
                    last = mm(bank[5][:, cols(g)], pT1[s][:, cols(g)], y2[s][:, cols(g)], start=False, stop=True)
                last.then_inc(sem("L1_z_mm"), 1)

            def layer1(b, s, turn):
                l1_front(b, s, turn)
                if real(b - 1):
                    l1_back(b - 1, 1 - s)
            if layers > 1:
                every_batch(pe, layer1)
                l1_back(BATCHES - 1, 1)

            def transpose_p(L, b, u, lag, ready):
                bb, uu = b + (u - lag) // UNITS, (u - lag) % UNITS
                if real(bb):
                    U = UNITS * bb + uu
                    pe.wait_ge(sem(ready), U + 1)
                    need(pe, sem(f"L{L}_pT"), U - 1)
                    transposes(bank[2 + uu % 2], P[uu % 4], HQ).then_inc(sem(f"L{L}_pT_mm"), 1)

            def p_times_v(L, b, s, u, lag):
                bb, uu = b + (u - lag) // UNITS, (u - lag) % UNITS
                ss = (s + (u - lag) // UNITS) % 2
                if real(bb):
                    g, hq = uu // 2, uu % 2
                    pe.wait_ge(sem(f"L{L}_pT"), UNITS * bb + uu + 1)
                    if hq == 0:
                        need(pe, sem(f"L{L}_oT"), G * bb + g)
                    if uu == 0:
                        pe.wait_ge(sem("L2_v" if L == 2 else "L3_wh"), bb + 1)
                    for j in range(HQ):
                        last = mm(bank[6][HP * j:HP * j + HP, cols(2 * (g % 2) + hq)],
                                  vx[ss][:, cols(HEADS * g + HQ * hq + j, HP)], pT[uu % 2][:, cols(j)],
                                  start=True, stop=True)
                    last.then_inc(sem(f"L{L}_pv_mm"), 1)

            def layer2(b, s, turn):
                for u in range(UNITS):
                    if real(b):
                        U = UNITS * b + u
                        g, hq = u // 2, u % 2
                        if u == 0:
                            pe.wait_ge(sem("L2_q"), b + 1)
                            pe.wait_ge(sem("L2_kexp"), b + 1)
                        need(pe, sem("L2_exp"), U - 1)
                        mm(bank[u % 2][:], identb[:], heads_of(mask2, b, g), start=True, stop=False)
                        kh = v3(kexp[:, cols(s, HEADS * W)], HEADS)[:, HQ * hq:HQ * hq + HQ, cols(g)]
                        mm(bank[u % 2][:], qT[s][:, cols(g)], kh, start=False, stop=True).then_inc(sem("L2_s_mm"), 1)
                    if real(b + 1):
                        if u == 1:
                            pe.wait_ge(sem(f"L2_staged{1 - s}"), 16 * (turn + 1 if s == 0 else turn + 2))
                            need(pe, sem("L2_q"), b + 1)
                            transposes(bank[4], xs[1 - s], G).then_inc(sem("L2_xT_mm"), 1)
                        if u == 3:
                            pe.wait_ge(sem("L2_xT"), b + 2)
                            need_or(pe, sem("L2_v"), b + 1, sem("L1_elu"), BATCHES)
                            mm(bank[5][:], kT_w[:], xT[1 - s][:], start=True, stop=True).then_inc(sem("L2_k_mm"), 1)
                        if u == 5:
                            mm(bank[4][:], qT_w[:], xT[1 - s][:], start=True, stop=True).then_inc(sem("L2_q_mm"), 1)
                        if u == 7:
                            pe.wait_ge(sem("L2_k"), b + 2)
                            for g in range(G):
                                last = mm(bank[5][:, cols(g)], xT[1 - s][:, cols(g)], vT_w[:], start=True, stop=True)
                            last.then_inc(sem("L2_v_mm"), 1)
                    if u % 2 == 0:
                        bb, g = b + (u - 6) // UNITS, (u - 6) % UNITS // 2
                        if real(bb):
                            pe.wait_ge(sem("L2_oT"), G * bb + g + 1)
                            if g == 0:
                                need(pe, sem("L2_out"), bb)
                            for hq in range(2):
                                last = mm(bank[7][:, cols(g)], oT[g % 2][:, cols(hq)], woT_pad[:, cols(hq)],
                                          start=hq == 0, stop=hq == 1)
                            last.then_inc(sem("L2_out_mm"), 1)
                    transpose_p(2, b, u, 2, "L2_p")
                    p_times_v(2, b, s, u, 3)
            if layers > 2:
                every_batch(pe, layer2, before=True, after=True)

            def layer3(b, s, turn):
                for u in range(UNITS):
                    if real(b):
                        U = UNITS * b + u
                        g, hq = u // 2, u % 2
                        if u == 0:
                            pe.wait_ge(sem("L3_e"), b + 1)
                        need(pe, sem("L3_leaky"), U - 1)
                        mm(bank[u % 2][:], identb[:], heads_of(mask2, b, g), start=True, stop=False)
                        mm(bank[u % 2][:], eT[s][:, cols(g)], sel1[:, cols(hq, HQ * 128)], start=False, stop=False)
                        for j in range(HQ):
                            last = mm(bank[u % 2][:, cols(j)], sel2[:, cols(HQ * hq + j)], eT[s][:, cols(g)],
                                      start=False, stop=j == HQ - 1)
                        last.then_inc(sem("L3_s_mm"), 1)
                    if real(b + 1):
                        if u == 1:
                            pe.wait_ge(sem(f"L3_staged{1 - s}"), 16 * (turn + 1 if s == 0 else turn + 2))
                            need(pe, sem("L3_wh"), b + 1)
                            transposes(bank[4], xs[1 - s], G).then_inc(sem("L3_xT_mm"), 1)
                        if u == 3:
                            pe.wait_ge(sem("L3_xT"), b + 2)
                            need(pe, sem("L3_e"), b + 1)
                            mm(bank[5][:], a3_w[:], xT[1 - s][:], start=True, stop=True).then_inc(sem("L3_e_mm"), 1)
                        if u == 5:
                            for g in range(G):
                                last = mm(bank[4][:, cols(g)], xT[1 - s][:, cols(g)], nat["L3_gnn_W"], start=True, stop=True)
                            last.then_inc(sem("L3_wh_mm"), 1)
                    if u % 2 == 1:
                        bb, g = b + (u - 7) // UNITS, (u - 7) % UNITS // 2
                        if real(bb):
                            pe.wait_ge(sem("L3_oT"), G * bb + g + 1)
                            need_or(pe, sem("L3_out"), G * bb + g, sem("L2_out"), BATCHES)
                            transposes(bank[7][:, cols(g % 2, 2 * N)], oT[g % 2], 2).then_inc(sem("L3_out_mm"), 1)
                    transpose_p(3, b, u, 3, "L3_exp")
                    p_times_v(3, b, s, u, 4)
            if layers > 3:
                every_batch(pe, layer3, before=True, after=True)



def kernel(**inputs):
    import numpy as np
    import concourse.bacc as bacc
    from concourse.bass_utils import run_bass_kernel_spmd

    nc = bacc.Bacc("TRN2", target_bir_lowering=False, num_devices=1)
    arrays, handles = {}, {}
    for name, value in inputs.items():
        a = np.ascontiguousarray(value)
        arrays[f"in_{name}"] = a
        handles[name] = nc.dram_tensor(f"in_{name}", a.shape, mybir.dt.from_np(a.dtype), kind="ExternalInput").ap()
    out = nc.dram_tensor("out", (GRAPHS, N, D), F32, kind="ExternalOutput").ap()
    build(nc, handles, out)
    result = run_bass_kernel_spmd(nc, [arrays], core_ids=[0])
    return result.results[0]["out"]
```

```python
from contextlib import ExitStack

import concourse.bass as bass
from concourse import mybir

F32 = mybir.dt.float32
BF16 = mybir.dt.bfloat16
I32 = mybir.dt.int32
ALU = mybir.AluOpType
ACT = mybir.ActivationFunctionType
AX = mybir.AxisListType

GRAPHS, N, D = 64, 128, 128
G = 4
BATCHES = GRAPHS // G
W = G * D
HEADS = 8
HD = D // HEADS
HP = 32
HQ = 4
UNITS = G * HEADS // HQ
ALPHA = 0.2
EPS = 1e-5
MASKED = -1e30
REL_LAST = 40
RELS = REL_LAST - 1


def need(eng, sem, value):
    if not isinstance(value, int) or value > 0:
        eng.wait_ge(sem, value)


def need_or(eng, sem, value, before, count):
    if isinstance(value, int) and value <= 0:
        eng.wait_ge(before, count)
    else:
        eng.wait_ge(sem, value)


def real(b):
    return not isinstance(b, int) or 0 <= b < BATCHES


def every_batch(eng, body, before=False, after=0):
    for b in range(-1 if before else 0, 4):
        body(b, b % 2, b // 2)
    with eng.Fori(2, BATCHES // 2 - 1) as turn:
        body(2 * turn, 0, turn)
        body(2 * turn + 1, 1, turn)
    for b in range(BATCHES - 2, BATCHES + after):
        body(b, b % 2, b // 2)


def build(nc, t, out, layers=4):
    ctx = ExitStack()
    with ctx:
        def sb(name, shape, dt=F32):
            return ctx.enter_context(nc.sbuf_tensor(name, shape, dt))

        sems = {}

        def sem(name):
            if name not in sems:
                sems[name] = ctx.enter_context(nc.semaphore(name))
            return sems[name]

        bank = [ctx.enter_context(nc.psum_tensor(f"bank{i}", [128, 512], F32)) for i in range(8)]

        def cols(i, n=D):
            return slice(i * n, i * n + n)

        identf = sb("identf", [128, 128])
        identb = sb("identb", [128, 128], BF16)
        headmask = sb("headmask", [128, HEADS])
        sel1 = sb("sel1", [128, HEADS * 128], BF16)
        sel2 = sb("sel2", [128, HEADS * 128], BF16)
        neghalf = sb("neghalf", [128, G])
        NAT = ["L0_gnn_W_loop", "L0_gnn_Wg_loop", "L1_gnn_W", "L1_gnn_a_12", "L2_gnn_Wq", "L2_gnn_Wk",
               "L2_gnn_Wv", "L2_gnn_Wo", "L3_gnn_W", "L0_gnn_W_fwd", "L0_gnn_Wg_fwd", "L0_gnn_W_bwd",
               "L0_gnn_Wg_bwd"]
        nat_all = sb("nat_all", [128, len(NAT) * 128])
        nat = {n: nat_all[:, cols(i)] for i, n in enumerate(NAT)}
        hg_w = {k: sb(f"hg_w_{k}", [128, 2 * D]) for k in ("loop", "fwd", "bwd")}
        hg_bias = sb("hg_bias", [128, 2 * D])
        bias_rest = sb("bias_rest", [128, 2 * D])
        bias_part = sb("bias_part", [128, 2 * D], BF16)
        bias3 = sb("bias3", [128, 4 * D], BF16)
        ones = sb("ones", [128, 128], BF16)
        minus_one = sb("minus_one", [128, 1])
        a_cols = sb("a_cols", [128, 2])
        qk_bias = sb("qk_bias", [128, 3])
        bv_row = sb("bv_row", [128, D])
        bo_row = sb("bo_row", [128, D])
        a3_row = sb("a3_row", [128, 2 * HD])
        w12 = sb("w12", [128, 2 * D])
        w1T = sb("w1T", [128, 128])
        a12T = sb("a12T", [128, 128])
        a12w = sb("a12w", [128, 128])
        bil = sb("bil", [128, 128])
        wa1 = sb("wa1", [128, 128])
        wa2 = sb("wa2", [128, 128])
        gT = {k: sb(f"gT_{k}", [128, 128]) for k in ("loop", "fwd", "bwd")}
        qT_w = sb("qT_w", [128, 128])
        kT_w = sb("kT_w", [128, 128])
        vT_w = sb("vT_w", [128, 128])
        wo_pad = sb("wo_pad", [128, HEADS * HP])
        woT_pad = sb("woT_pad", [128, 2 * D])
        a3_prod = sb("a3_prod", [128, 2 * D])
        a3_sum = sb("a3_sum", [128, 2 * HEADS])
        wh_w = sb("wh_w", [128, D + 2 * HEADS])

        X = sb("X", [128, GRAPHS * D])
        mask1 = sb("mask1", [128, GRAPHS * N], BF16)
        mask2 = sb("mask2", [128, GRAPHS * N], BF16)
        top = sb("top", [128, BATCHES])
        topmost = sb("topmost", [128, 1])
        toprow = sb("toprow", [1, 1])
        flag = sb("flag", [1, 1], I32)

        xs = [sb(f"xs{s}", [128, W]) for s in range(2)]
        xT = [sb(f"xT{s}", [128, W]) for s in range(2)]
        xn = [sb(f"xn{s}", [128, W]) for s in range(2)]
        yb = [sb(f"yb{s}", [128, W]) for s in range(2)]
        bn = [sb(f"bn{s}", [128, G * 6]) for s in range(2)]
        mv = [sb(f"mv{s}", [128, G * 2]) for s in range(2)]
        ln = [sb(f"ln{s}", [128, 3 * G]) for s in range(2)]
        loopm = [sb(f"loopm{s}", [128, W]) for s in range(2)]
        hg = [sb(f"hg{s}", [128, 2 * W]) for s in range(2)]
        vals = [sb(f"vals{s}", [128, W]) for s in range(2)]
        uT = [hg[s][:, 0:W] for s in range(2)]
        y2 = [hg[s][:, W:2 * W] for s in range(2)]
        lk = [sb(f"lk{s}", [128, W]) for s in range(2)]
        e1 = [loopm[s] for s in range(2)]
        small_t = [vals[s] for s in range(2)]
        pT1 = [sb(f"pT1{s}", [128, W]) for s in range(2)]
        elu = [sb(f"elu{s}", [128, W]) for s in range(2)]
        nm1 = [sb(f"nm1{s}", [128, G]) for s in range(2)]
        den1 = [sb(f"den1{s}", [128, G]) for s in range(2)]
        rd1 = [sb(f"rd1{s}", [128, G]) for s in range(2)]
        qT = [uT[s] for s in range(2)]
        kT = sb("kT", [128, W])
        kexp = sb("kexp", [128, 2 * HEADS * W])
        adj = kexp[:].bitcast(I32)
        vx = [sb(f"vx{s}", [128, G * HEADS * HP]) for s in range(2)]
        P = [sb(f"P{i}", [128, HQ * N]) for i in range(4)]
        pT = [sb(f"pT{i}", [128, HQ * N]) for i in range(2)]
        t3 = [sb(f"t3{i}", [128, HQ * N]) for i in range(2)]
        nmx = [sb(f"nmx{i}", [128, HQ]) for i in range(4)]
        den = [sb(f"den{i}", [128, HQ]) for i in range(4)]
        rd = [sb(f"rd{i}", [128, HQ]) for i in range(4)]
        rd3 = [sb(f"rd3{i}", [128, HEADS]) for i in range(2)]
        oT = [sb(f"oT{i}", [128, 2 * N]) for i in range(2)]
        eT = [sb(f"eT{s}", [128, W], BF16) for s in range(2)]
        er = sb("er", [128, G * 2 * HEADS])
        ep = sb("ep", [128, G * 128], BF16)

        block = ctx.enter_context(nc.Block())

        def v3(ap, a):
            return ap.rearrange("p (a c) -> p a c", a=a)

        def over(ap, shape):
            return ap.broadcast_to(shape)

        def x_of(b):
            return X[:, bass.ts(b, W)]

        def adj_of(b):
            return adj[:, bass.ts(b, W)]

        def heads_of(mask, b, g):
            return mask[:, bass.ts(G * b + g, N)].unsqueeze(1).broadcast_to([128, HQ, N])

        prep = []

        def add(dst, lhsT, rhs=None, after=-1):
            prep.append((dst, lhsT, rhs, after))
            return len(prep) - 1

        for k in ("loop", "fwd", "bwd"):
            add(hg_w[k][:, 0:D], nat[f"L0_gnn_W_{k}"])
            p = add(gT[k][:], nat[f"L0_gnn_Wg_{k}"])
            add(hg_w[k][:, D:2 * D], nat[f"L0_gnn_W_{k}"], gT[k][:], p)
            if k == "loop":
                first = len(prep)
        p = add(w1T[:], nat["L1_gnn_W"])
        add(wa1[:], w1T[:], a_cols[:, 0:1].broadcast_to([128, 128]), p)
        add(wa2[:], w1T[:], a_cols[:, 1:2].broadcast_to([128, 128]), p)
        p = add(a12T[:], nat["L1_gnn_a_12"])
        p = add(a12w[:], a12T[:], w1T[:], p)
        add(bil[:], w1T[:], a12w[:], p)
        add(qT_w[:], nat["L2_gnn_Wq"])
        add(kT_w[:], nat["L2_gnn_Wk"])
        add(vT_w[:], nat["L2_gnn_Wv"])
        add(woT_pad[:, 0:D], wo_pad[:, 0:D])
        add(woT_pad[:, D:2 * D], wo_pad[:, D:2 * D])

        def prep_dve(dve, steps):
            for i in steps:
                dst = prep[i][0]
                dve.wait_ge(sem("prep_mm"), i + 1)
                nc.vector.tensor_copy(dst, bank[4 + i % 4][:, 0:dst.shape[-1]]).then_inc(sem("prep"), 1)

        def prep_pe(pe, steps):
            for i in steps:
                dst, lhsT, rhs, after = prep[i]
                need(pe, sem("prep"), max(after + 1, i - 3))
                o = bank[4 + i % 4][:, 0:128]
                if rhs is None:
                    last = nc.tensor.transpose(o, lhsT, identf[:])
                else:
                    last = nc.tensor.matmul(o, lhsT, rhs, start=True, stop=True)
                last.then_inc(sem("prep_mm"), 1)
            pe.wait_ge(sem("prep"), steps[-1] + 1)

        gx, ga = xs[0][:, 0:D], sb("ga", [128, N], I32)[:]
        gaf, gxT = yb[0][:, 0:N], xT[0][:, 0:D]
        onehot = pT1[0][:, 0:2 * N]
        ghg, gvals = hg[0][:, 0:4 * D], vals[0][:, 0:2 * D]
        gbias = lk[0][:, 0:4 * D]
        gsum = kexp[:, 0:GRAPHS * D]
        rel = sb("rel", [128, 1])
        gmv, gbn, gln = mv[0][:, 0:2], bn[0][:, 0:6], ln[0][:, 0:3]
        STEPS = GRAPHS * (RELS + 1)

        def if_general(eng, body):
            eng.wait_ge(sem("flag_set"), 1)
            value = eng.value_load(flag[0:1, 0:1], min_val=0, max_val=1)
            with eng.If(value > 0):
                eng.wait_ge(sem("L0_norm_done"), BATCHES)
                body(eng)
                eng.wait_ge(sem("G_kept"), 16 * GRAPHS)

        def general_steps(eng, step, bias=None):
            step(0, 0, True, 0)
            with eng.Fori(1, GRAPHS) as g:
                step(g, g, True, 0)
            with eng.Fori(0, RELS) as r:
                if bias:
                    bias(r)
                with eng.Fori(0, GRAPHS) as g:
                    step(GRAPHS * (r + 1) + g, g, False, r)

        def general_sync(sp):
            def body(sp):
                def bias(r):
                    sp.wait_ge(sem("G_hg"), GRAPHS * (r + 1))
                    for i, n in enumerate(("b_fwd", "bg_fwd", "b_bwd", "bg_bwd")):
                        src = t[f"L0_gnn_{n}"][bass.ds(r, 1), :].rearrange("a d -> (a d)").partition_broadcast(128)
                        sp.dma_start(gbias[:, cols(i)], src).then_inc(sem("G_bias"), 16)

                def load(i, g, loop, r):
                    need(sp, sem("G_sum"), i)
                    sp.dma_start(gx, t["x"][bass.ds(g, 1)].rearrange("g n d -> (g n) d")).then_inc(sem("G_x"), 16)
                    sp.dma_start(ga, t["adj"][bass.ds(g, 1)].rearrange("g n d -> (g n) d")).then_inc(sem("G_adj"), 16)
                general_steps(sp, load, bias)

                def again(g):
                    sp.wait_ge(sem("G_sum"), STEPS)
                    need(sp, sem("G_y"), g)
                    sp.dma_start(gx, t["x"][bass.ds(g, 1)].rearrange("g n d -> (g n) d")).then_inc(sem("G_x"), 16)
                    sp.wait_ge(sem("G_norm"), g + 1)
                    sp.dma_start(X[:, bass.ts(g, D)], xn[0][:, 0:D]).then_inc(sem("G_kept"), 16)
                for s in range(2):
                    sp.wait_ge(sem(f"L0_kept{s}"), 16 * BATCHES // 2)
                again(0)
                with sp.Fori(1, GRAPHS) as g:
                    again(g)
            if_general(sp, body)

        def general_dve(dve):
            dve.wait_ge(sem("top_mm"), 1)
            nc.vector.tensor_reduce(toprow[:], bank[7][0:1, 0:128], AX.X, ALU.max).then_inc(sem("top_set"), 1)
            dve.wait_ge(sem("top_set"), 2)
            nc.vector.tensor_scalar(flag[:], toprow[:], 1.0, None, ALU.is_ge).then_inc(sem("flag_set"), 1)

            def body(dve):
                nc.vector.memset(rel[:], 1.0).then_inc(sem("G_rel"), 1)
                nc.vector.memset(gvals, 0.0).then_inc(sem("G_rel"), 1)
                dve.wait_ge(sem("G_rel"), 2)

                def bias(r):
                    dve.wait_ge(sem("G_onehot"), GRAPHS * (r + 1))
                    dve.wait_ge(sem("G_bias"), 64 * (r + 1))
                    nc.vector.tensor_scalar(rel[:], rel[:], 1.0, None, ALU.add).then_inc(sem("G_rel"), 1)

                def step(i, g, loop, r):
                    dve.wait_ge(sem("G_adj"), 16 * (i + 1))
                    nc.vector.tensor_copy(gaf, ga).then_inc(sem("G_adjf"), 1)
                    dve.wait_ge(sem("G_T_mm"), i + 1)
                    nc.vector.tensor_copy(gxT, bank[0][:, 0:128]).then_inc(sem("G_xT"), 1)
                    if not loop:
                        dve.wait_ge(sem("G_rel"), r + 3)
                        nc.vector.tensor_scalar(onehot[:, 0:N], bank[1][:, 0:N], rel[:], None, ALU.is_equal)
                    nc.vector.tensor_scalar(onehot[:, N:2 * N], gaf, rel[:], None, ALU.is_equal).then_inc(sem("G_onehot"), 1)
                    dve.wait_ge(sem("G_hg_mm"), i + 1)
                    if loop:
                        nc.vector.tensor_tensor(ghg[:, 0:2 * D], bank[2][:, 0:2 * D], hg_bias[:], ALU.add).then_inc(sem("G_hg"), 1)
                    else:
                        nc.vector.tensor_tensor(ghg, bank[2][:], gbias, ALU.add).then_inc(sem("G_hg"), 1)
                    dve.wait_ge(sem("G_gate"), i + 1)
                    n = 1 if loop else 2
                    h = v3(ghg, 4)
                    nc.vector.tensor_tensor(v3(gvals, 2)[:, 0:n, :], h[:, 0:2 * n:2, :], h[:, 1:2 * n:2, :], ALU.mult)\
                      .then_inc(sem("G_vals"), 1)
                    dve.wait_ge(sem("G_z_mm"), i + 1)
                    total = gsum[:, bass.ts(g, D)]
                    if loop:
                        nc.vector.tensor_copy(total, bank[3][:, 0:D]).then_inc(sem("G_sum"), 1)
                    else:
                        nc.vector.tensor_tensor(total, bank[3][:, 0:D], total, ALU.add).then_inc(sem("G_sum"), 1)
                general_steps(dve, step, bias)

                def norm(g):
                    dve.wait_ge(sem("G_sum"), STEPS)
                    dve.wait_ge(sem("G_x"), 16 * (STEPS + g + 1))
                    need(dve, sem("G_norm"), g)
                    nc.vector.scalar_tensor_tensor(yb[0][:, 0:D], gsum[:, bass.ts(g, D)], 0.0, gx, ALU.max, ALU.add)\
                      .then_inc(sem("G_y"), 1)
                    dve.wait_ge(sem("G_y"), g + 1)
                    nc.vector.bn_stats(gbn, yb[0][:, 0:D])
                    dve.drain()
                    nc.vector.bn_aggr(gmv, gbn)
                    dve.drain()
                    nc.vector.tensor_scalar(gln[:, 0:1], gmv[:, 0:1], -1.0, None, ALU.mult)
                    nc.vector.tensor_scalar(gln[:, 1:2], gmv[:, 1:2], EPS, None, ALU.add).then_inc(sem("G_stats"), 1)
                norm(0)
                with dve.Fori(1, GRAPHS) as g:
                    norm(g)
            if_general(dve, body)

        def general_act(act):
            def body(act):
                def step(i, g, loop, r):
                    act.wait_ge(sem("G_hg"), i + 1)
                    gate = v3(ghg, 4)[:, 1:(2 if loop else 4):2, :]
                    nc.scalar.activation(gate, gate, ACT.Sigmoid).then_inc(sem("G_gate"), 1)
                general_steps(act, step)
            if_general(act, body)

        def general_pe(pe):
            pe.wait_ge(sem("top_set"), 1)
            nc.tensor.transpose(bank[7][0:1, 0:128], topmost[:], identf[:]).then_inc(sem("top_mm"), 1)

            def body(pe):
                def step(i, g, loop, r):
                    mm = nc.tensor.matmul
                    pe.wait_ge(sem("G_x"), 16 * (i + 1))
                    pe.wait_ge(sem("G_adjf"), i + 1)
                    nc.tensor.transpose(bank[0][:, 0:128], gx, identf[:])
                    nc.tensor.transpose(bank[1][:, 0:128], gaf, identf[:]).then_inc(sem("G_T_mm"), 1)
                    pe.wait_ge(sem("G_onehot"), i + 1)
                    if loop:
                        mm(bank[2][:, 0:2 * D], gxT, hg_w["loop"][:], start=True, stop=True).then_inc(sem("G_hg_mm"), 1)
                    else:
                        mm(bank[2][:, 0:2 * D], gxT, hg_w["fwd"][:], start=True, stop=True)
                        mm(bank[2][:, 2 * D:4 * D], gxT, hg_w["bwd"][:], start=True, stop=True).then_inc(sem("G_hg_mm"), 1)
                    pe.wait_ge(sem("G_vals"), i + 1)
                    if loop:
                        mm(bank[3][:, 0:D], onehot[:, N:2 * N], gvals[:, 0:D], start=True, stop=True).then_inc(sem("G_z_mm"), 1)
                    else:
                        mm(bank[3][:, 0:D], onehot[:, 0:N], gvals[:, 0:D], start=True, stop=False)
                        mm(bank[3][:, 0:D], onehot[:, N:2 * N], gvals[:, D:2 * D], start=False, stop=True).then_inc(sem("G_z_mm"), 1)
                general_steps(pe, step)
            if_general(pe, body)

        def general_pool(pool):
            def body(pool):
                def norm(g):
                    need(pool, sem("G_kept"), 16 * g)
                    pool.wait_ge(sem("G_stats"), g + 1)
                    nc.gpsimd.tensor_tensor(gln[:, 2:3], gln[:, 1:2], neghalf[:, 0:1], ALU.pow)
                    pool.drain()
                    nc.gpsimd.tensor_scalar(xn[0][:, 0:D], yb[0][:, 0:D], gln[:, 0:1], gln[:, 2:3], ALU.add, ALU.mult)\
                      .then_inc(sem("G_norm"), 1)
                norm(0)
                with pool.Fori(1, GRAPHS) as g:
                    norm(g)
            if_general(pool, body)

        @block.sync
        def _(sp):
            def load(b, s, turn):
                need(sp, sem(f"adj_loaded{s}"), 16 * turn)
                need(sp, sem(f"x_loaded{s}"), 16 * turn)
                sp.dma_start(v3(x_of(b), G), t["x"][bass.ts(b, G)].rearrange("g n d -> n g d"))\
                  .then_inc(sem(f"x_loaded{s}"), 16)
                sp.dma_start(v3(adj_of(b), G), t["adj"][bass.ts(b, G)].rearrange("g n m -> n g m"))\
                  .then_inc(sem(f"adj_loaded{s}"), 16)

            def stage0(b, s, turn):
                sp.wait_ge(sem(f"x_loaded{s}"), 16 * (turn + 1))
                need(sp, sem("L0_xT_mm"), b - 1)
                sp.dma_start(xs[s][:], x_of(b)).then_inc(sem(f"L0_staged{s}"), 16)

            def layer0(b, s, turn):
                if real(b + 2):
                    load(b + 2, s, turn + 1)
                if real(b + 1):
                    stage0(b + 1, 1 - s, turn + s)
                if real(b - 4):
                    keep(0, b - 4, s, turn - 2)

            def keep(L, b, s, turn):
                sp.wait_ge(sem(f"L{L}_norm_done"), b + 1)
                if L < layers - 1:
                    sp.dma_start(x_of(b), xn[s][:]).then_inc(sem(f"L{L}_kept{s}"), 16)
                else:
                    sp.dma_start(out[bass.ts(b, G)].rearrange("g n d -> n g d"), v3(xn[s][:], G))\
                      .then_inc(sem(f"L{L}_kept{s}"), 16)

            def layer(L, load, lag):
                def both(b, s, turn):
                    if real(b):
                        load(b, s, turn)
                    if real(b - lag):
                        keep(L, b - lag, (s + lag) % 2, turn)
                every_batch(sp, both)
                for b in range(BATCHES, BATCHES + lag):
                    both(b, b % 2, b // 2)

            def stage(L):
                def load(b, s, turn):
                    if isinstance(b, int) and b < 2:
                        sp.wait_ge(sem(f"L{L - 1}_xT_mm"), BATCHES - 1 + b)
                        free = None
                    else:
                        free = sp.snap(b - 1)
                        sp.wait_ge(sem(f"L{L}_xT_mm"), free)
                    sp.wait_ge(sem(f"L{L - 1}_kept{s}"), 16 * (turn + 1))
                    sp.dma_start(xs[s][:], x_of(b)).then_inc(sem(f"L{L}_staged{s}"), 16)
                return load

            load(0, 0, 0)
            every_batch(sp, layer0, before=True, after=4)
            general_sync(sp)
            for L, lag in ((1, 4), (2, 4), (3, 4)):
                if L < layers:
                    layer(L, stage(L), lag)
            for s in range(2):
                sp.wait_ge(sem(f"L{layers - 1}_kept{s}"), 16 * BATCHES // 2)

        def norm_pow(pool, L, b, s, turn):
            if isinstance(b, int) and b < 2:
                if L > 0:
                    pool.wait_ge(sem(f"L{L - 1}_kept{s}"), 16 * BATCHES // 2)
            else:
                pool.wait_ge(sem(f"L{L}_kept{s}"), 16 * turn)
            pool.wait_ge(sem(f"L{L}_stats_done"), b + 1)
            nc.gpsimd.tensor_tensor(ln[s][:, 2 * G:3 * G], ln[s][:, G:2 * G], neghalf[:], ALU.pow)
            pool.drain()

        def norm_scale(L, s, graphs):
            for g in graphs:
                last = nc.gpsimd.tensor_scalar(xn[s][:, cols(g)], yb[s][:, cols(g)], ln[s][:, g:g + 1],
                                               ln[s][:, 2 * G + g:2 * G + g + 1], ALU.add, ALU.mult)
            if g == G - 1:
                last.then_inc(sem(f"L{L}_norm_done"), 1)

        def norm_pool(pool, L, b, s, turn):
            norm_pow(pool, L, b, s, turn)
            norm_scale(L, s, range(G))

        def y_slot_free(dve, L, b):
            if isinstance(b, int) and b < 2:
                if L > 0:
                    dve.wait_ge(sem(f"L{L - 1}_norm_done"), BATCHES - 1 + b)
            else:
                dve.wait_ge(sem(f"L{L}_norm_done"), b - 1)

        def stats_nodes(dve, L, b, s, graphs):
            dve.wait_ge(sem(f"L{L}_y_done"), b + 1)
            for g in graphs:
                nc.vector.bn_stats(bn[s][:, cols(g, 6)], yb[s][:, cols(g)])

        def stats_done(dve, L, s):
            dve.drain()
            for g in range(G):
                nc.vector.bn_aggr(mv[s][:, cols(g, 2)], bn[s][:, cols(g, 6)])
            dve.drain()
            m = v3(mv[s][:], G)
            nc.vector.tensor_scalar(ln[s][:, 0:G], m[:, :, 0], -1.0, None, ALU.mult)
            nc.vector.tensor_scalar(ln[s][:, G:2 * G], m[:, :, 1], EPS, None, ALU.add)\
              .then_inc(sem(f"L{L}_stats_done"), 1)

        def stats_dve(dve, L, b, s):
            stats_nodes(dve, L, b, s, range(G))
            stats_done(dve, L, s)

        @block.gpsimd
        def _(pool):
            nc.gpsimd.memset(identf[:], 0.0)
            nc.gpsimd.memset(ones[:], 1.0)
            nc.gpsimd.memset(minus_one[:], -1.0)
            nc.gpsimd.memset(sel1[:], 0.0)
            nc.gpsimd.memset(sel2[:], 0.0)
            nc.gpsimd.memset(headmask[:], 1.0)
            nc.gpsimd.memset(neghalf[:], -0.5).then_inc(sem("pool_set"), 1)
            steps = 1
            pool.wait_ge(sem("pool_set"), steps)

            def select(out_, pattern, base, op=ALU.not_equal, fill=1.0, step=1):
                nonlocal steps
                nc.gpsimd.affine_select(out=out_, in_=out_, compare_op=op, fill=fill, base=base,
                                        pattern=pattern, channel_multiplier=step).then_inc(sem("pool_set"), 1)
                steps += 1
                pool.wait_ge(sem("pool_set"), steps)

            select(identf[:], [[-1, 128]], 0)
            nc.gpsimd.tensor_copy(identb[:], identf[:]).then_inc(sem("ident"), 1)
            select(headmask[:], [[-HD, HEADS]], 0, ALU.is_ge, 0.0)
            select(headmask[:], [[HD, HEADS]], HD - 1, ALU.is_ge, 0.0, -1)
            for part in range(3):
                select(sel2[:].rearrange("p (h c) -> p h c", h=HEADS), [[-1, HEADS], [0, 128]], -32 * part)
                select(sel1[:].rearrange("p (h c) -> p h c", h=HEADS), [[-1, HEADS], [0, 128]], -32 * part - HEADS)
            nc.gpsimd.memset(ep[:], 0.0).then_inc(sem("pool_ready"), 1)

            every_batch(pool, lambda b, s, turn: norm_pool(pool, 0, b, s, turn))
            general_pool(pool)
            if layers > 1:
                every_batch(pool, lambda b, s, turn: norm_pool(pool, 1, b, s, turn))
            if layers > 2:
                def layer2(b, s, turn):
                    if real(b + 1):
                        pool.wait_ge(sem("L2_k"), b + 2)
                        need(pool, sem("L2_s_mm"), UNITS * b)
                        nc.gpsimd.tensor_tensor(kexp[:, cols((1 - s) * HEADS, W)], kT[:],
                                                headmask[:, 0:1].broadcast_to([128, W]), ALU.mult)
                        for h in range(1, HEADS):
                            last = nc.gpsimd.tensor_scalar(kexp[:, cols((1 - s) * HEADS + h, W)], kT[:],
                                                           headmask[:, h:h + 1], 1.0, ALU.mult, ALU.mult)
                        last.then_inc(sem("L2_kexp"), 1)
                    if real(b - 1):
                        norm_pool(pool, 2, b - 1, 1 - s, turn - 1 + s)
                every_batch(pool, layer2, before=True, after=1)
            if layers > 3:
                def layer3(b, s, turn):
                    for u in range(UNITS):
                        if real(b):
                            pool.wait_ge(sem("L3_max"), UNITS * b + u + 1)
                            nc.gpsimd.tensor_tensor(v3(P[u % 4][:], HQ), v3(P[u % 4][:], HQ),
                                                    nmx[u % 4][:].unsqueeze(2).broadcast_to([128, HQ, N]), ALU.add)\
                              .then_inc(sem("L3_less_max"), 1)
                        if real(b - 2):
                            if u == 5:
                                norm_pow(pool, 3, b - 2, s, turn - 1)
                            if u >= 6:
                                norm_scale(3, s, (2 * (u - 6), 2 * (u - 6) + 1))
                every_batch(pool, layer3, after=2)


        @block.scalar
        def _(act):
            def row(ap, n):
                return ap.rearrange("a n -> (a n)").partition_broadcast(128) if len(ap.shape) == 2 else ap.partition_broadcast(128)

            def col(ap):
                return ap.rearrange("n a -> n a") if len(ap.shape) == 2 else ap.unsqueeze(1)
            for dst, src in ((nat["L0_gnn_W_loop"], t["L0_gnn_W_loop"][:, :]), (nat["L0_gnn_Wg_loop"], t["L0_gnn_Wg_loop"][:, :]),
                             (hg_bias[:, 0:D], row(t["L0_gnn_b_loop"], D)), (hg_bias[:, D:2 * D], row(t["L0_gnn_bg_loop"], D))):
                act.dma_start(dst, src).then_inc(sem("L0_params"), 16)
            loads = [(nat[n], t[n][:, :]) for n in NAT[2:]]
            loads += [(a_cols[:, 0:1], col(t["L1_gnn_a_1"])), (a_cols[:, 1:2], col(t["L1_gnn_a_2"])),
                      (w12[:, 0:D], t["L1_gnn_W_1"][:, :]), (w12[:, D:2 * D], t["L1_gnn_W_2"][:, :]),
                      (qk_bias[:, 0:1], col(t["L2_gnn_bq"])), (qk_bias[:, 1:2], col(t["L2_gnn_bk"])),
                      (bv_row[:], row(t["L2_gnn_bv"], D)), (bo_row[:], row(t["L2_gnn_bo"], D)),
                      (a3_row[:], row(t["L3_gnn_a"], 2 * HD))]
            sems["n_params"] = 16 * len(loads)
            act.wait_ge(sem("pool_set"), 1)

            def layer0(b, s, turn):
                if real(b + 1):
                    act.wait_ge(sem("L0_xT_mm"), b + 2)
                    need(act, sem("L0_hg_mm"), b)
                    nc.scalar.copy(xT[1 - s][:], bank[0][:]).then_inc(sem("L0_xT"), 1)
                if real(b):
                    act.wait_ge(sem(f"adj_loaded{s}"), 16 * (turn + 1))
                    need(act, sem("L0_top"), b - 1)
                    nc.scalar.activation(elu[s][:], adj_of(b), ACT.Relu, bias=minus_one[:],
                                         accum_out=top[:, bass.ds(b, 1)]).then_inc(sem("L0_top"), 1)
                    act.wait_ge(sem("L0_hg_mm"), b + 1)
                    need(act, sem("L0_vals"), b - 1)
                    for i in range(2):
                        last = nc.scalar.activation(v3(hg[s][:, cols(i, 2 * D)], 2),
                                                    v3(bank[1 + 3 * s + i][:], 4)[:, 1:4:2, :], ACT.Sigmoid)
                    last.then_inc(sem("L0_gate"), 1)
                    if isinstance(b, int) and b < 4:
                        share = -(-len(loads) // 4)
                        for dst, src in loads[b * share:(b + 1) * share]:
                            act.dma_start(dst, src).then_inc(sem("params"), 16)
            every_batch(act, layer0, before=True)
            act.wait_ge(sem("params"), 16 * len(loads))
            nc.scalar.mul(qk_bias[:, 2:3], qk_bias[:, 0:1], HD ** -0.5).then_inc(sem("bq_scaled"), 1)
            general_act(act)

            def layer1(b, s, turn):
                if real(b - 1):
                    act.wait_ge(sem("L1_max"), b)
                    need(act, sem("L1_pT_mm"), b - 2)
                    for g in range(G):
                        last = nc.scalar.activation(e1[1 - s][:, cols(g)], lk[1 - s][:, cols(g)], ACT.Exp,
                                                    bias=nm1[1 - s][:, g:g + 1], accum_out=den1[1 - s][:, g:g + 1])
                    last.then_inc(sem("L1_exp"), 1)
                if real(b - 2):
                    act.wait_ge(sem("L1_z_mm"), b - 1)
                    need(act, sem("L1_y_done"), b - 3)
                    nc.scalar.activation(elu[s][:], bank[5][:], ACT.Relu, scale=-1.0).then_inc(sem("L1_neg"), 1)
                    act.wait_ge(sem("L1_neg"), b - 1)
                    nc.scalar.activation(elu[s][:], elu[s][:], ACT.Exp, scale=-1.0).then_inc(sem("L1_elu_exp"), 1)
                if real(b):
                    act.wait_ge(sem("L1_u_mm"), b + 1)
                    nc.scalar.activation(uT[s], bank[1][:], ACT.Identity, bias=wa1[:, 0:1]).then_inc(sem("L1_uT"), 1)
                    act.wait_ge(sem("L1_y2_mm"), b + 1)
                    nc.scalar.copy(y2[s], bank[3][:]).then_inc(sem("L1_y2"), 1)
                if real(b - 1):
                    act.wait_ge(sem("L1_pT_mm"), b)
                    need(act, sem("L1_z_mm"), b - 2)
                    nc.scalar.copy(pT1[1 - s][:], bank[4][:]).then_inc(sem("L1_pT"), 1)
                if real(b):
                    act.wait_ge(sem("L1_logits_mm"), b + 1)
                    need(act, sem("L1_leaky"), b - 1)
                    nc.scalar.mul(small_t[s][:], bank[2][:], ALPHA).then_inc(sem("L1_scaled"), 1)
            if layers > 1:
                every_batch(act, layer1, after=2)

            def copy_pT(L, b, u, lag):
                bb, uu = b + (u - lag) // UNITS, (u - lag) % UNITS
                if real(bb):
                    act.wait_ge(sem(f"L{L}_pT_mm"), UNITS * bb + uu + 1)
                    need(act, sem(f"L{L}_pv_mm"), UNITS * bb + uu - 1)
                    nc.scalar.copy(pT[uu % 2][:], bank[2 + uu % 2][:]).then_inc(sem(f"L{L}_pT"), 1)

            def copy_oT(L, b, u, lag):
                if (u - lag) % 2 == 0:
                    bb, g = b + (u - lag) // UNITS, (u - lag) % UNITS // 2
                    if real(bb):
                        act.wait_ge(sem(f"L{L}_pv_mm"), UNITS * bb + 2 * g + 2)
                        need(act, sem(f"L{L}_out_mm"), G * bb + g - 1)
                        nc.scalar.copy(oT[g % 2][:], bank[6][:, cols(g % 2, 2 * N)]).then_inc(sem(f"L{L}_oT"), 1)

            def layer2(b, s, turn):
                for u in range(UNITS):
                    if u == 6 and real(b + 1):
                        act.wait_ge(sem("L2_q_mm"), b + 2)
                        need(act, sem("L2_s_mm"), UNITS * b)
                        nc.scalar.activation(qT[1 - s], bank[4][:], ACT.Identity, bias=qk_bias[:, 2:3],
                                             scale=HD ** -0.5).then_inc(sem("L2_q"), 1)
                    copy_oT(2, b, u, 5)
                    if real(b):
                        U = UNITS * b + u
                        act.wait_ge(sem("L2_max"), U + 1)
                        need(act, sem("L2_pT_mm"), U - 3)
                        for j in range(HQ):
                            last = nc.scalar.activation(P[u % 4][:, cols(j)], bank[u % 2][:, cols(j)], ACT.Exp,
                                                        bias=nmx[u % 4][:, j:j + 1], accum_out=den[u % 4][:, j:j + 1])
                        last.then_inc(sem("L2_exp"), 1)
                    copy_pT(2, b, u, 2)
            if layers > 2:
                every_batch(act, layer2, before=True, after=1)

            def layer3(b, s, turn):
                for u in range(UNITS):
                    copy_oT(3, b, u, 6)
                    if real(b):
                        U = UNITS * b + u
                        act.wait_ge(sem("L3_s_mm"), U + 1)
                        need(act, sem("L3_leaky"), U - 1)
                        nc.scalar.mul(t3[u % 2][:], bank[u % 2][:], ALPHA).then_inc(sem("L3_scaled"), 1)
                    bb, uu = b + (u - 2) // UNITS, (u - 2) % UNITS
                    if real(bb):
                        act.wait_ge(sem("L3_less_max"), UNITS * bb + uu + 1)
                        nc.scalar.activation(P[uu % 4][:], P[uu % 4][:], ACT.Exp).then_inc(sem("L3_exp"), 1)
                    copy_pT(3, b, u, 3)
                    if real(b + 1):
                        if u == 1:
                            act.wait_ge(sem("L3_xT_mm"), b + 2)
                            need(act, sem("L3_wh_mm"), b + 1)
                            nc.scalar.copy(xT[1 - s][:], bank[4][:]).then_inc(sem("L3_xT"), 1)
                        if u == 5:
                            act.wait_ge(sem("L3_split"), 6 * (b + 1) + 1)
                            need(act, sem("L3_pv_mm"), UNITS * b)
                            for i in range(2):
                                last = nc.scalar.copy(
                                    vx[1 - s][:, cols(i, 2 * HEADS * HP)].rearrange("p (g h c) -> p g h c", g=2, h=HEADS)[:, :, :, 0:HD],
                                    v3(bank[4 + i][:], 2)[:, :, 0:D].rearrange("p g (h c) -> p g h c", h=HEADS))
                            last.then_inc(sem("L3_wh"), 1)
                        if u == 7:
                            act.wait_ge(sem("L3_eT_mm"), b + 2)
                            need(act, sem("L3_s_mm"), UNITS * b)
                            nc.scalar.copy(eT[1 - s][:], bank[5][:].bitcast(BF16)[:, 0:W]).then_inc(sem("L3_eT"), 1)
            if layers > 3:
                every_batch(act, layer3, before=True, after=1)


        @block.vector
        def _(dve):
            nc.vector.memset(bias3[:], 0.0)
            for s in range(2):
                nc.vector.memset(vx[s][:], 0.0)
            nc.vector.memset(wo_pad[:], 0.0).then_inc(sem("dve_set"), 1)
            dve.wait_ge(sem("dve_set"), 1)
            for s in range(2):
                nc.vector.memset(vx[s][:].rearrange("p (a c) -> p a c", c=HP)[:, :, HD:HD + 1], 1.0)
            prep_dve(dve, range(first))
            dve.wait_ge(sem("L0_params"), 64)
            rest = hg_bias
            for part in range(3):
                row = slice(32 * part, 32 * part + 1)
                nc.vector.tensor_copy(bias_part[:], rest[:]).then_inc(sem("bias_split"), 1)
                dve.wait_ge(sem("bias_split"), 2 * part + 1)
                for i in range(2):
                    nc.vector.tensor_copy(bias3[row, cols(i, 2 * D)], bias_part[row, :])
                nc.vector.tensor_tensor(bias_rest[:], rest[:], bias_part[:], ALU.subtract).then_inc(sem("bias_split"), 1)
                dve.wait_ge(sem("bias_split"), 2 * part + 2)
                rest = bias_rest

            def layer0(b, s, turn):
                if real(b):
                    dve.wait_ge(sem(f"adj_loaded{s}"), 16 * (turn + 1))
                    need(dve, sem("L0_z_mm"), b - 1)
                    nc.vector.tensor_scalar(loopm[s][:], adj_of(b), 1.0, None, ALU.is_equal)
                    nc.vector.tensor_scalar(mask1[:, bass.ts(b, W)], adj_of(b), 0.0, MASKED, ALU.is_le, ALU.mult)
                    nc.vector.tensor_scalar(mask2[:, bass.ts(b, W)], adj_of(b), 0.0, MASKED, ALU.is_equal, ALU.mult)
                    dve.wait_ge(sem("L0_gate"), b + 1)
                    for i in range(2):
                        last = nc.vector.tensor_tensor(v3(vals[s][:, cols(i, 2 * D)], 2), v3(bank[1 + 3 * s + i][:], 4)[:, 0:4:2, :],
                                                       v3(hg[s][:, cols(i, 2 * D)], 2), ALU.mult)
                    last.then_inc(sem("L0_vals"), 1)
                if real(b - 1):
                    dve.wait_ge(sem("L0_z_mm"), b)
                    y_slot_free(dve, 0, b - 1)
                    nc.vector.scalar_tensor_tensor(yb[1 - s][:], bank[3][:], 0.0, x_of(b - 1), ALU.max, ALU.add)\
                      .then_inc(sem("L0_y_done"), 1)
                    stats_dve(dve, 0, b - 1, 1 - s)
            every_batch(dve, layer0, after=1)
            dve.wait_ge(sem("L0_top"), BATCHES)
            nc.vector.tensor_reduce(topmost[:], top[:], AX.X, ALU.max).then_inc(sem("top_set"), 1)

            dve.wait_ge(sem("params"), sems["n_params"])
            nc.vector.tensor_copy(v3(wo_pad[:], HEADS)[:, :, 0:HD], v3(nat["L2_gnn_Wo"], HEADS))\
              .then_inc(sem("wo_padded"), 1)
            for half in range(2):
                nc.vector.tensor_tensor(v3(a3_prod[:, cols(half)], HEADS), v3(nat["L3_gnn_W"], HEADS),
                                        a3_row[:, cols(half, HD)].unsqueeze(1).broadcast_to([128, HEADS, HD]), ALU.mult)\
                  .then_inc(sem("dve_set"), 1)
            nc.vector.tensor_copy(wh_w[:, 0:D], nat["L3_gnn_W"])
            dve.wait_ge(sem("dve_set"), 3)
            nc.vector.tensor_reduce(a3_sum[:], v3(a3_prod[:], 2 * HEADS), AX.X, ALU.add).then_inc(sem("dve_set"), 1)
            dve.wait_ge(sem("dve_set"), 4)
            nc.vector.tensor_copy(wh_w[:, D:D + HEADS], a3_sum[:, HEADS:2 * HEADS])
            nc.vector.tensor_copy(wh_w[:, D + HEADS:], a3_sum[:, 0:HEADS])
            prep_dve(dve, range(first, len(prep)))
            general_dve(dve)

            def layer1(b, s, turn):
                if real(b):
                    dve.wait_ge(sem("L1_xT_mm"), b + 1)
                    need(dve, sem("L1_z_mm"), b - 1)
                    nc.vector.tensor_copy(xT[s][:], bank[0][:]).then_inc(sem("L1_xT"), 1)
                if real(b - 1):
                    dve.wait_ge(sem("L1_exp"), b)
                    nc.vector.reciprocal(rd1[1 - s][:], den1[1 - s][:]).then_inc(sem("L1_rden"), 1)
                    dve.wait_ge(sem("L1_rden"), b)
                    nc.vector.tensor_tensor(v3(e1[1 - s][:], G), v3(e1[1 - s][:], G),
                                            rd1[1 - s][:].unsqueeze(2).broadcast_to([128, G, N]),
                                            ALU.mult).then_inc(sem("L1_p"), 1)
                if real(b - 2):
                    dve.wait_ge(sem("L1_elu_exp"), b - 1)
                    nc.vector.scalar_tensor_tensor(elu[s][:], bank[5][:], 0.0, elu[s][:], ALU.max, ALU.add)\
                      .then_inc(sem("L1_elu"), 1)
                    y_slot_free(dve, 1, b - 2)
                    dve.wait_ge(sem("L1_elu"), b - 1)
                    nc.vector.scalar_tensor_tensor(yb[s][:], elu[s][:], -1.0, x_of(b - 2), ALU.add, ALU.add)\
                      .then_inc(sem("L1_y_done"), 1)
                    stats_dve(dve, 1, b - 2, s)
                if real(b):
                    dve.wait_ge(sem("L1_scaled"), b + 1)
                    need(dve, sem("L1_exp"), b - 1)
                    nc.vector.tensor_tensor(lk[s][:], bank[2][:], small_t[s][:], ALU.max).then_inc(sem("L1_leaky"), 1)
                    dve.wait_ge(sem("L1_leaky"), b + 1)
                    nc.vector.tensor_reduce(nm1[s][:], v3(lk[s][:], G), AX.X, ALU.max, negate=True).then_inc(sem("L1_max"), 1)
            if layers > 1:
                every_batch(dve, layer1, after=2)

            def layer2(b, s, turn):
                for u in range(UNITS):
                    if real(b):
                        U = UNITS * b + u
                        dve.wait_ge(sem("L2_s_mm"), U + 1)
                        need(dve, sem("L2_exp"), U - 3)
                        nc.vector.tensor_reduce(nmx[u % 4][:], v3(bank[u % 2][:], HQ), AX.X, ALU.max, negate=True)\
                          .then_inc(sem("L2_max"), 1)
                    if u == 2 and real(b + 1):
                        dve.wait_ge(sem("L2_xT_mm"), b + 2)
                        need(dve, sem("L2_v_mm"), b)
                        nc.vector.tensor_copy(xT[1 - s][:], bank[4][:]).then_inc(sem("L2_xT"), 1)
                    if u == 4 and real(b + 1):
                        dve.wait_ge(sem("L2_k_mm"), b + 2)
                        need(dve, sem("L2_kexp"), b + 1)
                        nc.vector.tensor_scalar(kT[:], bank[5][:], qk_bias[:, 1:2], None, ALU.add).then_inc(sem("L2_k"), 1)
                    if u == 0 and real(b):
                        dve.wait_ge(sem("L2_v_mm"), b + 1)
                        need(dve, sem("L2_pv_mm"), UNITS * (b - 1))
                        nc.vector.tensor_tensor(
                            vx[s][:].rearrange("p (g h c) -> p g h c", g=G, h=HEADS)[:, :, :, 0:HD],
                            bank[5][:].rearrange("p (g h c) -> p g h c", g=G, h=HEADS),
                            bv_row[:].rearrange("p (h c) -> p h c", h=HEADS).unsqueeze(1).broadcast_to([128, G, HEADS, HD]),
                            ALU.add).then_inc(sem("L2_v"), 1)
                    bb, uu = b + (u - 1) // UNITS, (u - 1) % UNITS
                    if real(bb):
                        U = UNITS * bb + uu
                        dve.wait_ge(sem("L2_exp"), U + 1)
                        nc.vector.reciprocal(rd[uu % 4][:], den[uu % 4][:]).then_inc(sem("L2_rden"), 1)
                        dve.wait_ge(sem("L2_rden"), U + 1)
                        nc.vector.tensor_tensor(v3(P[uu % 4][:], HQ), v3(P[uu % 4][:], HQ),
                                                rd[uu % 4][:].unsqueeze(2).broadcast_to([128, HQ, N]), ALU.mult)\
                          .then_inc(sem("L2_p"), 1)
                    if u == 5 and real(b - 1):
                        dve.wait_ge(sem("L2_out_mm"), G * b)
                        y_slot_free(dve, 2, b - 1)
                        nc.vector.tensor_tensor(v3(yb[1 - s][:], G), v3(bank[7][:], G),
                                                bo_row[:].unsqueeze(1).broadcast_to([128, G, D]), ALU.add)\
                          .then_inc(sem("L2_out"), 1)
                        dve.wait_ge(sem("L2_out"), b)
                        nc.vector.tensor_tensor(yb[1 - s][:], yb[1 - s][:], x_of(b - 1), ALU.add)\
                          .then_inc(sem("L2_y_done"), 1)
                    if u == 6 and real(b - 1):
                        stats_dve(dve, 2, b - 1, 1 - s)
            if layers > 2:
                every_batch(dve, layer2, before=True, after=1)

            def split_e(dve, b, n):
                def part(k):
                    return v3(ep[:], G)[:, :, 32 * k:32 * k + 2 * HEADS]
                rest = v3(er[:], G)
                if n == 0:
                    dve.wait_ge(sem("L3_wh_mm"), b + 1)
                    for i in range(2):
                        last = nc.vector.tensor_copy(rest[:, 2 * i:2 * i + 2, :], v3(bank[4 + i][:], 2)[:, :, D:D + 2 * HEADS])
                else:
                    dve.wait_ge(sem("L3_split"), 6 * b + n)
                    if n == 1:
                        need(dve, sem("L3_eT_mm"), b)
                    if n % 2 == 1:
                        last = nc.vector.tensor_copy(part(n // 2), rest)
                    else:
                        last = nc.vector.tensor_tensor(rest, rest, part(n // 2 - 1), ALU.subtract)
                last.then_inc(sem("L3_split"), 1)

            def layer3(b, s, turn):
                for u in range(UNITS):
                    if real(b):
                        U = UNITS * b + u
                        dve.wait_ge(sem("L3_scaled"), U + 1)
                        need(dve, sem("L3_pT_mm"), U - 3)
                        nc.vector.tensor_tensor(P[u % 4][:], bank[u % 2][:], t3[u % 2][:], ALU.max)\
                          .then_inc(sem("L3_leaky"), 1)
                    if u in (3, 4, 5) and real(b + 1):
                        split_e(dve, b + 1, 2 * u - 5)
                    if real(b):
                        dve.wait_ge(sem("L3_leaky"), U + 1)
                        need(dve, sem("L3_less_max"), U - 3)
                        nc.vector.tensor_reduce(nmx[u % 4][:], v3(P[u % 4][:], HQ), AX.X, ALU.max, negate=True)\
                          .then_inc(sem("L3_max"), 1)
                    if u in (2, 3, 4) and real(b + 1):
                        split_e(dve, b + 1, 2 * u - 4)
                    if u % 2 == 0:
                        bb, g = b + (u - 8) // UNITS, u // 2
                        if real(bb):
                            o = bank[7][:, cols(g % 2, 2 * N)].rearrange("p (h c) -> p h c", h=HEADS)
                            dve.wait_ge(sem("L3_out_mm"), G * bb + g + 1)
                            if g == 0:
                                y_slot_free(dve, 3, bb)
                            nc.vector.reciprocal(rd3[g % 2][:], o[:, :, HD]).then_inc(sem("L3_rden"), 1)
                            dve.wait_ge(sem("L3_rden"), G * bb + g + 1)
                            nc.vector.tensor_tensor(v3(yb[1 - s][:, cols(g)], HEADS), o[:, :, 0:HD],
                                                    rd3[g % 2][:].unsqueeze(2).broadcast_to([128, HEADS, HD]), ALU.mult)\
                              .then_inc(sem("L3_out"), 1)
                    if u == 7 and real(b - 1):
                        dve.wait_ge(sem("L3_out"), G * b)
                        nc.vector.tensor_tensor(yb[1 - s][:], yb[1 - s][:], x_of(b - 1), ALU.add)\
                          .then_inc(sem("L3_y_done"), 1)
                    if real(b - 2):
                        if u == 1:
                            stats_nodes(dve, 3, b - 2, s, (0, 1))
                        if u == 3:
                            stats_nodes(dve, 3, b - 2, s, (2, 3))
                        if u == 5:
                            stats_done(dve, 3, s)
            if layers > 3:
                every_batch(dve, layer3, before=True, after=2)


        @block.tensor
        def _(pe):
            mm = nc.tensor.matmul
            pe.wait_ge(sem("ident"), 1)
            pe.wait_ge(sem("L0_params"), 64)
            prep_pe(pe, range(first))

            def transposes(dst, src, n):
                for i in range(n):
                    last = nc.tensor.transpose(dst[:, cols(i)], src[:, cols(i)], identf[:])
                return last

            def layer0(b, s, turn):
                if real(b):
                    pe.wait_ge(sem("L0_xT"), b + 1)
                    need(pe, sem("L0_vals"), b - 1)
                    if isinstance(b, int) and b == 0:
                        pe.wait_ge(sem("bias_split"), 6)
                    for i in range(2):
                        mm(bank[1 + 3 * s + i][:], ones[:], bias3[:], start=True, stop=False)
                        for g in range(2):
                            last = mm(bank[1 + 3 * s + i][:, cols(g, 2 * D)], xT[s][:, cols(2 * i + g)], hg_w["loop"][:],
                                      start=False, stop=g == 1)
                    last.then_inc(sem("L0_hg_mm"), 1)
                if real(b + 1):
                    pe.wait_ge(sem(f"L0_staged{1 - s}"), 16 * (turn + 1 if s == 0 else turn + 2))
                    need(pe, sem("L0_xT"), b + 1)
                    transposes(bank[0], xs[1 - s], G).then_inc(sem("L0_xT_mm"), 1)
                if real(b - 1):
                    pe.wait_ge(sem("L0_vals"), b)
                    need(pe, sem("L0_y_done"), b - 1)
                    for g in range(G):
                        last = mm(bank[3][:, cols(g)], loopm[1 - s][:, cols(g)], vals[1 - s][:, cols(g)], start=True, stop=True)
                    last.then_inc(sem("L0_z_mm"), 1)
            every_batch(pe, layer0, before=True, after=1)
            pe.wait_ge(sem("params"), sems["n_params"])
            pe.wait_ge(sem("wo_padded"), 1)
            prep_pe(pe, range(first, len(prep)))
            pe.wait_ge(sem("pool_ready"), 1)
            general_pe(pe)

            def layer1(b, s, turn):
                if real(b - 2):
                    pe.wait_ge(sem("L1_pT"), b - 1)
                    need(pe, sem("L1_elu"), b - 2)
                    for g in range(G):
                        mm(bank[5][:, cols(g)], xT[s][:, cols(g)], w12[:, 0:D], start=True, stop=False)
                        last = mm(bank[5][:, cols(g)], pT1[s][:, cols(g)], y2[s][:, cols(g)], start=False, stop=True)
                    last.then_inc(sem("L1_z_mm"), 1)
                if real(b):
                    pe.wait_ge(sem(f"L1_staged{s}"), 16 * (turn + 1))
                    need(pe, sem("L1_xT"), b)
                    transposes(bank[0], xs[s], G).then_inc(sem("L1_xT_mm"), 1)
                    pe.wait_ge(sem("L1_xT"), b + 1)
                    need(pe, sem("L1_uT"), b)
                    mm(bank[1][:], bil[:], xT[s][:], start=True, stop=True).then_inc(sem("L1_u_mm"), 1)
                    need_or(pe, sem("L1_y2"), b, sem("L0_y_done"), BATCHES)
                    for g in range(G):
                        last = mm(bank[3][:, cols(g)], xT[s][:, cols(g)], w12[:, D:2 * D], start=True, stop=True)
                    last.then_inc(sem("L1_y2_mm"), 1)
                if real(b - 1):
                    pe.wait_ge(sem("L1_p"), b)
                    need(pe, sem("L1_pT"), b - 1)
                    transposes(bank[4], e1[1 - s], G).then_inc(sem("L1_pT_mm"), 1)
                if real(b):
                    need(pe, sem("L1_leaky"), b)
                    mm(bank[2][:], identb[:], mask1[:, bass.ts(b, W)], start=True, stop=False)
                    for g in range(G):
                        mm(bank[2][:, cols(g)], xT[s][:, cols(g)], wa2[:], start=False, stop=False)
                    pe.wait_ge(sem("L1_uT"), b + 1)
                    for g in range(G):
                        last = mm(bank[2][:, cols(g)], uT[s][:, cols(g)], xT[s][:, cols(g)], start=False, stop=g == G - 1)
                    last.then_inc(sem("L1_logits_mm"), 1)
            if layers > 1:
                every_batch(pe, layer1, after=2)

            def transpose_p(L, b, u, lag, ready):
                bb, uu = b + (u - lag) // UNITS, (u - lag) % UNITS
                if real(bb):
                    U = UNITS * bb + uu
                    pe.wait_ge(sem(ready), U + 1)
                    need(pe, sem(f"L{L}_pT"), U - 1)
                    transposes(bank[2 + uu % 2], P[uu % 4], HQ).then_inc(sem(f"L{L}_pT_mm"), 1)

            def p_times_v(L, b, s, u, lag):
                bb, uu = b + (u - lag) // UNITS, (u - lag) % UNITS
                ss = (s + (u - lag) // UNITS) % 2
                if real(bb):
                    g, hq = uu // 2, uu % 2
                    pe.wait_ge(sem(f"L{L}_pT"), UNITS * bb + uu + 1)
                    if hq == 0:
                        need(pe, sem(f"L{L}_oT"), G * bb + g)
                    if uu == 0:
                        pe.wait_ge(sem("L2_v" if L == 2 else "L3_wh"), bb + 1)
                    for j in range(HQ):
                        last = mm(bank[6][HP * j:HP * j + HP, cols(2 * (g % 2) + hq)],
                                  vx[ss][:, cols(HEADS * g + HQ * hq + j, HP)], pT[uu % 2][:, cols(j)],
                                  start=True, stop=True)
                    last.then_inc(sem(f"L{L}_pv_mm"), 1)

            def layer2(b, s, turn):
                for u in range(UNITS):
                    if real(b):
                        U = UNITS * b + u
                        g, hq = u // 2, u % 2
                        if u == 0:
                            pe.wait_ge(sem("L2_q"), b + 1)
                            pe.wait_ge(sem("L2_kexp"), b + 1)
                        need(pe, sem("L2_exp"), U - 1)
                        mm(bank[u % 2][:], identb[:], heads_of(mask2, b, g), start=True, stop=False)
                        kh = v3(kexp[:, cols(s, HEADS * W)], HEADS)[:, HQ * hq:HQ * hq + HQ, cols(g)]
                        mm(bank[u % 2][:], qT[s][:, cols(g)], kh, start=False, stop=True).then_inc(sem("L2_s_mm"), 1)
                    if real(b + 1):
                        if u == 1:
                            pe.wait_ge(sem(f"L2_staged{1 - s}"), 16 * (turn + 1 if s == 0 else turn + 2))
                            need(pe, sem("L2_q"), b + 1)
                            transposes(bank[4], xs[1 - s], G).then_inc(sem("L2_xT_mm"), 1)
                        if u == 3:
                            pe.wait_ge(sem("L2_xT"), b + 2)
                            need_or(pe, sem("L2_v"), b + 1, sem("L1_elu"), BATCHES)
                            mm(bank[5][:], kT_w[:], xT[1 - s][:], start=True, stop=True).then_inc(sem("L2_k_mm"), 1)
                        if u == 5:
                            mm(bank[4][:], qT_w[:], xT[1 - s][:], start=True, stop=True).then_inc(sem("L2_q_mm"), 1)
                        if u == 7:
                            pe.wait_ge(sem("L2_k"), b + 2)
                            for g in range(G):
                                last = mm(bank[5][:, cols(g)], xT[1 - s][:, cols(g)], vT_w[:], start=True, stop=True)
                            last.then_inc(sem("L2_v_mm"), 1)
                    if u % 2 == 0:
                        bb, g = b + (u - 6) // UNITS, (u - 6) % UNITS // 2
                        if real(bb):
                            pe.wait_ge(sem("L2_oT"), G * bb + g + 1)
                            if g == 0:
                                need(pe, sem("L2_out"), bb)
                            for hq in range(2):
                                last = mm(bank[7][:, cols(g)], oT[g % 2][:, cols(hq)], woT_pad[:, cols(hq)],
                                          start=hq == 0, stop=hq == 1)
                            last.then_inc(sem("L2_out_mm"), 1)
                    transpose_p(2, b, u, 2, "L2_p")
                    p_times_v(2, b, s, u, 3)
            if layers > 2:
                every_batch(pe, layer2, before=True, after=1)

            def layer3(b, s, turn):
                for u in range(UNITS):
                    if real(b):
                        U = UNITS * b + u
                        g, hq = u // 2, u % 2
                        if u == 0:
                            pe.wait_ge(sem("L3_eT"), b + 1)
                        need(pe, sem("L3_leaky"), U - 1)
                        mm(bank[u % 2][:], identb[:], heads_of(mask2, b, g), start=True, stop=False)
                        mm(bank[u % 2][:], eT[s][:, cols(g)], sel1[:, cols(hq, HQ * 128)], start=False, stop=False)
                        for j in range(HQ):
                            last = mm(bank[u % 2][:, cols(j)], sel2[:, cols(HQ * hq + j)], eT[s][:, cols(g)],
                                      start=False, stop=j == HQ - 1)
                        last.then_inc(sem("L3_s_mm"), 1)
                    transpose_p(3, b, u, 3, "L3_exp")
                    if real(b + 1):
                        if u == 0:
                            pe.wait_ge(sem(f"L3_staged{1 - s}"), 16 * (turn + 1 if s == 0 else turn + 2))
                            need(pe, sem("L3_wh"), b + 1)
                            transposes(bank[4], xs[1 - s], G).then_inc(sem("L3_xT_mm"), 1)
                        if u == 2:
                            pe.wait_ge(sem("L3_xT"), b + 2)
                            need(pe, sem("L3_eT"), b + 1)
                            for g in range(G):
                                last = mm(v3(bank[4 + g // 2][:], 2)[:, g % 2, 0:D + 2 * HEADS], xT[1 - s][:, cols(g)], wh_w[:],
                                          start=True, stop=True)
                            last.then_inc(sem("L3_wh_mm"), 1)
                        if u == 6:
                            pe.wait_ge(sem("L3_split"), 6 * (b + 2))
                            pe.wait_ge(sem("L3_wh"), b + 2)
                            for g in range(G):
                                last = nc.tensor.transpose(bank[5][:].bitcast(BF16)[:, cols(g)], ep[:, cols(g)], identb[:])
                            last.then_inc(sem("L3_eT_mm"), 1)
                    p_times_v(3, b, s, u, 4)
                    if u % 2 == 1:
                        bb, g = b + (u - 7) // UNITS, (u - 7) % UNITS // 2
                        if real(bb):
                            pe.wait_ge(sem("L3_oT"), G * bb + g + 1)
                            need_or(pe, sem("L3_out"), G * bb + g, sem("L2_out"), BATCHES)
                            transposes(bank[7][:, cols(g % 2, 2 * N)], oT[g % 2], 2).then_inc(sem("L3_out_mm"), 1)
            if layers > 3:
                every_batch(pe, layer3, before=True, after=1)



def kernel(**inputs):
    import numpy as np
    import concourse.bacc as bacc
    from concourse.bass_utils import run_bass_kernel_spmd

    nc = bacc.Bacc("TRN2", target_bir_lowering=False, num_devices=1)
    arrays, handles = {}, {}
    for name, value in inputs.items():
        a = np.ascontiguousarray(value)
        arrays[f"in_{name}"] = a
        handles[name] = nc.dram_tensor(f"in_{name}", a.shape, mybir.dt.from_np(a.dtype), kind="ExternalInput").ap()
    out = nc.dram_tensor("out", (GRAPHS, N, D), F32, kind="ExternalOutput").ap()
    build(nc, handles, out)
    result = run_bass_kernel_spmd(nc, [arrays], core_ids=[0])
    return result.results[0]["out"]
```

```python
from contextlib import ExitStack

import concourse.bass as bass
from concourse import mybir

F32 = mybir.dt.float32
BF16 = mybir.dt.bfloat16
I32 = mybir.dt.int32
ALU = mybir.AluOpType
ACT = mybir.ActivationFunctionType
AX = mybir.AxisListType

GRAPHS, N, D = 64, 128, 128
LAYERS = 4
G = 4
BATCHES = GRAPHS // G
W = G * D
HEADS = 8
HD = D // HEADS
HP = 32
HQ = 4
UNITS = G * HEADS // HQ
ALPHA = 0.2
EPS = 1e-5
MASKED = -1e30
REL_LAST = 40
RELS = REL_LAST - 1


def need(eng, sem, value):
    if not isinstance(value, int) or value > 0:
        eng.wait_ge(sem, value)


def need_or(eng, sem, value, before, count):
    if isinstance(value, int) and value <= 0:
        eng.wait_ge(before, count)
    else:
        eng.wait_ge(sem, value)


def real(b):
    return not isinstance(b, int) or 0 <= b < BATCHES


def every_batch(eng, body, before=False, after=0):
    for b in range(-1 if before else 0, 4):
        body(b, b % 2, b // 2)
    with eng.Fori(2, BATCHES // 2 - 1) as turn:
        body(2 * turn, 0, turn)
        body(2 * turn + 1, 1, turn)
    for b in range(BATCHES - 2, BATCHES + after):
        body(b, b % 2, b // 2)


def later_layers(eng, layer1, layer2, layer3, last):
    every_batch(eng, layer1, before=True, after=1)
    layer2(-1, 1, -1)
    layer1(BATCHES + 1, 1, BATCHES // 2)
    every_batch(eng, layer2)
    for u in range(UNITS):
        layer2(BATCHES, 0, BATCHES // 2, (u,))
        layer3(-1, 1, -1, (u,))
    layer2(BATCHES + 1, 1, BATCHES // 2)
    every_batch(eng, layer3, after=last)


def build(nc, t, out):
    ctx = ExitStack()
    with ctx:
        def sb(name, shape, dt=F32):
            return ctx.enter_context(nc.sbuf_tensor(name, shape, dt))

        sems = {}

        def sem(name):
            if name not in sems:
                sems[name] = ctx.enter_context(nc.semaphore(name))
            return sems[name]

        bank = [ctx.enter_context(nc.psum_tensor(f"bank{i}", [128, 512], F32)) for i in range(8)]

        def cols(i, n=D):
            return slice(i * n, i * n + n)

        identf = sb("identf", [128, 128])
        identb = sb("identb", [128, 128], BF16)
        headmask = sb("headmask", [128, HEADS])
        sel1 = sb("sel1", [128, HEADS * 128], BF16)
        sel2 = sb("sel2", [128, HEADS * 128], BF16)
        neghalf = sb("neghalf", [128, G])
        NAT = ["L0_gnn_W_loop", "L0_gnn_Wg_loop", "L1_gnn_W", "L1_gnn_a_12", "L2_gnn_Wq", "L2_gnn_Wk",
               "L2_gnn_Wv", "L2_gnn_Wo", "L3_gnn_W", "L0_gnn_W_fwd", "L0_gnn_Wg_fwd", "L0_gnn_W_bwd",
               "L0_gnn_Wg_bwd"]
        nat_all = sb("nat_all", [128, len(NAT) * 128])
        nat = {n: nat_all[:, cols(i)] for i, n in enumerate(NAT)}
        hg_w = {k: sb(f"hg_w_{k}", [128, 2 * D]) for k in ("loop", "fwd", "bwd")}
        hg_bias = sb("hg_bias", [128, 2 * D])
        bias_rest = sb("bias_rest", [128, 2 * D])
        bias_part = sb("bias_part", [128, 2 * D], BF16)
        bias3 = sb("bias3", [128, 4 * D], BF16)
        ones = sb("ones", [128, 128], BF16)
        minus_one = sb("minus_one", [128, 1])
        a_cols = sb("a_cols", [128, 2])
        qk_bias = sb("qk_bias", [128, 3])
        bv_row = sb("bv_row", [128, D])
        bo_row = sb("bo_row", [128, D])
        a3_row = sb("a3_row", [128, 2 * HD])
        w12 = sb("w12", [128, 2 * D])
        w1T = sb("w1T", [128, 128])
        a12T = sb("a12T", [128, 128])
        a12w = sb("a12w", [128, 128])
        bil = sb("bil", [128, 128])
        wa1 = sb("wa1", [128, 128])
        wa2 = sb("wa2", [128, 128])
        gT = {k: sb(f"gT_{k}", [128, 128]) for k in ("loop", "fwd", "bwd")}
        qT_w = sb("qT_w", [128, 128])
        kT_w = sb("kT_w", [128, 128])
        vT_w = sb("vT_w", [128, 128])
        oT_w = sb("oT_w", [128, 128])
        a3_prod = sb("a3_prod", [128, 2 * D])
        a3_sum = sb("a3_sum", [128, 2 * HEADS])
        wh_w = sb("wh_w", [128, D + 2 * HEADS])

        X = sb("X", [128, GRAPHS * D])
        mask1 = sb("mask1", [128, GRAPHS * N], BF16)
        mask2 = sb("mask2", [128, GRAPHS * N], BF16)
        top = sb("top", [128, BATCHES])
        topmost = sb("topmost", [128, 1])
        toprow = sb("toprow", [1, 1])
        flag = sb("flag", [1, 1], I32)

        xs = [sb(f"xs{s}", [128, W]) for s in range(2)]
        xT = [sb(f"xT{s}", [128, W]) for s in range(2)]
        xn = [sb(f"xn{s}", [128, W]) for s in range(2)]
        yb = [sb(f"yb{s}", [128, W]) for s in range(2)]
        bn = [sb(f"bn{s}", [128, G * 6]) for s in range(2)]
        mv = [sb(f"mv{s}", [128, G * 2]) for s in range(2)]
        ln = [sb(f"ln{s}", [128, 3 * G]) for s in range(2)]
        loopm = [sb(f"loopm{s}", [128, W]) for s in range(2)]
        hg = [sb(f"hg{s}", [128, 2 * W]) for s in range(2)]
        vals = [sb(f"vals{s}", [128, W]) for s in range(2)]
        work = [sb(f"work{s}", [128, 2 * W]) for s in range(2)]
        uT = [hg[s][:, 0:W] for s in range(2)]
        y2 = [hg[s][:, W:2 * W] for s in range(2)]
        small_t = vals
        lk = [work[s][:, 0:W] for s in range(2)]
        e1 = loopm
        pT1 = [work[s][:, W:2 * W] for s in range(2)]
        elu = [sb(f"elu{s}", [128, W]) for s in range(2)]
        P = [sb(f"P{i}", [128, HQ * N]) for i in range(4)]
        pT = [sb(f"pT{i}", [128, HQ * N]) for i in range(2)]
        xw1 = [P[s] for s in range(2)]
        z1 = [pT[s] for s in range(2)]
        nm1 = [sb(f"nm1{s}", [128, G]) for s in range(2)]
        den1 = [sb(f"den1{s}", [128, G]) for s in range(2)]
        rd1 = [sb(f"rd1{s}", [128, G]) for s in range(2)]
        qT = [uT[s] for s in range(2)]
        kT = sb("kT", [128, W])
        kexp = sb("kexp", [128, 2 * HEADS * W])
        adj = kexp[:].bitcast(I32)
        v2 = work
        vx = [sb(f"vx{s}", [128, G * HEADS * HP]) for s in range(2)]
        t3 = [sb(f"t3{i}", [128, HQ * N]) for i in range(2)]
        nmx = [sb(f"nmx{i}", [128, HQ]) for i in range(4)]
        den = [sb(f"den{i}", [128, HQ]) for i in range(4)]
        rd = [sb(f"rd{i}", [128, HQ]) for i in range(4)]
        rd3 = [sb(f"rd3{i}", [128, HEADS]) for i in range(2)]
        oT = [sb(f"oT{i}", [128, 2 * N]) for i in range(2)]
        eT = [sb(f"eT{s}", [128, W], BF16) for s in range(2)]
        er = sb("er", [128, G * 2 * HEADS])
        ep = sb("ep", [128, G * 128], BF16)

        block = ctx.enter_context(nc.Block())

        def v3(ap, a):
            return ap.rearrange("p (a c) -> p a c", a=a)

        def x_of(b):
            return X[:, bass.ts(b, W)]

        def adj_of(b):
            return adj[:, bass.ts(b, W)]

        def heads_of(mask, b, g):
            return mask[:, bass.ts(G * b + g, N)].unsqueeze(1).broadcast_to([128, HQ, N])

        prep = []

        def add(dst, lhsT, rhs=None, after=-1):
            prep.append((dst, lhsT, rhs, after))
            return len(prep) - 1

        add(hg_w["loop"][:, 0:D], nat["L0_gnn_W_loop"])
        p = add(gT["loop"][:], nat["L0_gnn_Wg_loop"])
        add(hg_w["loop"][:, D:2 * D], nat["L0_gnn_W_loop"], gT["loop"][:], p)
        first = len(prep)
        w1_at = add(w1T[:], nat["L1_gnn_W"])
        a12_at = add(a12T[:], nat["L1_gnn_a_12"])
        gT_at = {k: add(gT[k][:], nat[f"L0_gnn_Wg_{k}"]) for k in ("fwd", "bwd")}
        for k in ("fwd", "bwd"):
            add(hg_w[k][:, 0:D], nat[f"L0_gnn_W_{k}"])
        a12w_at = add(a12w[:], a12T[:], w1T[:], a12_at)
        add(qT_w[:], nat["L2_gnn_Wq"])
        add(kT_w[:], nat["L2_gnn_Wk"])
        add(vT_w[:], nat["L2_gnn_Wv"])
        add(oT_w[:], nat["L2_gnn_Wo"])
        add(bil[:], w1T[:], a12w[:], a12w_at)
        add(wa1[:], w1T[:], a_cols[:, 0:1].broadcast_to([128, 128]), w1_at)
        add(wa2[:], w1T[:], a_cols[:, 1:2].broadcast_to([128, 128]), w1_at)
        for k in ("fwd", "bwd"):
            add(hg_w[k][:, D:2 * D], nat[f"L0_gnn_W_{k}"], gT[k][:], gT_at[k])

        def prep_copies(eng, copy, steps):
            for i in steps:
                dst = prep[i][0]
                eng.wait_ge(sem("prep_mm"), i + 1)
                copy(dst, bank[4 + i % 4][:, 0:dst.shape[-1]]).then_inc(sem("prep"), 1)

        def prep_pe(pe, steps):
            for i in steps:
                dst, lhsT, rhs, after = prep[i]
                need(pe, sem("prep"), max(after + 1, i - 3))
                o = bank[4 + i % 4][:, 0:128]
                if rhs is None:
                    last = nc.tensor.transpose(o, lhsT, identf[:])
                else:
                    last = nc.tensor.matmul(o, lhsT, rhs, start=True, stop=True)
                last.then_inc(sem("prep_mm"), 1)
            pe.wait_ge(sem("prep"), steps[-1] + 1)

        gx, ga = xs[0][:, 0:D], sb("ga", [128, N], I32)[:]
        gaf, gxT = yb[0][:, 0:N], xT[0][:, 0:D]
        onehot = pT1[0][:, 0:2 * N]
        ghg, gvals = hg[0][:, 0:4 * D], vals[0][:, 0:2 * D]
        gbias = lk[0][:, 0:4 * D]
        gsum = kexp[:, 0:GRAPHS * D]
        rel = sb("rel", [128, 1])
        gmv, gbn, gln = mv[0][:, 0:2], bn[0][:, 0:6], ln[0][:, 0:3]
        STEPS = GRAPHS * (RELS + 1)

        def if_general(eng, body):
            eng.wait_ge(sem("flag_set"), 1)
            value = eng.value_load(flag[0:1, 0:1], min_val=0, max_val=1)
            with eng.If(value > 0):
                eng.wait_ge(sem("L0_norm_done"), BATCHES)
                body(eng)
                eng.wait_ge(sem("G_kept"), 16 * GRAPHS)
                eng.wait_ge(sem("G_staged"), 32)

        def general_steps(eng, step, bias=None):
            step(0, 0, True, 0)
            with eng.Fori(1, GRAPHS) as g:
                step(g, g, True, 0)
            with eng.Fori(0, RELS) as r:
                if bias:
                    bias(r)
                with eng.Fori(0, GRAPHS) as g:
                    step(GRAPHS * (r + 1) + g, g, False, r)

        def general_sync(sp):
            def body(sp):
                for s in range(2):
                    sp.wait_ge(sem(f"L1_staged{s}"), 16)
                def bias(r):
                    sp.wait_ge(sem("G_hg"), GRAPHS * (r + 1))
                    for i, n in enumerate(("b_fwd", "bg_fwd", "b_bwd", "bg_bwd")):
                        src = t[f"L0_gnn_{n}"][bass.ds(r, 1), :].rearrange("a d -> (a d)").partition_broadcast(128)
                        sp.dma_start(gbias[:, cols(i)], src).then_inc(sem("G_bias"), 16)

                def load(i, g, loop, r):
                    need(sp, sem("G_sum"), i)
                    sp.dma_start(gx, t["x"][bass.ds(g, 1)].rearrange("g n d -> (g n) d")).then_inc(sem("G_x"), 16)
                    sp.dma_start(ga, t["adj"][bass.ds(g, 1)].rearrange("g n d -> (g n) d")).then_inc(sem("G_adj"), 16)
                general_steps(sp, load, bias)

                def again(g):
                    sp.wait_ge(sem("G_sum"), STEPS)
                    need(sp, sem("G_y"), g)
                    sp.dma_start(gx, t["x"][bass.ds(g, 1)].rearrange("g n d -> (g n) d")).then_inc(sem("G_x"), 16)
                    sp.wait_ge(sem("G_norm"), g + 1)
                    sp.dma_start(X[:, bass.ts(g, D)], xn[0][:, 0:D]).then_inc(sem("G_kept"), 16)
                for s in range(2):
                    sp.wait_ge(sem(f"L0_kept{s}"), 16 * BATCHES // 2)
                again(0)
                with sp.Fori(1, GRAPHS) as g:
                    again(g)
                sp.wait_ge(sem("G_kept"), 16 * GRAPHS)
                for s in range(2):
                    sp.dma_start(xs[s][:], x_of(s)).then_inc(sem("G_staged"), 16)
            if_general(sp, body)

        def find_flag(dve):
            dve.wait_ge(sem("top_mm"), 1)
            nc.vector.tensor_reduce(toprow[:], bank[7][0:1, 0:128], AX.X, ALU.max).then_inc(sem("top_set"), 1)
            dve.wait_ge(sem("top_set"), 2)
            nc.vector.tensor_scalar(flag[:], toprow[:], 1.0, None, ALU.is_ge).then_inc(sem("flag_set"), 1)

        def general_dve(dve):
            def body(dve):
                nc.vector.memset(rel[:], 1.0).then_inc(sem("G_rel"), 1)
                nc.vector.memset(gvals, 0.0).then_inc(sem("G_rel"), 1)
                dve.wait_ge(sem("G_rel"), 2)

                def bias(r):
                    dve.wait_ge(sem("G_onehot"), GRAPHS * (r + 1))
                    dve.wait_ge(sem("G_bias"), 64 * (r + 1))
                    nc.vector.tensor_scalar(rel[:], rel[:], 1.0, None, ALU.add).then_inc(sem("G_rel"), 1)

                def step(i, g, loop, r):
                    dve.wait_ge(sem("G_adj"), 16 * (i + 1))
                    nc.vector.tensor_copy(gaf, ga).then_inc(sem("G_adjf"), 1)
                    dve.wait_ge(sem("G_T_mm"), i + 1)
                    nc.vector.tensor_copy(gxT, bank[0][:, 0:128]).then_inc(sem("G_xT"), 1)
                    if not loop:
                        dve.wait_ge(sem("G_rel"), r + 3)
                        nc.vector.tensor_scalar(onehot[:, 0:N], bank[1][:, 0:N], rel[:], None, ALU.is_equal)
                    nc.vector.tensor_scalar(onehot[:, N:2 * N], gaf, rel[:], None, ALU.is_equal).then_inc(sem("G_onehot"), 1)
                    dve.wait_ge(sem("G_hg_mm"), i + 1)
                    if loop:
                        nc.vector.tensor_tensor(ghg[:, 0:2 * D], bank[2][:, 0:2 * D], hg_bias[:], ALU.add).then_inc(sem("G_hg"), 1)
                    else:
                        nc.vector.tensor_tensor(ghg, bank[2][:], gbias, ALU.add).then_inc(sem("G_hg"), 1)
                    dve.wait_ge(sem("G_gate"), i + 1)
                    n = 1 if loop else 2
                    h = v3(ghg, 4)
                    nc.vector.tensor_tensor(v3(gvals, 2)[:, 0:n, :], h[:, 0:2 * n:2, :], h[:, 1:2 * n:2, :], ALU.mult)\
                      .then_inc(sem("G_vals"), 1)
                    dve.wait_ge(sem("G_z_mm"), i + 1)
                    total = gsum[:, bass.ts(g, D)]
                    if loop:
                        nc.vector.tensor_copy(total, bank[3][:, 0:D]).then_inc(sem("G_sum"), 1)
                    else:
                        nc.vector.tensor_tensor(total, bank[3][:, 0:D], total, ALU.add).then_inc(sem("G_sum"), 1)
                general_steps(dve, step, bias)

                def norm(g):
                    dve.wait_ge(sem("G_sum"), STEPS)
                    dve.wait_ge(sem("G_x"), 16 * (STEPS + g + 1))
                    need(dve, sem("G_norm"), g)
                    nc.vector.scalar_tensor_tensor(yb[0][:, 0:D], gsum[:, bass.ts(g, D)], 0.0, gx, ALU.max, ALU.add)\
                      .then_inc(sem("G_y"), 1)
                    dve.wait_ge(sem("G_y"), g + 1)
                    nc.vector.bn_stats(gbn, yb[0][:, 0:D])
                    dve.drain()
                    nc.vector.bn_aggr(gmv, gbn)
                    dve.drain()
                    nc.vector.tensor_scalar(gln[:, 0:1], gmv[:, 0:1], -1.0, None, ALU.mult)
                    nc.vector.tensor_scalar(gln[:, 1:2], gmv[:, 1:2], EPS, None, ALU.add).then_inc(sem("G_stats"), 1)
                norm(0)
                with dve.Fori(1, GRAPHS) as g:
                    norm(g)
            if_general(dve, body)

        def l3_weights(dve):
            dve.wait_ge(sem("params"), sems["n_params"])
            for half in range(2):
                nc.vector.tensor_tensor(v3(a3_prod[:, cols(half)], HEADS), v3(nat["L3_gnn_W"], HEADS),
                                        a3_row[:, cols(half, HD)].unsqueeze(1).broadcast_to([128, HEADS, HD]), ALU.mult)\
                  .then_inc(sem("dve_set"), 1)
            nc.vector.tensor_copy(wh_w[:, 0:D], nat["L3_gnn_W"])
            dve.wait_ge(sem("dve_set"), 3)
            nc.vector.tensor_reduce(a3_sum[:], v3(a3_prod[:], 2 * HEADS), AX.X, ALU.add).then_inc(sem("dve_set"), 1)
            dve.wait_ge(sem("dve_set"), 4)
            nc.vector.tensor_copy(wh_w[:, D:D + HEADS], a3_sum[:, HEADS:2 * HEADS])
            nc.vector.tensor_copy(wh_w[:, D + HEADS:], a3_sum[:, 0:HEADS])


        def general_act(act):
            def body(act):
                def step(i, g, loop, r):
                    act.wait_ge(sem("G_hg"), i + 1)
                    gate = v3(ghg, 4)[:, 1:(2 if loop else 4):2, :]
                    nc.scalar.activation(gate, gate, ACT.Sigmoid).then_inc(sem("G_gate"), 1)
                general_steps(act, step)
            if_general(act, body)

        def general_pe(pe):
            pe.wait_ge(sem("top_set"), 1)
            nc.tensor.transpose(bank[7][0:1, 0:128], topmost[:], identf[:]).then_inc(sem("top_mm"), 1)

            def body(pe):
                def step(i, g, loop, r):
                    mm = nc.tensor.matmul
                    pe.wait_ge(sem("G_x"), 16 * (i + 1))
                    pe.wait_ge(sem("G_adjf"), i + 1)
                    nc.tensor.transpose(bank[0][:, 0:128], gx, identf[:])
                    nc.tensor.transpose(bank[1][:, 0:128], gaf, identf[:]).then_inc(sem("G_T_mm"), 1)
                    pe.wait_ge(sem("G_onehot"), i + 1)
                    if loop:
                        mm(bank[2][:, 0:2 * D], gxT, hg_w["loop"][:], start=True, stop=True).then_inc(sem("G_hg_mm"), 1)
                    else:
                        mm(bank[2][:, 0:2 * D], gxT, hg_w["fwd"][:], start=True, stop=True)
                        mm(bank[2][:, 2 * D:4 * D], gxT, hg_w["bwd"][:], start=True, stop=True).then_inc(sem("G_hg_mm"), 1)
                    pe.wait_ge(sem("G_vals"), i + 1)
                    if loop:
                        mm(bank[3][:, 0:D], onehot[:, N:2 * N], gvals[:, 0:D], start=True, stop=True).then_inc(sem("G_z_mm"), 1)
                    else:
                        mm(bank[3][:, 0:D], onehot[:, 0:N], gvals[:, 0:D], start=True, stop=False)
                        mm(bank[3][:, 0:D], onehot[:, N:2 * N], gvals[:, D:2 * D], start=False, stop=True).then_inc(sem("G_z_mm"), 1)
                general_steps(pe, step)
            if_general(pe, body)

        def general_pool(pool):
            def body(pool):
                def norm(g):
                    need(pool, sem("G_kept"), 16 * g)
                    pool.wait_ge(sem("G_stats"), g + 1)
                    nc.gpsimd.tensor_tensor(gln[:, 2:3], gln[:, 1:2], neghalf[:, 0:1], ALU.pow)
                    pool.drain()
                    nc.gpsimd.tensor_scalar(xn[0][:, 0:D], yb[0][:, 0:D], gln[:, 0:1], gln[:, 2:3], ALU.add, ALU.mult)\
                      .then_inc(sem("G_norm"), 1)
                norm(0)
                with pool.Fori(1, GRAPHS) as g:
                    norm(g)
            if_general(pool, body)

        @block.sync
        def _(sp):
            def load(b, s, turn):
                need(sp, sem(f"adj_loaded{s}"), 16 * turn)
                need(sp, sem(f"x_loaded{s}"), 16 * turn)
                sp.dma_start(v3(x_of(b), G), t["x"][bass.ts(b, G)].rearrange("g n d -> n g d"))\
                  .then_inc(sem(f"x_loaded{s}"), 16)
                sp.dma_start(v3(adj_of(b), G), t["adj"][bass.ts(b, G)].rearrange("g n m -> n g m"))\
                  .then_inc(sem(f"adj_loaded{s}"), 16)

            def stage(L):
                def load(b, s, turn):
                    if isinstance(b, int) and b < 2:
                        sp.wait_ge(sem(f"L{L - 1}_xT_mm"), BATCHES - 1 + b)
                    else:
                        free = sp.snap(b - 1)
                        sp.wait_ge(sem(f"L{L}_xT_mm"), free)
                    sp.wait_ge(sem(f"L{L - 1}_kept{s}"), 16 * (turn + 1))
                    sp.dma_start(xs[s][:], x_of(b)).then_inc(sem(f"L{L}_staged{s}"), 16)
                return load

            def stage0(b, s, turn):
                sp.wait_ge(sem(f"x_loaded{s}"), 16 * (turn + 1))
                need(sp, sem("L0_xT_mm"), b - 1)
                sp.dma_start(xs[s][:], x_of(b)).then_inc(sem(f"L0_staged{s}"), 16)

            def layer0(b, s, turn):
                if real(b + 2):
                    load(b + 2, s, turn + 1)
                if real(b + 1):
                    stage0(b + 1, 1 - s, turn + s)
                stage_next(0, b, s)
                if real(b - 4):
                    keep(0, b - 4, s, turn - 2)

            def keep(L, b, s, turn):
                sp.wait_ge(sem(f"L{L}_norm_done"), b + 1)
                if L < LAYERS - 1:
                    sp.dma_start(x_of(b), xn[s][:]).then_inc(sem(f"L{L}_kept{s}"), 16)
                else:
                    sp.dma_start(out[bass.ts(b, G)].rearrange("g n d -> n g d"), v3(xn[s][:], G))\
                      .then_inc(sem(f"L{L}_kept{s}"), 16)

            def stage_next(L, b, s):
                if isinstance(b, int) and BATCHES <= b < BATCHES + 2:
                    stage(L + 1)(b - BATCHES, s, 0)

            def layer(L, lag):
                def both(b, s, turn):
                    if real(b) and (not isinstance(b, int) or b >= 2):
                        stage(L)(b, s, turn)
                    if L < LAYERS - 1:
                        stage_next(L, b, s)
                    if real(b - lag):
                        keep(L, b - lag, (s + lag) % 2, turn)
                every_batch(sp, both, after=lag)

            load(0, 0, 0)
            every_batch(sp, layer0, before=True, after=4)
            general_sync(sp)
            for L in range(1, LAYERS):
                layer(L, lag=4)
            for s in range(2):
                sp.wait_ge(sem(f"L{LAYERS - 1}_kept{s}"), 16 * BATCHES // 2)

        def norm_pow(pool, L, b, s, turn):
            if isinstance(b, int) and b < 2:
                if L > 0:
                    pool.wait_ge(sem(f"L{L - 1}_kept{s}"), 16 * BATCHES // 2)
            else:
                pool.wait_ge(sem(f"L{L}_kept{s}"), 16 * turn)
            pool.wait_ge(sem(f"L{L}_stats_done"), b + 1)
            nc.gpsimd.tensor_tensor(ln[s][:, 2 * G:3 * G], ln[s][:, G:2 * G], neghalf[:], ALU.pow)
            pool.drain()

        def norm_scale(L, s, graphs):
            for g in graphs:
                last = nc.gpsimd.tensor_scalar(xn[s][:, cols(g)], yb[s][:, cols(g)], ln[s][:, g:g + 1],
                                               ln[s][:, 2 * G + g:2 * G + g + 1], ALU.add, ALU.mult)
            if g == G - 1:
                last.then_inc(sem(f"L{L}_norm_done"), 1)

        def norm_pool(pool, L, b, s, turn):
            norm_pow(pool, L, b, s, turn)
            norm_scale(L, s, range(G))

        def y_slot_free(dve, L, b):
            if isinstance(b, int) and b < 2:
                if L > 0:
                    dve.wait_ge(sem(f"L{L - 1}_norm_done"), BATCHES - 1 + b)
            else:
                dve.wait_ge(sem(f"L{L}_norm_done"), b - 1)

        def stats_nodes(dve, L, b, s, graphs):
            dve.wait_ge(sem(f"L{L}_y_done"), b + 1)
            for g in graphs:
                nc.vector.bn_stats(bn[s][:, cols(g, 6)], yb[s][:, cols(g)])

        def stats_done(dve, L, s):
            dve.drain()
            for g in range(G):
                nc.vector.bn_aggr(mv[s][:, cols(g, 2)], bn[s][:, cols(g, 6)])
            dve.drain()
            m = v3(mv[s][:], G)
            nc.vector.tensor_scalar(ln[s][:, 0:G], m[:, :, 0], -1.0, None, ALU.mult)
            nc.vector.tensor_scalar(ln[s][:, G:2 * G], m[:, :, 1], EPS, None, ALU.add)\
              .then_inc(sem(f"L{L}_stats_done"), 1)

        def stats_dve(dve, L, b, s):
            stats_nodes(dve, L, b, s, range(G))
            stats_done(dve, L, s)

        @block.gpsimd
        def _(pool):
            nc.gpsimd.memset(identf[:], 0.0)
            nc.gpsimd.memset(ones[:], 1.0)
            nc.gpsimd.memset(minus_one[:], -1.0)
            nc.gpsimd.memset(sel1[:], 0.0)
            nc.gpsimd.memset(sel2[:], 0.0)
            nc.gpsimd.memset(headmask[:], 1.0)
            nc.gpsimd.memset(neghalf[:], -0.5).then_inc(sem("pool_set"), 1)
            steps = 1
            pool.wait_ge(sem("pool_set"), steps)

            def select(out_, pattern, base, op=ALU.not_equal, fill=1.0, step=1):
                nonlocal steps
                nc.gpsimd.affine_select(out=out_, in_=out_, compare_op=op, fill=fill, base=base,
                                        pattern=pattern, channel_multiplier=step).then_inc(sem("pool_set"), 1)
                steps += 1
                pool.wait_ge(sem("pool_set"), steps)

            select(identf[:], [[-1, 128]], 0)
            nc.gpsimd.tensor_copy(identb[:], identf[:]).then_inc(sem("ident"), 1)
            select(headmask[:], [[-HD, HEADS]], 0, ALU.is_ge, 0.0)
            select(headmask[:], [[HD, HEADS]], HD - 1, ALU.is_ge, 0.0, -1)
            for part in range(3):
                select(sel2[:].rearrange("p (h c) -> p h c", h=HEADS), [[-1, HEADS], [0, 128]], -32 * part)
                select(sel1[:].rearrange("p (h c) -> p h c", h=HEADS), [[-1, HEADS], [0, 128]], -32 * part - HEADS)
            nc.gpsimd.memset(ep[:], 0.0).then_inc(sem("pool_ready"), 1)

            every_batch(pool, lambda b, s, turn: norm_pool(pool, 0, b, s, turn))
            general_pool(pool)

            def layer1(b, s, turn):
                if isinstance(b, int) and b == BATCHES - 1:
                    layer2(-1, 1, -1)
                norm_pool(pool, 1, b, s, turn)

            def layer2(b, s, turn):
                if real(b + 1):
                    pool.wait_ge(sem("L2_k"), b + 2)
                    need(pool, sem("L2_s_mm"), UNITS * b)
                    nc.gpsimd.tensor_tensor(kexp[:, cols((1 - s) * HEADS, W)], kT[:],
                                            headmask[:, 0:1].broadcast_to([128, W]), ALU.mult)
                    for h in range(1, HEADS):
                        last = nc.gpsimd.tensor_scalar(kexp[:, cols((1 - s) * HEADS + h, W)], kT[:],
                                                       headmask[:, h:h + 1], 1.0, ALU.mult, ALU.mult)
                    last.then_inc(sem("L2_kexp"), 1)
                if real(b - 2):
                    norm_pool(pool, 2, b - 2, s, turn - 1)

            every_batch(pool, layer1)
            every_batch(pool, layer2, after=2)

            def layer3(b, s, turn):
                for u in range(UNITS):
                    if real(b):
                        pool.wait_ge(sem("L3_max"), UNITS * b + u + 1)
                        nc.gpsimd.tensor_tensor(v3(P[u % 4][:], HQ), v3(P[u % 4][:], HQ),
                                                nmx[u % 4][:].unsqueeze(2).broadcast_to([128, HQ, N]), ALU.add)\
                          .then_inc(sem("L3_less_max"), 1)
                    if real(b - 2):
                        if u == 5:
                            norm_pow(pool, 3, b - 2, s, turn - 1)
                        if u >= 6:
                            norm_scale(3, s, (2 * (u - 6), 2 * (u - 6) + 1))
            every_batch(pool, layer3, after=2)

        @block.scalar
        def _(act):
            def row(ap, n):
                return ap.rearrange("a n -> (a n)").partition_broadcast(128) if len(ap.shape) == 2 else ap.partition_broadcast(128)

            def col(ap):
                return ap.rearrange("n a -> n a") if len(ap.shape) == 2 else ap.unsqueeze(1)
            for dst, src in ((nat["L0_gnn_W_loop"], t["L0_gnn_W_loop"][:, :]), (nat["L0_gnn_Wg_loop"], t["L0_gnn_Wg_loop"][:, :]),
                             (hg_bias[:, 0:D], row(t["L0_gnn_b_loop"], D)), (hg_bias[:, D:2 * D], row(t["L0_gnn_bg_loop"], D))):
                act.dma_start(dst, src).then_inc(sem("L0_params"), 16)
            loads = [(nat[n], t[n][:, :]) for n in NAT[2:]]
            loads += [(a_cols[:, 0:1], col(t["L1_gnn_a_1"])), (a_cols[:, 1:2], col(t["L1_gnn_a_2"])),
                      (w12[:, 0:D], t["L1_gnn_W_1"][:, :]), (w12[:, D:2 * D], t["L1_gnn_W_2"][:, :]),
                      (qk_bias[:, 0:1], col(t["L2_gnn_bq"])), (qk_bias[:, 1:2], col(t["L2_gnn_bk"])),
                      (bv_row[:], row(t["L2_gnn_bv"], D)), (bo_row[:], row(t["L2_gnn_bo"], D)),
                      (a3_row[:], row(t["L3_gnn_a"], 2 * HD))]
            sems["n_params"] = 16 * len(loads)
            act.wait_ge(sem("pool_set"), 1)

            def layer0(b, s, turn):
                if real(b + 1):
                    act.wait_ge(sem("L0_xT_mm"), b + 2)
                    need(act, sem("L0_hg_mm"), b)
                    nc.scalar.copy(xT[1 - s][:], bank[0][:]).then_inc(sem("L0_xT"), 1)
                if real(b):
                    act.wait_ge(sem(f"adj_loaded{s}"), 16 * (turn + 1))
                    need(act, sem("L0_top"), b - 1)
                    nc.scalar.activation(elu[s][:], adj_of(b), ACT.Relu, bias=minus_one[:],
                                         accum_out=top[:, bass.ds(b, 1)]).then_inc(sem("L0_top"), 1)
                    act.wait_ge(sem("L0_hg_mm"), b + 1)
                    need(act, sem("L0_vals"), b - 1)
                    for i in range(2):
                        last = nc.scalar.activation(v3(hg[s][:, cols(i, 2 * D)], 2),
                                                    v3(bank[1 + 3 * s + i][:], 4)[:, 1:4:2, :], ACT.Sigmoid)
                    last.then_inc(sem("L0_gate"), 1)
                    if isinstance(b, int) and b < 4:
                        share = -(-len(loads) // 4)
                        for dst, src in loads[b * share:(b + 1) * share]:
                            act.dma_start(dst, src).then_inc(sem("params"), 16)
            every_batch(act, layer0, before=True)
            act.wait_ge(sem("params"), 16 * len(loads))
            nc.scalar.mul(qk_bias[:, 2:3], qk_bias[:, 0:1], HD ** -0.5).then_inc(sem("bq_scaled"), 1)
            prep_copies(act, nc.scalar.copy, range(first, len(prep)))
            general_act(act)

            def layer1(b, s, turn):
                if real(b - 2):
                    act.wait_ge(sem("L1_z"), b - 1)
                    need(act, sem("L1_y_done"), b - 3)
                    nc.scalar.activation(elu[s][:], z1[s][:], ACT.Relu, scale=-1.0).then_inc(sem("L1_neg"), 1)
                    act.wait_ge(sem("L1_neg"), b - 1)
                    nc.scalar.activation(elu[s][:], elu[s][:], ACT.Exp, scale=-1.0).then_inc(sem("L1_elu_exp"), 1)
                if real(b):
                    act.wait_ge(sem("L1_u_mm"), b + 1)
                    need(act, sem("L1_logits_mm"), b - 1)
                    nc.scalar.activation(uT[s], bank[1][:], ACT.Identity, bias=wa1[:, 0:1]).then_inc(sem("L1_uT"), 1)
                if real(b - 1):
                    act.wait_ge(sem("L1_max"), b)
                    need(act, sem("L1_pT_mm"), b - 2)
                    for g in range(G):
                        last = nc.scalar.activation(e1[1 - s][:, cols(g)], lk[1 - s][:, cols(g)], ACT.Exp,
                                                    bias=nm1[1 - s][:, g:g + 1], accum_out=den1[1 - s][:, g:g + 1])
                    last.then_inc(sem("L1_exp"), 1)
                if real(b - 1):
                    act.wait_ge(sem("L1_pT_mm"), b)
                    need(act, sem("L1_z_mm"), b - 2)
                    nc.scalar.copy(pT1[1 - s], bank[4][:]).then_inc(sem("L1_pT"), 1)
                if real(b):
                    act.wait_ge(sem("L1_xw_mm"), b + 1)
                    need(act, sem("L1_z_mm"), b - 1)
                    need(act, sem("L1_z"), b - 1)
                    for half, dst in ((1, y2), (0, xw1)):
                        for i in range(2):
                            last = nc.scalar.copy(v3(dst[s][:, cols(i, 2 * D)], 2),
                                                  v3(bank[3 + 2 * i][:], 2)[:, :, cols(half)])
                    last.then_inc(sem("L1_xw"), 1)
                if real(b):
                    act.wait_ge(sem("L1_logits_mm"), b + 1)
                    need(act, sem("L1_leaky"), b - 1)
                    nc.scalar.mul(small_t[s][:], bank[2][:], ALPHA).then_inc(sem("L1_scaled"), 1)

            def copy_pT(L, b, u, lag):
                bb, uu = b + (u - lag) // UNITS, (u - lag) % UNITS
                if real(bb):
                    act.wait_ge(sem(f"L{L}_pT_mm"), UNITS * bb + uu + 1)
                    need(act, sem(f"L{L}_pv_mm"), UNITS * bb + uu - 1)
                    nc.scalar.copy(pT[uu % 2][:], bank[2 + uu % 2][:]).then_inc(sem(f"L{L}_pT"), 1)

            def copy_oT(L, b, u, lag):
                if (u - lag) % 2 == 0:
                    bb, g = b + (u - lag) // UNITS, (u - lag) % UNITS // 2
                    if real(bb):
                        act.wait_ge(sem(f"L{L}_pv_mm"), UNITS * bb + 2 * g + 2)
                        need(act, sem(f"L{L}_out_mm"), G * bb + g - 1)
                        n = N if L == 2 else 2 * N
                        nc.scalar.copy(oT[g % 2][:, 0:n], bank[6][:, cols(g % 2, n)]).then_inc(sem(f"L{L}_oT"), 1)

            def layer2(b, s, turn, units=range(UNITS)):
                for u in units:
                    if u == 6 and real(b + 1):
                        act.wait_ge(sem("L2_q_mm"), b + 2)
                        need(act, sem("L2_s_mm"), UNITS * b)
                        nc.scalar.activation(qT[1 - s], bank[4][:], ACT.Identity, bias=qk_bias[:, 2:3],
                                             scale=HD ** -0.5).then_inc(sem("L2_q"), 1)
                    copy_oT(2, b, u, 5)
                    if real(b):
                        U = UNITS * b + u
                        act.wait_ge(sem("L2_max"), U + 1)
                        need(act, sem("L2_pT_mm"), U - 3)
                        for j in range(HQ):
                            last = nc.scalar.activation(P[u % 4][:, cols(j)], bank[u % 2][:, cols(j)], ACT.Exp,
                                                        bias=nmx[u % 4][:, j:j + 1], accum_out=den[u % 4][:, j:j + 1])
                        last.then_inc(sem("L2_exp"), 1)
                    copy_pT(2, b, u, 2)

            def layer3(b, s, turn, units=range(UNITS)):
                for u in units:
                    if u == 7 and real(b + 1):
                        act.wait_ge(sem("L3_eT_mm"), b + 2)
                        need(act, sem("L3_s_mm"), UNITS * b)
                        nc.scalar.copy(eT[1 - s][:], bank[5][:].bitcast(BF16)[:, 0:W]).then_inc(sem("L3_eT"), 1)
                    if real(b):
                        U = UNITS * b + u
                        act.wait_ge(sem("L3_s_mm"), U + 1)
                        need(act, sem("L3_leaky"), U - 1)
                        nc.scalar.mul(t3[u % 2][:], bank[u % 2][:], ALPHA).then_inc(sem("L3_scaled"), 1)
                    bb, uu = b + (u - 2) // UNITS, (u - 2) % UNITS
                    if real(bb):
                        act.wait_ge(sem("L3_less_max"), UNITS * bb + uu + 1)
                        nc.scalar.activation(P[uu % 4][:], P[uu % 4][:], ACT.Exp).then_inc(sem("L3_exp"), 1)
                    copy_pT(3, b, u, 4)
                    copy_oT(3, b, u, 6)
                    if real(b + 1):
                        if u == 0:
                            act.wait_ge(sem("L3_xT_mm"), b + 2)
                            need(act, sem("L3_wh_mm"), b + 1)
                            nc.scalar.copy(xT[1 - s][:], bank[4][:]).then_inc(sem("L3_xT"), 1)
                        if u == 5:
                            act.wait_ge(sem("L3_split"), 6 * (b + 1) + 1)
                            need(act, sem("L3_pv_mm"), UNITS * b)
                            for i in range(2):
                                last = nc.scalar.copy(
                                    vx[1 - s][:, cols(i, 2 * HEADS * HP)].rearrange("p (g h c) -> p g h c", g=2, h=HEADS)[:, :, :, 0:HD],
                                    v3(bank[4 + i][:], 2)[:, :, 0:D].rearrange("p g (h c) -> p g h c", h=HEADS))
                            last.then_inc(sem("L3_wh"), 1)
            later_layers(act, layer1, layer2, layer3, last=1)

        @block.vector
        def _(dve):
            for s in range(2):
                nc.vector.memset(vx[s][:], 0.0)
            nc.vector.memset(bias3[:], 0.0).then_inc(sem("dve_set"), 1)
            dve.wait_ge(sem("dve_set"), 1)
            for s in range(2):
                nc.vector.memset(vx[s][:].rearrange("p (a c) -> p a c", c=HP)[:, :, HD:HD + 1], 1.0)
            prep_copies(dve, nc.vector.tensor_copy, range(first))
            dve.wait_ge(sem("L0_params"), 64)
            rest = hg_bias
            for part in range(3):
                row = slice(32 * part, 32 * part + 1)
                nc.vector.tensor_copy(bias_part[:], rest[:]).then_inc(sem("bias_split"), 1)
                dve.wait_ge(sem("bias_split"), 2 * part + 1)
                for i in range(2):
                    nc.vector.tensor_copy(bias3[row, cols(i, 2 * D)], bias_part[row, :])
                nc.vector.tensor_tensor(bias_rest[:], rest[:], bias_part[:], ALU.subtract).then_inc(sem("bias_split"), 1)
                dve.wait_ge(sem("bias_split"), 2 * part + 2)
                rest = bias_rest

            def layer0(b, s, turn):
                if real(b):
                    dve.wait_ge(sem(f"adj_loaded{s}"), 16 * (turn + 1))
                    need(dve, sem("L0_z_mm"), b - 1)
                    nc.vector.tensor_scalar(loopm[s][:], adj_of(b), 1.0, None, ALU.is_equal)
                    nc.vector.tensor_scalar(mask1[:, bass.ts(b, W)], adj_of(b), 0.0, MASKED, ALU.is_le, ALU.mult)
                    nc.vector.tensor_scalar(mask2[:, bass.ts(b, W)], adj_of(b), 0.0, MASKED, ALU.is_equal, ALU.mult)
                    dve.wait_ge(sem("L0_gate"), b + 1)
                    for i in range(2):
                        last = nc.vector.tensor_tensor(v3(vals[s][:, cols(i, 2 * D)], 2), v3(bank[1 + 3 * s + i][:], 4)[:, 0:4:2, :],
                                                       v3(hg[s][:, cols(i, 2 * D)], 2), ALU.mult)
                    last.then_inc(sem("L0_vals"), 1)
                if real(b - 1):
                    dve.wait_ge(sem("L0_z_mm"), b)
                    y_slot_free(dve, 0, b - 1)
                    nc.vector.scalar_tensor_tensor(yb[1 - s][:], bank[3][:], 0.0, x_of(b - 1), ALU.max, ALU.add)\
                      .then_inc(sem("L0_y_done"), 1)
                    stats_dve(dve, 0, b - 1, 1 - s)
            every_batch(dve, layer0, after=1)
            dve.wait_ge(sem("L0_top"), BATCHES)
            nc.vector.tensor_reduce(topmost[:], top[:], AX.X, ALU.max).then_inc(sem("top_set"), 1)
            find_flag(dve)
            l3_weights(dve)
            general_dve(dve)

            def layer1(b, s, turn):
                if real(b - 2):
                    dve.wait_ge(sem("L1_elu_exp"), b - 1)
                    nc.vector.scalar_tensor_tensor(elu[s][:], z1[s][:], 0.0, elu[s][:], ALU.max, ALU.add)\
                      .then_inc(sem("L1_elu"), 1)
                if real(b - 2):
                    y_slot_free(dve, 1, b - 2)
                    dve.wait_ge(sem("L1_elu"), b - 1)
                    nc.vector.scalar_tensor_tensor(yb[s][:], elu[s][:], -1.0, x_of(b - 2), ALU.add, ALU.add)\
                      .then_inc(sem("L1_y_done"), 1)
                    stats_dve(dve, 1, b - 2, s)
                if real(b + 1):
                    dve.wait_ge(sem("L1_xT_mm"), b + 2)
                    need(dve, sem("L1_logits_mm"), b)
                    nc.vector.tensor_copy(xT[1 - s][:], bank[0][:]).then_inc(sem("L1_xT"), 1)
                if real(b - 1):
                    dve.wait_ge(sem("L1_exp"), b)
                    nc.vector.reciprocal(rd1[1 - s][:], den1[1 - s][:]).then_inc(sem("L1_rden"), 1)
                if real(b - 1):
                    dve.wait_ge(sem("L1_rden"), b)
                    dve.wait_ge(sem("L1_z_mm"), b)
                    for g in range(G):
                        last = nc.vector.scalar_tensor_tensor(z1[1 - s][:, cols(g)], bank[6][:, cols(g)], rd1[1 - s][:, g:g + 1],
                                                              xw1[1 - s][:, cols(g)], ALU.mult, ALU.add)
                    last.then_inc(sem("L1_z"), 1)
                if real(b):
                    dve.wait_ge(sem("L1_scaled"), b + 1)
                    need(dve, sem("L1_exp"), b - 1)
                    nc.vector.tensor_tensor(lk[s], bank[2][:], small_t[s][:], ALU.max).then_inc(sem("L1_leaky"), 1)
                    dve.wait_ge(sem("L1_leaky"), b + 1)
                    nc.vector.tensor_reduce(nm1[s][:], v3(lk[s], G), AX.X, ALU.max, negate=True).then_inc(sem("L1_max"), 1)

            def layer2(b, s, turn, units=range(UNITS)):
                for u in units:
                    if real(b):
                        U = UNITS * b + u
                        dve.wait_ge(sem("L2_s_mm"), U + 1)
                        need(dve, sem("L2_exp"), U - 3)
                        nc.vector.tensor_reduce(nmx[u % 4][:], v3(bank[u % 2][:], HQ), AX.X, ALU.max, negate=True)\
                          .then_inc(sem("L2_max"), 1)
                    if u == 2 and real(b + 1):
                        dve.wait_ge(sem("L2_xT_mm"), b + 2)
                        need(dve, sem("L2_v_mm"), b)
                        nc.vector.tensor_copy(xT[1 - s][:], bank[4][:]).then_inc(sem("L2_xT"), 1)
                    if u == 4 and real(b + 1):
                        dve.wait_ge(sem("L2_k_mm"), b + 2)
                        need(dve, sem("L2_kexp"), b + 1)
                        nc.vector.tensor_scalar(kT[:], bank[5][:], qk_bias[:, 1:2], None, ALU.add).then_inc(sem("L2_k"), 1)
                    if u == 0 and isinstance(b, int) and b == 0:
                        for i in range(2):
                            last = nc.vector.memset(v2[i][:], 0.0)
                        last.then_inc(sem("L2_v_zero"), 1)
                        dve.wait_ge(sem("L2_v_zero"), 1)
                    if u == 0 and real(b):
                        dve.wait_ge(sem("L2_v_mm"), b + 1)
                        need(dve, sem("L2_pv_mm"), UNITS * (b - 1))
                        for odd in range(2):
                            at = odd * (HP + HD)
                            last = nc.vector.tensor_tensor(
                                v2[s][:].rearrange("p (g h c) -> p g h c", g=G, h=HEADS // 2)[:, :, :, at:at + HD],
                                bank[5][:].rearrange("p (g h c) -> p g h c", g=G, h=HEADS // 2)[:, :, :, odd * HD:odd * HD + HD],
                                v3(bv_row[:], HEADS // 2)[:, :, odd * HD:odd * HD + HD].unsqueeze(1)
                                .broadcast_to([128, G, HEADS // 2, HD]), ALU.add)
                        last.then_inc(sem("L2_v"), 1)
                    bb, uu = b + (u - 1) // UNITS, (u - 1) % UNITS
                    if real(bb):
                        U = UNITS * bb + uu
                        dve.wait_ge(sem("L2_exp"), U + 1)
                        nc.vector.reciprocal(rd[uu % 4][:], den[uu % 4][:]).then_inc(sem("L2_rden"), 1)
                        dve.wait_ge(sem("L2_rden"), U + 1)
                        nc.vector.tensor_tensor(v3(P[uu % 4][:], HQ), v3(P[uu % 4][:], HQ),
                                                rd[uu % 4][:].unsqueeze(2).broadcast_to([128, HQ, N]), ALU.mult)\
                          .then_inc(sem("L2_p"), 1)
                    if u == 5 and real(b - 1):
                        dve.wait_ge(sem("L2_out_mm"), G * b)
                        y_slot_free(dve, 2, b - 1)
                        nc.vector.tensor_tensor(v3(yb[1 - s][:], G), v3(bank[7][:], G),
                                                bo_row[:].unsqueeze(1).broadcast_to([128, G, D]), ALU.add)\
                          .then_inc(sem("L2_out"), 1)
                    if u == 6 and real(b - 1):
                        dve.wait_ge(sem("L2_out"), b)
                        nc.vector.tensor_tensor(yb[1 - s][:], yb[1 - s][:], x_of(b - 1), ALU.add)\
                          .then_inc(sem("L2_y_done"), 1)
                    if u == 7 and real(b - 1):
                        stats_nodes(dve, 2, b - 1, 1 - s, (0, 1))
                    if u == 1 and real(b - 2):
                        stats_nodes(dve, 2, b - 2, s, (2, 3))
                    if u == 3 and real(b - 2):
                        stats_done(dve, 2, s)

            def split_e(dve, b, n):
                def part(k):
                    return v3(ep[:], G)[:, :, 32 * k:32 * k + 2 * HEADS]
                rest = v3(er[:], G)
                if n == 0:
                    dve.wait_ge(sem("L3_wh_mm"), b + 1)
                    for i in range(2):
                        last = nc.vector.tensor_copy(rest[:, 2 * i:2 * i + 2, :], v3(bank[4 + i][:], 2)[:, :, D:D + 2 * HEADS])
                else:
                    dve.wait_ge(sem("L3_split"), 6 * b + n)
                    if n == 1:
                        need(dve, sem("L3_eT_mm"), b)
                    if n % 2 == 1:
                        last = nc.vector.tensor_copy(part(n // 2), rest)
                    else:
                        last = nc.vector.tensor_tensor(rest, rest, part(n // 2 - 1), ALU.subtract)
                last.then_inc(sem("L3_split"), 1)

            def layer3(b, s, turn, units=range(UNITS)):
                for u in units:
                    if real(b):
                        U = UNITS * b + u
                        dve.wait_ge(sem("L3_scaled"), U + 1)
                        need(dve, sem("L3_pT_mm"), U - 3)
                        nc.vector.tensor_tensor(P[u % 4][:], bank[u % 2][:], t3[u % 2][:], ALU.max)\
                          .then_inc(sem("L3_leaky"), 1)
                    if u in (3, 4, 5) and real(b + 1):
                        split_e(dve, b + 1, 2 * u - 5)
                    if u % 2 == 1:
                        bb, g = b + (u - 9) // UNITS, u // 2
                        if real(bb):
                            o = bank[7][:, cols(g % 2, 2 * N)].rearrange("p (h c) -> p h c", h=HEADS)
                            dve.wait_ge(sem("L3_out_mm"), G * bb + g + 1)
                            nc.vector.reciprocal(rd3[g % 2][:], o[:, :, HD]).then_inc(sem("L3_rden"), 1)
                    if real(b - 2):
                        if u == 0:
                            dve.wait_ge(sem("L3_out"), G * (b - 1))
                            nc.vector.tensor_tensor(yb[s][:], yb[s][:], x_of(b - 2), ALU.add).then_inc(sem("L3_y_done"), 1)
                        if u == 2:
                            stats_nodes(dve, 3, b - 2, s, (1,))
                    if real(b):
                        dve.wait_ge(sem("L3_leaky"), U + 1)
                        need(dve, sem("L3_less_max"), U - 3)
                        nc.vector.tensor_reduce(nmx[u % 4][:], v3(P[u % 4][:], HQ), AX.X, ALU.max, negate=True)\
                          .then_inc(sem("L3_max"), 1)
                    if u in (2, 3, 4) and real(b + 1):
                        split_e(dve, b + 1, 2 * u - 4)
                    if u % 2 == 1 and real(bb):
                        if g == 0:
                            y_slot_free(dve, 3, bb)
                        dve.wait_ge(sem("L3_rden"), G * bb + g + 1)
                        nc.vector.tensor_tensor(v3(yb[1 - s][:, cols(g)], HEADS), o[:, :, 0:HD],
                                                rd3[g % 2][:].unsqueeze(2).broadcast_to([128, HEADS, HD]), ALU.mult)\
                          .then_inc(sem("L3_out"), 1)
                    if real(b - 2):
                        if u in (1, 2, 3):
                            stats_nodes(dve, 3, b - 2, s, ((0,), (2,), (3,))[u - 1])
                        if u == 4:
                            stats_done(dve, 3, s)
            later_layers(dve, layer1, layer2, layer3, last=2)

        @block.tensor
        def _(pe):
            mm = nc.tensor.matmul
            pe.wait_ge(sem("ident"), 1)
            pe.wait_ge(sem("L0_params"), 64)
            prep_pe(pe, range(first))

            def transposes(dst, src, n):
                for i in range(n):
                    last = nc.tensor.transpose(dst[:, cols(i)], src[:, cols(i)], identf[:])
                return last

            def layer0(b, s, turn):
                if real(b):
                    pe.wait_ge(sem("L0_xT"), b + 1)
                    need(pe, sem("L0_vals"), b - 1)
                    if isinstance(b, int) and b == 0:
                        pe.wait_ge(sem("bias_split"), 6)
                    for i in range(2):
                        mm(bank[1 + 3 * s + i][:], ones[:], bias3[:], start=True, stop=False)
                        for g in range(2):
                            last = mm(bank[1 + 3 * s + i][:, cols(g, 2 * D)], xT[s][:, cols(2 * i + g)], hg_w["loop"][:],
                                      start=False, stop=g == 1)
                    last.then_inc(sem("L0_hg_mm"), 1)
                if real(b + 1):
                    pe.wait_ge(sem(f"L0_staged{1 - s}"), 16 * (turn + 1 if s == 0 else turn + 2))
                    need(pe, sem("L0_xT"), b + 1)
                    transposes(bank[0], xs[1 - s], G).then_inc(sem("L0_xT_mm"), 1)
                if real(b - 1):
                    pe.wait_ge(sem("L0_vals"), b)
                    need(pe, sem("L0_y_done"), b - 1)
                    for g in range(G):
                        last = mm(bank[3][:, cols(g)], loopm[1 - s][:, cols(g)], vals[1 - s][:, cols(g)], start=True, stop=True)
                    last.then_inc(sem("L0_z_mm"), 1)
            every_batch(pe, layer0, before=True, after=1)
            pe.wait_ge(sem("params"), sems["n_params"])
            prep_pe(pe, range(first, len(prep)))
            pe.wait_ge(sem("pool_ready"), 1)
            general_pe(pe)

            def layer1(b, s, turn):
                if real(b):
                    pe.wait_ge(sem("L1_xT"), b + 1)
                    need(pe, sem("L1_uT"), b)
                    mm(bank[1][:], bil[:], xT[s][:], start=True, stop=True).then_inc(sem("L1_u_mm"), 1)
                if real(b):
                    need_or(pe, sem("L1_xw"), b, sem("L0_y_done"), BATCHES)
                    for g in range(G):
                        last = mm(bank[3 + 2 * (g // 2)][:, cols(g % 2, 2 * D)], xT[s][:, cols(g)], w12[:], start=True, stop=True)
                    last.then_inc(sem("L1_xw_mm"), 1)
                if real(b):
                    need(pe, sem("L1_leaky"), b)
                    mm(bank[2][:], identb[:], mask1[:, bass.ts(b, W)], start=True, stop=False)
                    for g in range(G):
                        mm(bank[2][:, cols(g)], xT[s][:, cols(g)], wa2[:], start=False, stop=False)
                if real(b + 1):
                    pe.wait_ge(sem(f"L1_staged{1 - s}"), 16 * (turn + 1 if s == 0 else turn + 2))
                    need(pe, sem("L1_xT"), b + 1)
                    transposes(bank[0], xs[1 - s], G).then_inc(sem("L1_xT_mm"), 1)
                if real(b - 1):
                    pe.wait_ge(sem("L1_exp"), b)
                    need(pe, sem("L1_pT"), b - 1)
                    transposes(bank[4], e1[1 - s], G).then_inc(sem("L1_pT_mm"), 1)
                if real(b):
                    pe.wait_ge(sem("L1_uT"), b + 1)
                    for g in range(G):
                        last = mm(bank[2][:, cols(g)], uT[s][:, cols(g)], xT[s][:, cols(g)], start=False, stop=g == G - 1)
                    last.then_inc(sem("L1_logits_mm"), 1)
                if real(b - 1):
                    pe.wait_ge(sem("L1_pT"), b)
                    need(pe, sem("L1_z"), b - 1)
                    for g in range(G):
                        last = mm(bank[6][:, cols(g)], pT1[1 - s][:, cols(g)], y2[1 - s][:, cols(g)], start=True, stop=True)
                    last.then_inc(sem("L1_z_mm"), 1)

            def transpose_p(L, b, u, lag, ready):
                bb, uu = b + (u - lag) // UNITS, (u - lag) % UNITS
                if real(bb):
                    U = UNITS * bb + uu
                    pe.wait_ge(sem(ready), U + 1)
                    need(pe, sem(f"L{L}_pT"), U - 1)
                    transposes(bank[2 + uu % 2], P[uu % 4], HQ).then_inc(sem(f"L{L}_pT_mm"), 1)

            def p_times_v(L, b, s, u, lag):
                bb, uu = b + (u - lag) // UNITS, (u - lag) % UNITS
                ss = (s + (u - lag) // UNITS) % 2
                if real(bb):
                    g, hq = uu // 2, uu % 2
                    pe.wait_ge(sem(f"L{L}_pT"), UNITS * bb + uu + 1)
                    if hq == 0:
                        need_or(pe, sem(f"L{L}_oT"), G * bb + g, sem("L1_z"), BATCHES)
                    if uu == 0:
                        pe.wait_ge(sem("L2_v" if L == 2 else "L3_wh"), bb + 1)
                    for j in range(HQ):
                        h = HQ * hq + j
                        if L == 2:
                            row, col, start, stop = HP * (h // 2), g % 2, h % 2 == 0, h % 2 == 1
                        else:
                            row, col, start, stop = HP * j, 2 * (g % 2) + hq, True, True
                        last = mm(bank[6][row:row + HP, cols(col)], (v2 if L == 2 else vx)[ss][:, cols(HEADS * g + h, HP)],
                                  pT[uu % 2][:, cols(j)], start=start, stop=stop)
                    last.then_inc(sem(f"L{L}_pv_mm"), 1)

            def layer2(b, s, turn, units=range(UNITS)):
                for u in units:
                    if real(b):
                        U = UNITS * b + u
                        g, hq = u // 2, u % 2
                        if u == 0:
                            pe.wait_ge(sem("L2_q"), b + 1)
                            pe.wait_ge(sem("L2_kexp"), b + 1)
                        need(pe, sem("L2_exp"), U - 1)
                        mm(bank[u % 2][:], identb[:], heads_of(mask2, b, g), start=True, stop=False)
                        kh = v3(kexp[:, cols(s, HEADS * W)], HEADS)[:, HQ * hq:HQ * hq + HQ, cols(g)]
                        mm(bank[u % 2][:], qT[s][:, cols(g)], kh, start=False, stop=True).then_inc(sem("L2_s_mm"), 1)
                    if real(b + 1):
                        if u == 1:
                            pe.wait_ge(sem(f"L2_staged{1 - s}"), 16 * (turn + 1 if s == 0 else turn + 2))
                            need_or(pe, sem("L2_q"), b + 1, sem("L1_pT"), BATCHES)
                            transposes(bank[4], xs[1 - s], G).then_inc(sem("L2_xT_mm"), 1)
                        if u == 3:
                            pe.wait_ge(sem("L2_xT"), b + 2)
                            need(pe, sem("L2_v"), b + 1)
                            mm(bank[5][:], kT_w[:], xT[1 - s][:], start=True, stop=True).then_inc(sem("L2_k_mm"), 1)
                        if u == 5:
                            mm(bank[4][:], qT_w[:], xT[1 - s][:], start=True, stop=True).then_inc(sem("L2_q_mm"), 1)
                        if u == 7:
                            pe.wait_ge(sem("L2_k"), b + 2)
                            for g in range(G):
                                last = mm(bank[5][:, cols(g)], xT[1 - s][:, cols(g)], vT_w[:], start=True, stop=True)
                            last.then_inc(sem("L2_v_mm"), 1)
                    if u % 2 == 0:
                        bb, g = b + (u - 6) // UNITS, (u - 6) % UNITS // 2
                        if real(bb):
                            pe.wait_ge(sem("L2_oT"), G * bb + g + 1)
                            if g == 0:
                                need(pe, sem("L2_out"), bb)
                            mm(bank[7][:, cols(g)], oT[g % 2][:, 0:N], oT_w[:], start=True, stop=True)\
                              .then_inc(sem("L2_out_mm"), 1)
                    transpose_p(2, b, u, 2, "L2_p")
                    p_times_v(2, b, s, u, 3)

            def layer3(b, s, turn, units=range(UNITS)):
                for u in units:
                    if real(b):
                        U = UNITS * b + u
                        g, hq = u // 2, u % 2
                        if u == 0:
                            pe.wait_ge(sem("L3_eT"), b + 1)
                        need(pe, sem("L3_leaky"), U - 1)
                        mm(bank[u % 2][:], identb[:], heads_of(mask2, b, g), start=True, stop=False)
                        mm(bank[u % 2][:], eT[s][:, cols(g)], sel1[:, cols(hq, HQ * 128)], start=False, stop=False)
                        for j in range(HQ):
                            last = mm(bank[u % 2][:, cols(j)], sel2[:, cols(HQ * hq + j)], eT[s][:, cols(g)],
                                      start=False, stop=j == HQ - 1)
                        last.then_inc(sem("L3_s_mm"), 1)
                    transpose_p(3, b, u, 4, "L3_exp")
                    if real(b + 1):
                        if u == 0:
                            pe.wait_ge(sem(f"L3_staged{1 - s}"), 16 * (turn + 1 if s == 0 else turn + 2))
                            need(pe, sem("L3_wh"), b + 1)
                            transposes(bank[4], xs[1 - s], G).then_inc(sem("L3_xT_mm"), 1)
                        if u in (1, 2):
                            pe.wait_ge(sem("L3_xT"), b + 2)
                            need(pe, sem("L3_eT"), b + 1)
                            for g in range(2 * u - 2, 2 * u):
                                last = mm(v3(bank[4 + g // 2][:], 2)[:, g % 2, 0:D + 2 * HEADS], xT[1 - s][:, cols(g)], wh_w[:],
                                          start=True, stop=True)
                            if u == 2:
                                last.then_inc(sem("L3_wh_mm"), 1)
                        if u == 6:
                            pe.wait_ge(sem("L3_split"), 6 * (b + 2))
                            pe.wait_ge(sem("L3_wh"), b + 2)
                            for g in range(G):
                                last = nc.tensor.transpose(bank[5][:].bitcast(BF16)[:, cols(g)], ep[:, cols(g)], identb[:])
                            last.then_inc(sem("L3_eT_mm"), 1)
                    p_times_v(3, b, s, u, 5)
                    if u % 2 == 0:
                        bb, g = b + (u - 8) // UNITS, (u - 8) % UNITS // 2
                        if real(bb):
                            pe.wait_ge(sem("L3_oT"), G * bb + g + 1)
                            need_or(pe, sem("L3_out"), G * bb + g, sem("L2_out"), BATCHES)
                            transposes(bank[7][:, cols(g % 2, 2 * N)], oT[g % 2], 2).then_inc(sem("L3_out_mm"), 1)
            later_layers(pe, layer1, layer2, layer3, last=1)



def kernel(**inputs):
    import numpy as np
    import concourse.bacc as bacc
    from concourse.bass_utils import run_bass_kernel_spmd

    nc = bacc.Bacc("TRN2", target_bir_lowering=False, num_devices=1)
    arrays, handles = {}, {}
    for name, value in inputs.items():
        a = np.ascontiguousarray(value)
        arrays[f"in_{name}"] = a
        handles[name] = nc.dram_tensor(f"in_{name}", a.shape, mybir.dt.from_np(a.dtype), kind="ExternalInput").ap()
    out = nc.dram_tensor("out", (GRAPHS, N, D), F32, kind="ExternalOutput").ap()
    build(nc, handles, out)
    result = run_bass_kernel_spmd(nc, [arrays], core_ids=[0])
    return result.results[0]["out"]
```
